# Optimizing a Trainium2 kernel written in Bass

```python
import numpy as np
import jax
import jax.numpy as jnp

def _softmax(x, axis=-1):
    return jax.nn.softmax(x, axis=axis)

def _gelu(x):
    return jax.nn.gelu(x, approximate=True)

def _silu(x):
    return jax.nn.silu(x)

def _sigmoid(x):
    return jax.nn.sigmoid(x)

def _layernorm(x, axis=-1, eps=1e-05):
    m = jnp.mean(x, axis=axis, keepdims=True)
    v = jnp.var(x, axis=axis, keepdims=True)
    return (x - m) / jnp.sqrt(v + eps)

def _scatter_add(tgt, idx, src, axis=0):
    return tgt.at[idx].add(src)

def _segment_sum(src, seg, n):
    return jax.ops.segment_sum(src, seg, n)
kernel_name = 'mk_perceiver_d2_seqx_r8_0d6d33'

def setup_inputs(seed: int=0):
    np.random.seed(seed)
    _w = jnp.asarray

    def _rec_inputs():
        import jax
        import jax.numpy as jnp
        _rk = jax.random.key(seed)
        x = 7.22e-05 + 1 * jax.random.normal(jax.random.fold_in(_rk, 1), (16, 64, 128), jnp.float32)
        _lenS = 64 - jax.random.randint(jax.random.fold_in(_rk, 7), (16,), 0, max(1, 64 // 4) + 1, jnp.int32)
        _lenS2 = 1601 - jax.random.randint(jax.random.fold_in(_rk, 8), (16,), 0, max(1, 1601 // 4) + 1, jnp.int32)
        _ctx_768P = jax.random.normal(jax.random.fold_in(_rk, 11), (16, 16, 96), jnp.float32)
        _ctx_768c = jax.random.dirichlet(jax.random.fold_in(_rk, 511), 0.3 * jnp.ones((16,), jnp.float32), (16, 1601))
        _ctx_768t = jnp.einsum('bsk,bkd->bsd', _ctx_768c, _ctx_768P)
        _ctx_768t = _ctx_768t * jax.lax.rsqrt(jnp.mean(jnp.square(_ctx_768t)) + 1e-12) * 0.953939
        ctx_768 = -0.000191848 + 0.999787 * (_ctx_768t + 0.3 * jax.random.normal(jax.random.fold_in(_rk, 611), (16, 1601, 96), jnp.float32))
        _validS = jnp.arange(64)[None, :] < _lenS[:, None]
        _validS2 = jnp.arange(1601)[None, :] < _lenS2[:, None]
        _causal = jnp.tril(jnp.ones((64, 64), dtype=bool))
        mask_BxS2_bk0 = jnp.logical_not(jnp.broadcast_to(_validS2[:, :], (16, 1601)))
        return (x, ctx_768, mask_BxS2_bk0)
    x, ctx_768, mask_BxS2_bk0 = _rec_inputs()

    def _L0_xattn_setup():
        import jax, jax.numpy as jnp
        import numpy as np
        HEADS = 8
        DIM_HEAD = 64
        SCALE = DIM_HEAD ** (-0.5)
        key = jax.random.key(seed)
        ks = jax.random.split(key, 7)
        B, Nq, Nc = (4, 256, 256)
        Dq, Dc = (128, 96)
        inner = HEADS * DIM_HEAD
        x = jax.random.normal(ks[0], (B, Nq, Dq), dtype=jnp.float32)
        context = jax.random.normal(ks[1], (B, Nc, Dc), dtype=jnp.float32)
        Wq = jax.random.normal(ks[2], (Dq, inner), dtype=jnp.float32) * Dq ** (-0.5)
        Wk = jax.random.normal(ks[3], (Dc, inner), dtype=jnp.float32) * Dc ** (-0.5)
        Wv = jax.random.normal(ks[4], (Dc, inner), dtype=jnp.float32) * Dc ** (-0.5)
        Wo = jax.random.normal(ks[5], (inner, Dq), dtype=jnp.float32) * inner ** (-0.5)
        bo = jax.random.normal(ks[6], (Dq,), dtype=jnp.float32) * 0.01
        return {'x': x, 'context': context, 'Wq': Wq, 'Wk': Wk, 'Wv': Wv, 'Wo': Wo, 'bo': bo}
    _L0_xattn_all = _L0_xattn_setup()
    _L0_xattn_in = {k: v for k, v in _L0_xattn_all.items() if k in ('Wq', 'Wk', 'Wv', 'Wo', 'bo')}
    del _L0_xattn_all

    def _L0_attn_setup():
        import jax, jax.numpy as jnp
        import numpy as np
        B, S, D_MODEL = (1, 256, 128)
        H = 16
        D = D_MODEL // H
        G = 32
        TOP2, TOP1 = (4, 8)
        WIN = 64
        SCALE = D ** (-0.5)

        def _rotate_half(x):
            x1, x2 = jnp.split(x, 2, axis=-1)
            return jnp.concatenate([-x2, x1], axis=-1)

        def _rope(q, k):
            s = q.shape[2]
            inv_freq = 1.0 / 10000.0 ** (jnp.arange(0, D, 2, dtype=jnp.float32) / D)
            freqs = jnp.arange(s, dtype=jnp.float32)[:, None] * inv_freq[None, :]
            emb = jnp.concatenate([freqs, freqs], axis=-1)
            cos = jnp.cos(emb)[None, None]
            sin = jnp.sin(emb)[None, None]
            return (q * cos + _rotate_half(q) * sin, k * cos + _rotate_half(k) * sin)
        key = jax.random.key(seed)
        ks = jax.random.split(key, 9)
        std = 0.02
        return {'x': jax.random.normal(ks[0], (B, S, D_MODEL), jnp.float32), 'W_q': jax.random.normal(ks[1], (D_MODEL, D_MODEL), jnp.float32) * std, 'W_k': jax.random.normal(ks[2], (D_MODEL, D_MODEL), jnp.float32) * std, 'W_v': jax.random.normal(ks[3], (D_MODEL, D_MODEL), jnp.float32) * std, 'W_o': jax.random.normal(ks[4], (D_MODEL, D_MODEL), jnp.float32) * std, 'k_lod1': jax.random.normal(ks[5], (D, G * D), jnp.float32) * std, 'v_lod1': jax.random.normal(ks[6], (D, G * D), jnp.float32) * std, 'k_lod2': jax.random.normal(ks[7], (D, G * D), jnp.float32) * std, 'v_lod2': jax.random.normal(ks[8], (D, G * D), jnp.float32) * std}
    _L0_attn_all = _L0_attn_setup()
    _L0_attn_in = {k: v for k, v in _L0_attn_all.items() if k in ('W_q', 'W_k', 'W_v', 'W_o', 'k_lod1', 'v_lod1', 'k_lod2', 'v_lod2')}
    del _L0_attn_all

    def _L0_ffn_setup():
        import jax, jax.numpy as jnp
        import numpy as np
        B, S, D = (2, 128, 128)
        H, HD = (16, 64)
        E_R = 31
        K_ACT = 3
        INTER = 128
        EPS = 1e-05
        BASE = 10000.0

        def _rmsnorm(x, gamma):
            rms = jnp.sqrt(jnp.mean(x * x, axis=-1, keepdims=True) + EPS)
            return x / rms * gamma

        def _rope(x, theta):
            seq = x.shape[2]
            angles = jnp.arange(seq, dtype=theta.dtype)[:, None] * theta
            cos = jnp.cos(angles)[None, None]
            sin = jnp.sin(angles)[None, None]
            x1, x2 = (x[..., 0::2], x[..., 1::2])
            return jnp.concatenate([x1 * cos - x2 * sin, x1 * sin + x2 * cos], axis=-1)

        def _forward(x, theta, gamma1, gamma2, q_w, q_b, k_w, k_b, v_w, v_b, o_w, o_b, router_w, router_b, sh_w1, sh_b1, sh_w2, sh_b2, re_w1, re_b1, re_w2, re_b2):
            b, s, d = x.shape
            xn = _rmsnorm(x, gamma1)
            q = (xn @ q_w + q_b).reshape(b, s, H, HD).transpose(0, 2, 1, 3)
            k = (xn @ k_w + k_b).reshape(b, s, H, HD).transpose(0, 2, 1, 3)
            v = (xn @ v_w + v_b).reshape(b, s, H, HD).transpose(0, 2, 1, 3)
            q = _rope(q, theta)
            k = _rope(k, theta)
            scale = 1.0 / np.sqrt(HD)
            scores = jnp.einsum('bhqd,bhkd->bhqk', q, k) * scale
            causal = jnp.tril(jnp.ones((s, s), dtype=bool))
            scores = jnp.where(causal, scores, -jnp.inf)
            attn = jax.nn.softmax(scores, axis=-1)
            ctx = jnp.einsum('bhqk,bhkd->bhqd', attn, v)
            ctx = ctx.transpose(0, 2, 1, 3).reshape(b, s, H * HD)
            attn_out = ctx @ o_w + o_b + xn
            an = _rmsnorm(attn_out, gamma2)
            shared = jax.nn.gelu(an @ sh_w1 + sh_b1, approximate=False) @ sh_w2 + sh_b2
            logits = an @ router_w + router_b
            aff = jax.nn.softmax(logits, axis=-1)
            topv, topi = jax.lax.top_k(aff, K_ACT)
            gates = jnp.sum(jax.nn.one_hot(topi, E_R, dtype=aff.dtype) * topv[..., None], axis=-2)
            h = jax.nn.gelu(jnp.einsum('bsd,edh->besh', an, re_w1) + re_b1[None, :, None, :], approximate=False)
            routed = jnp.einsum('bse,besh,ehd->bsd', gates, h, re_w2) + jnp.einsum('bse,ed->bsd', gates, re_b2)
            return shared + routed + an + attn_out
        key = jax.random.key(seed)
        ks = jax.random.split(key, 24)
        s = 0.02
        theta = BASE ** (-jnp.arange(HD // 2, dtype=jnp.float32) * 2.0 / HD)
        inp = {'x': jax.random.normal(ks[0], (B, S, D), jnp.float32), 'positions': jnp.arange(S, dtype=jnp.int32), 'theta': theta, 'gamma1': jnp.ones((D,), jnp.float32), 'gamma2': jnp.ones((D,), jnp.float32), 'q_w': jax.random.normal(ks[1], (D, H * HD), jnp.float32) * s, 'q_b': jnp.zeros((H * HD,), jnp.float32), 'k_w': jax.random.normal(ks[2], (D, H * HD), jnp.float32) * s, 'k_b': jnp.zeros((H * HD,), jnp.float32), 'v_w': jax.random.normal(ks[3], (D, H * HD), jnp.float32) * s, 'v_b': jnp.zeros((H * HD,), jnp.float32), 'o_w': jax.random.normal(ks[4], (H * HD, D), jnp.float32) * s, 'o_b': jnp.zeros((D,), jnp.float32), 'router_w': jax.random.normal(ks[5], (D, E_R), jnp.float32) * s, 'router_b': jnp.zeros((E_R,), jnp.float32), 'sh_w1': jax.random.normal(ks[6], (D, INTER), jnp.float32) * s, 'sh_b1': jnp.zeros((INTER,), jnp.float32), 'sh_w2': jax.random.normal(ks[7], (INTER, D), jnp.float32) * s, 'sh_b2': jnp.zeros((D,), jnp.float32), 're_w1': jax.random.normal(ks[8], (E_R, D, INTER), jnp.float32) * s, 're_b1': jnp.zeros((E_R, INTER), jnp.float32), 're_w2': jax.random.normal(ks[9], (E_R, INTER, D), jnp.float32) * s, 're_b2': jnp.zeros((E_R, D), jnp.float32)}
        return inp
    _L0_ffn_all = _L0_ffn_setup()
    _L0_ffn_in = {k: v for k, v in _L0_ffn_all.items() if k in ('positions', 'theta', 'gamma1', 'gamma2', 'q_w', 'q_b', 'k_w', 'k_b', 'v_w', 'v_b', 'o_w', 'o_b', 'router_w', 'router_b', 'sh_w1', 'sh_b1', 'sh_w2', 'sh_b2', 're_w1', 're_b1', 're_w2', 're_b2')}
    del _L0_ffn_all

    def _L1_xattn_setup():
        import jax, jax.numpy as jnp
        import numpy as np
        DIM_IN, DIM_LAT, DIM_HEAD = (96, 128, 64)
        INNER = max(DIM_LAT, DIM_IN)
        HEADS = INNER // DIM_HEAD
        SCALE = DIM_HEAD ** (-0.5)
        RMS_EPS = 1e-08
        LN_EPS = 1e-05

        def layernorm(x, g, b):
            mu = jnp.mean(x, axis=-1, keepdims=True)
            var = jnp.mean((x - mu) ** 2, axis=-1, keepdims=True)
            return (x - mu) * jax.lax.rsqrt(var + LN_EPS) * g + b

        def rmsnorm(x, gamma):
            norm = jnp.sqrt(jnp.sum(x * x, axis=-1, keepdims=True)) * x.shape[-1] ** (-0.5)
            return x / jnp.maximum(norm, RMS_EPS) * gamma
        key = jax.random.key(seed)
        ks = jax.random.split(key, 12)
        b, n, m = (4, 512, 64)
        x = jax.random.normal(ks[0], (b, n, DIM_IN), jnp.float32)
        latents = jax.random.normal(ks[1], (b, m, DIM_LAT), jnp.float32)
        mask = jax.random.randint(ks[2], (b, n), 0, 2).astype(bool)
        s = lambda k, sh, fan: jax.random.normal(k, sh, jnp.float32) * fan ** (-0.5)
        return {'x': x, 'latents': latents, 'mask': mask, 'ln_x_g': jnp.ones((DIM_IN,), jnp.float32), 'ln_x_b': jnp.zeros((DIM_IN,), jnp.float32), 'ln_l_g': jnp.ones((DIM_LAT,), jnp.float32), 'ln_l_b': jnp.zeros((DIM_LAT,), jnp.float32), 'qn_g': jnp.ones((DIM_HEAD,), jnp.float32), 'kn_g': jnp.ones((DIM_HEAD,), jnp.float32), 'Wq': s(ks[3], (INNER, DIM_LAT), DIM_LAT), 'Wkv': s(ks[4], (2 * INNER, DIM_IN), DIM_IN), 'Wlkv': s(ks[5], (2 * INNER, DIM_LAT), DIM_LAT), 'Wo': s(ks[6], (DIM_LAT, INNER), INNER), 'bo': jnp.zeros((DIM_LAT,), jnp.float32)}
    _L1_xattn_all = _L1_xattn_setup()
    _L1_xattn_in = {k: v for k, v in _L1_xattn_all.items() if k in ('ln_x_g', 'ln_x_b', 'ln_l_g', 'ln_l_b', 'qn_g', 'kn_g', 'Wq', 'Wkv', 'Wlkv', 'Wo', 'bo')}
    del _L1_xattn_all

    def _L1_attn_setup():
        import math
        import jax, jax.numpy as jnp
        import numpy as np
        N_HEAD = 16
        STEP_DIM = 4

        def _make_mask(T):
            m = jnp.tril(jnp.ones((T, T), dtype=jnp.float32))
            cols = jnp.arange(T)
            keep_col = cols % STEP_DIM != STEP_DIM - 1
            return m * keep_col[None, :].astype(jnp.float32)
        key = jax.random.key(seed)
        ks = jax.random.split(key, 9)
        B, T, C = (2, 256, 128)
        s = 1.0 / math.sqrt(C)
        return {'x': jax.random.normal(ks[0], (B, T, C), dtype=jnp.float32), 'Wq': jax.random.normal(ks[1], (C, C), dtype=jnp.float32) * s, 'bq': jnp.zeros((C,), dtype=jnp.float32), 'Wk': jax.random.normal(ks[2], (C, C), dtype=jnp.float32) * s, 'bk': jnp.zeros((C,), dtype=jnp.float32), 'Wv': jax.random.normal(ks[3], (C, C), dtype=jnp.float32) * s, 'bv': jnp.zeros((C,), dtype=jnp.float32), 'Wp': jax.random.normal(ks[4], (C, C), dtype=jnp.float32) * s, 'bp': jnp.zeros((C,), dtype=jnp.float32)}
    _L1_attn_all = _L1_attn_setup()
    _L1_attn_in = {k: v for k, v in _L1_attn_all.items() if k in ('Wq', 'bq', 'Wk', 'bk', 'Wv', 'bv', 'Wp', 'bp')}
    del _L1_attn_all

    def _L1_ffn_setup():
        import jax, jax.numpy as jnp
        import numpy as np
        D, H, O, E, TOPK = (128, 512, 128, 8, 2)
        B, S = (4, 128)
        key = jax.random.key(seed)
        ks = jax.random.split(key, 12)
        std = 0.02
        return {'hidden_states': jax.random.normal(ks[0], (B, S, D), dtype=jnp.float32), 'norm_weight': jnp.ones((D,), dtype=jnp.float32), 'router_w': jax.random.normal(ks[1], (E, D), dtype=jnp.float32) * std, 'sw1': jax.random.normal(ks[2], (D, H), dtype=jnp.float32) * (1.0 / np.sqrt(D)), 'sb1': jnp.zeros((H,), dtype=jnp.float32), 'sw2': jax.random.normal(ks[3], (H, O), dtype=jnp.float32) * (1.0 / np.sqrt(H)), 'sb2': jnp.zeros((O,), dtype=jnp.float32), 'ew1': jax.random.normal(ks[4], (E, D, H), dtype=jnp.float32) * (1.0 / np.sqrt(D)), 'eb1': jnp.zeros((E, H), dtype=jnp.float32), 'ew2': jax.random.normal(ks[5], (E, H, O), dtype=jnp.float32) * (1.0 / np.sqrt(H)), 'eb2': jnp.zeros((E, O), dtype=jnp.float32)}
    _L1_ffn_all = _L1_ffn_setup()
    _L1_ffn_in = {k: v for k, v in _L1_ffn_all.items() if k in ('norm_weight', 'router_w', 'sw1', 'sb1', 'sw2', 'sb2', 'ew1', 'eb1', 'ew2', 'eb2')}
    del _L1_ffn_all
    return {'x': x, 'ctx_768': ctx_768, 'mask_BxS2_bk0': mask_BxS2_bk0, 'L0_xattn_Wq': _L0_xattn_in['Wq'], 'L0_xattn_Wk': _L0_xattn_in['Wk'], 'L0_xattn_Wv': _L0_xattn_in['Wv'], 'L0_xattn_Wo': _L0_xattn_in['Wo'], 'L0_xattn_bo': _L0_xattn_in['bo'], 'L0_attn_W_q': _L0_attn_in['W_q'], 'L0_attn_W_k': _L0_attn_in['W_k'], 'L0_attn_W_v': _L0_attn_in['W_v'], 'L0_attn_W_o': _L0_attn_in['W_o'], 'L0_attn_k_lod1': _L0_attn_in['k_lod1'], 'L0_attn_v_lod1': _L0_attn_in['v_lod1'], 'L0_attn_k_lod2': _L0_attn_in['k_lod2'], 'L0_attn_v_lod2': _L0_attn_in['v_lod2'], 'L0_ffn_positions': _L0_ffn_in['positions'], 'L0_ffn_theta': _L0_ffn_in['theta'], 'L0_ffn_gamma1': _L0_ffn_in['gamma1'], 'L0_ffn_gamma2': _L0_ffn_in['gamma2'], 'L0_ffn_q_w': _L0_ffn_in['q_w'], 'L0_ffn_q_b': _L0_ffn_in['q_b'], 'L0_ffn_k_w': _L0_ffn_in['k_w'], 'L0_ffn_k_b': _L0_ffn_in['k_b'], 'L0_ffn_v_w': _L0_ffn_in['v_w'], 'L0_ffn_v_b': _L0_ffn_in['v_b'], 'L0_ffn_o_w': _L0_ffn_in['o_w'], 'L0_ffn_o_b': _L0_ffn_in['o_b'], 'L0_ffn_router_w': _L0_ffn_in['router_w'], 'L0_ffn_router_b': _L0_ffn_in['router_b'], 'L0_ffn_sh_w1': _L0_ffn_in['sh_w1'], 'L0_ffn_sh_b1': _L0_ffn_in['sh_b1'], 'L0_ffn_sh_w2': _L0_ffn_in['sh_w2'], 'L0_ffn_sh_b2': _L0_ffn_in['sh_b2'], 'L0_ffn_re_w1': _L0_ffn_in['re_w1'], 'L0_ffn_re_b1': _L0_ffn_in['re_b1'], 'L0_ffn_re_w2': _L0_ffn_in['re_w2'], 'L0_ffn_re_b2': _L0_ffn_in['re_b2'], 'L1_xattn_ln_x_g': _L1_xattn_in['ln_x_g'], 'L1_xattn_ln_x_b': _L1_xattn_in['ln_x_b'], 'L1_xattn_ln_l_g': _L1_xattn_in['ln_l_g'], 'L1_xattn_ln_l_b': _L1_xattn_in['ln_l_b'], 'L1_xattn_qn_g': _L1_xattn_in['qn_g'], 'L1_xattn_kn_g': _L1_xattn_in['kn_g'], 'L1_xattn_Wq': _L1_xattn_in['Wq'], 'L1_xattn_Wkv': _L1_xattn_in['Wkv'], 'L1_xattn_Wlkv': _L1_xattn_in['Wlkv'], 'L1_xattn_Wo': _L1_xattn_in['Wo'], 'L1_xattn_bo': _L1_xattn_in['bo'], 'L1_attn_Wq': _L1_attn_in['Wq'], 'L1_attn_bq': _L1_attn_in['bq'], 'L1_attn_Wk': _L1_attn_in['Wk'], 'L1_attn_bk': _L1_attn_in['bk'], 'L1_attn_Wv': _L1_attn_in['Wv'], 'L1_attn_bv': _L1_attn_in['bv'], 'L1_attn_Wp': _L1_attn_in['Wp'], 'L1_attn_bp': _L1_attn_in['bp'], 'L1_ffn_norm_weight': _L1_ffn_in['norm_weight'], 'L1_ffn_router_w': _L1_ffn_in['router_w'], 'L1_ffn_sw1': _L1_ffn_in['sw1'], 'L1_ffn_sb1': _L1_ffn_in['sb1'], 'L1_ffn_sw2': _L1_ffn_in['sw2'], 'L1_ffn_sb2': _L1_ffn_in['sb2'], 'L1_ffn_ew1': _L1_ffn_in['ew1'], 'L1_ffn_eb1': _L1_ffn_in['eb1'], 'L1_ffn_ew2': _L1_ffn_in['ew2'], 'L1_ffn_eb2': _L1_ffn_in['eb2']}

def reference(x, ctx_768, mask_BxS2_bk0, L0_xattn_Wq, L0_xattn_Wk, L0_xattn_Wv, L0_xattn_Wo, L0_xattn_bo, L0_attn_W_q, L0_attn_W_k, L0_attn_W_v, L0_attn_W_o, L0_attn_k_lod1, L0_attn_v_lod1, L0_attn_k_lod2, L0_attn_v_lod2, L0_ffn_positions, L0_ffn_theta, L0_ffn_gamma1, L0_ffn_gamma2, L0_ffn_q_w, L0_ffn_q_b, L0_ffn_k_w, L0_ffn_k_b, L0_ffn_v_w, L0_ffn_v_b, L0_ffn_o_w, L0_ffn_o_b, L0_ffn_router_w, L0_ffn_router_b, L0_ffn_sh_w1, L0_ffn_sh_b1, L0_ffn_sh_w2, L0_ffn_sh_b2, L0_ffn_re_w1, L0_ffn_re_b1, L0_ffn_re_w2, L0_ffn_re_b2, L1_xattn_ln_x_g, L1_xattn_ln_x_b, L1_xattn_ln_l_g, L1_xattn_ln_l_b, L1_xattn_qn_g, L1_xattn_kn_g, L1_xattn_Wq, L1_xattn_Wkv, L1_xattn_Wlkv, L1_xattn_Wo, L1_xattn_bo, L1_attn_Wq, L1_attn_bq, L1_attn_Wk, L1_attn_bk, L1_attn_Wv, L1_attn_bv, L1_attn_Wp, L1_attn_bp, L1_ffn_norm_weight, L1_ffn_router_w, L1_ffn_sw1, L1_ffn_sb1, L1_ffn_sw2, L1_ffn_sb2, L1_ffn_ew1, L1_ffn_eb1, L1_ffn_ew2, L1_ffn_eb2):
    import jax
    import jax.numpy as jnp

    def _L0_xattn_ref(x, context, Wq, Wk, Wv, Wo, bo):
        import jax, jax.numpy as jnp
        import numpy as np
        HEADS = 8
        DIM_HEAD = 64
        SCALE = DIM_HEAD ** (-0.5)
        B, Nq, _ = x.shape
        q = (x @ Wq).reshape(B, Nq, HEADS, DIM_HEAD)
        k = (context @ Wk).reshape(B, context.shape[1], HEADS, DIM_HEAD)
        v = (context @ Wv).reshape(B, context.shape[1], HEADS, DIM_HEAD)
        sim = jnp.einsum('bihd,bjhd->bhij', q, k) * SCALE
        attn = jax.nn.softmax(sim, axis=-1)
        out = jnp.einsum('bhij,bjhd->bihd', attn, v)
        out = out.reshape(B, Nq, HEADS * DIM_HEAD)
        return out @ Wo + bo

    def _L0_attn_ref(x, W_q, W_k, W_v, W_o, k_lod1, v_lod1, k_lod2, v_lod2):
        import jax, jax.numpy as jnp
        import numpy as np
        B, S, D_MODEL = (1, 256, 128)
        H = 16
        D = D_MODEL // H
        G = 32
        TOP2, TOP1 = (4, 8)
        WIN = 64
        SCALE = D ** (-0.5)

        def _rotate_half(x):
            x1, x2 = jnp.split(x, 2, axis=-1)
            return jnp.concatenate([-x2, x1], axis=-1)

        def _rope(q, k):
            s = q.shape[2]
            inv_freq = 1.0 / 10000.0 ** (jnp.arange(0, D, 2, dtype=jnp.float32) / D)
            freqs = jnp.arange(s, dtype=jnp.float32)[:, None] * inv_freq[None, :]
            emb = jnp.concatenate([freqs, freqs], axis=-1)
            cos = jnp.cos(emb)[None, None]
            sin = jnp.sin(emb)[None, None]
            return (q * cos + _rotate_half(q) * sin, k * cos + _rotate_half(k) * sin)
        b, s, _ = x.shape
        q = (x @ W_q.T).reshape(b, s, H, D).transpose(0, 2, 1, 3)
        k = (x @ W_k.T).reshape(b, s, H, D).transpose(0, 2, 1, 3)
        v = (x @ W_v.T).reshape(b, s, H, D).transpose(0, 2, 1, 3)
        q, k = _rope(q, k)
        n1 = s // G
        k1 = k[:, :, :n1 * G].reshape(b, H, n1, G * D) @ k_lod1.T
        n2 = n1 // G
        if n2 > 0:
            k2 = k1[:, :, :n2 * G].reshape(b, H, n2, G * D) @ k_lod2.T
        else:
            k2 = k1
            n2 = n1
        scores2 = jnp.einsum('bhqd,bhkd->bhqk', q, k2) * SCALE
        q_pos = jnp.arange(s)
        lod2_end = jnp.arange(n2) * G * G + G * G - 1
        causal2 = lod2_end[None, :] < q_pos[:, None]
        scores2 = jnp.where(causal2[None, None], scores2, -jnp.inf)
        top2 = min(TOP2, n2)
        top2_idx = jax.lax.top_k(scores2, top2)[1]
        lod1_idx = jnp.clip(top2_idx[..., None] * G + jnp.arange(G), 0, n1 - 1)
        lod1_idx = lod1_idx.reshape(b, H, s, top2 * G)
        bi = jnp.arange(b)[:, None, None, None]
        hi = jnp.arange(H)[None, :, None, None]
        k1_g = k1[bi, hi, lod1_idx]
        scores1 = jnp.einsum('bhsd,bhstd->bhst', q, k1_g) * SCALE
        top1 = min(TOP1, scores1.shape[-1])
        top1_rel = jax.lax.top_k(scores1, top1)[1]
        top1_abs = jnp.take_along_axis(lod1_idx, top1_rel, axis=-1)
        pos = jnp.clip(top1_abs[..., None] * G + jnp.arange(G), 0, s - 1)
        pos = pos.reshape(b, H, s, top1 * G)
        si = jnp.arange(s)[None, None, :, None]
        attend = jnp.zeros((b, H, s, s), dtype=bool).at[bi, hi, si, pos].set(True)
        row = q_pos[:, None]
        col = q_pos[None, :]
        local = (col <= row) & (col >= row - WIN + 1)
        attend = (attend | local[None, None]) & (col <= row)[None, None]
        scores = jnp.einsum('bhqd,bhkd->bhqk', q, k) * SCALE
        scores = jnp.where(attend, scores, -jnp.inf)
        attn = jax.nn.softmax(scores, axis=-1)
        attn = jnp.where(jnp.isnan(attn), 0.0, attn)
        out = jnp.einsum('bhqk,bhkd->bhqd', attn, v)
        out = out.transpose(0, 2, 1, 3).reshape(b, s, D_MODEL)
        return out @ W_o.T

    def _L0_ffn_ref(x, positions, theta, gamma1, gamma2, q_w, q_b, k_w, k_b, v_w, v_b, o_w, o_b, router_w, router_b, sh_w1, sh_b1, sh_w2, sh_b2, re_w1, re_b1, re_w2, re_b2):
        import jax, jax.numpy as jnp
        import numpy as np
        B, S, D = (2, 128, 128)
        H, HD = (16, 64)
        E_R = 31
        K_ACT = 3
        INTER = 128
        EPS = 1e-05
        BASE = 10000.0

        def _rmsnorm(x, gamma):
            rms = jnp.sqrt(jnp.mean(x * x, axis=-1, keepdims=True) + EPS)
            return x / rms * gamma

        def _rope(x, theta):
            seq = x.shape[2]
            angles = jnp.arange(seq, dtype=theta.dtype)[:, None] * theta
            cos = jnp.cos(angles)[None, None]
            sin = jnp.sin(angles)[None, None]
            x1, x2 = (x[..., 0::2], x[..., 1::2])
            return jnp.concatenate([x1 * cos - x2 * sin, x1 * sin + x2 * cos], axis=-1)

        def _forward(x, theta, gamma1, gamma2, q_w, q_b, k_w, k_b, v_w, v_b, o_w, o_b, router_w, router_b, sh_w1, sh_b1, sh_w2, sh_b2, re_w1, re_b1, re_w2, re_b2):
            b, s, d = x.shape
            xn = _rmsnorm(x, gamma1)
            q = (xn @ q_w + q_b).reshape(b, s, H, HD).transpose(0, 2, 1, 3)
            k = (xn @ k_w + k_b).reshape(b, s, H, HD).transpose(0, 2, 1, 3)
            v = (xn @ v_w + v_b).reshape(b, s, H, HD).transpose(0, 2, 1, 3)
            q = _rope(q, theta)
            k = _rope(k, theta)
            scale = 1.0 / np.sqrt(HD)
            scores = jnp.einsum('bhqd,bhkd->bhqk', q, k) * scale
            causal = jnp.tril(jnp.ones((s, s), dtype=bool))
            scores = jnp.where(causal, scores, -jnp.inf)
            attn = jax.nn.softmax(scores, axis=-1)
            ctx = jnp.einsum('bhqk,bhkd->bhqd', attn, v)
            ctx = ctx.transpose(0, 2, 1, 3).reshape(b, s, H * HD)
            attn_out = ctx @ o_w + o_b + xn
            an = _rmsnorm(attn_out, gamma2)
            shared = jax.nn.gelu(an @ sh_w1 + sh_b1, approximate=False) @ sh_w2 + sh_b2
            logits = an @ router_w + router_b
            aff = jax.nn.softmax(logits, axis=-1)
            topv, topi = jax.lax.top_k(aff, K_ACT)
            gates = jnp.sum(jax.nn.one_hot(topi, E_R, dtype=aff.dtype) * topv[..., None], axis=-2)
            h = jax.nn.gelu(jnp.einsum('bsd,edh->besh', an, re_w1) + re_b1[None, :, None, :], approximate=False)
            routed = jnp.einsum('bse,besh,ehd->bsd', gates, h, re_w2) + jnp.einsum('bse,ed->bsd', gates, re_b2)
            return shared + routed + an + attn_out
        del positions
        return _forward(x, theta, gamma1, gamma2, q_w, q_b, k_w, k_b, v_w, v_b, o_w, o_b, router_w, router_b, sh_w1, sh_b1, sh_w2, sh_b2, re_w1, re_b1, re_w2, re_b2)

    def _L1_xattn_ref(x, latents, mask, ln_x_g, ln_x_b, ln_l_g, ln_l_b, qn_g, kn_g, Wq, Wkv, Wlkv, Wo, bo):
        import jax, jax.numpy as jnp
        import numpy as np
        DIM_IN, DIM_LAT, DIM_HEAD = (96, 128, 64)
        INNER = max(DIM_LAT, DIM_IN)
        HEADS = INNER // DIM_HEAD
        SCALE = DIM_HEAD ** (-0.5)
        RMS_EPS = 1e-08
        LN_EPS = 1e-05

        def layernorm(x, g, b):
            mu = jnp.mean(x, axis=-1, keepdims=True)
            var = jnp.mean((x - mu) ** 2, axis=-1, keepdims=True)
            return (x - mu) * jax.lax.rsqrt(var + LN_EPS) * g + b

        def rmsnorm(x, gamma):
            norm = jnp.sqrt(jnp.sum(x * x, axis=-1, keepdims=True)) * x.shape[-1] ** (-0.5)
            return x / jnp.maximum(norm, RMS_EPS) * gamma
        b, n, _ = x.shape
        m = latents.shape[1]
        xn = layernorm(x, ln_x_g, ln_x_b)
        ln = layernorm(latents, ln_l_g, ln_l_b)
        q = ln @ Wq.T
        kv = jnp.concatenate([xn @ Wkv.T, ln @ Wlkv.T], axis=1)
        k, v = (kv[..., :INNER], kv[..., INNER:])
        split_heads = lambda t: t.reshape(t.shape[0], t.shape[1], HEADS, DIM_HEAD).transpose(0, 2, 1, 3)
        q, k, v = (split_heads(q), split_heads(k), split_heads(v))
        qn = rmsnorm(q, qn_g) * SCALE
        kn = rmsnorm(k, kn_g)
        attn = jnp.einsum('bhid,bhjd->bhij', qn, kn)
        full_mask = jnp.pad(mask, ((0, 0), (0, m)), constant_values=True)
        attn = jnp.where(full_mask[:, None, None, :], attn, -jnp.finfo(attn.dtype).max)
        attn = jax.nn.softmax(attn, axis=-1)
        out = jnp.einsum('bhij,bhjd->bhid', attn, v)
        out = out.transpose(0, 2, 1, 3).reshape(b, m, INNER)
        return out @ Wo.T + bo

    def _L1_attn_ref(x, Wq, bq, Wk, bk, Wv, bv, Wp, bp):
        import math
        import jax, jax.numpy as jnp
        import numpy as np
        N_HEAD = 16
        STEP_DIM = 4

        def _make_mask(T):
            m = jnp.tril(jnp.ones((T, T), dtype=jnp.float32))
            cols = jnp.arange(T)
            keep_col = cols % STEP_DIM != STEP_DIM - 1
            return m * keep_col[None, :].astype(jnp.float32)
        B, T, C = x.shape
        H = N_HEAD
        D = C // H

        def heads(y):
            return y.reshape(B, T, H, D).transpose(0, 2, 1, 3)
        q = heads(x @ Wq + bq)
        k = heads(x @ Wk + bk)
        v = heads(x @ Wv + bv)
        att = jnp.einsum('bhtd,bhsd->bhts', q, k) * (1.0 / math.sqrt(D))
        mask = _make_mask(T)
        att = jnp.where(mask[None, None, :, :] == 0, -jnp.inf, att)
        att = jax.nn.softmax(att, axis=-1)
        y = jnp.einsum('bhts,bhsd->bhtd', att, v)
        y = y.transpose(0, 2, 1, 3).reshape(B, T, C)
        return y @ Wp + bp

    def _L1_ffn_ref(hidden_states, norm_weight, router_w, sw1, sb1, sw2, sb2, ew1, eb1, ew2, eb2):
        import jax, jax.numpy as jnp
        import numpy as np
        D, H, O, E, TOPK = (128, 512, 128, 8, 2)
        B, S = (4, 128)
        b, s, d = hidden_states.shape
        var = jnp.mean(jnp.square(hidden_states), axis=-1, keepdims=True)
        normed = hidden_states * jax.lax.rsqrt(var + 1e-08) * norm_weight
        shared = jnp.maximum(normed @ sw1 + sb1, 0.0) @ sw2 + sb2
        flat = normed.reshape(-1, d)
        T = flat.shape[0]
        probs = jax.nn.sigmoid(flat @ router_w.T)
        scores, idx = jax.lax.top_k(probs, TOPK)
        w = scores / (jnp.sum(scores, axis=-1, keepdims=True) + 1e-06)
        comb = jnp.zeros((T, E), dtype=flat.dtype)
        comb = comb.at[jnp.arange(T)[:, None], idx].add(w)
        h = jnp.maximum(jnp.einsum('td,edh->teh', flat, ew1) + eb1[None, :, :], 0.0)
        eo = jnp.einsum('teh,eho->teo', h, ew2) + eb2[None, :, :]
        routed = jnp.einsum('teo,te->to', eo, comb)
        return shared + routed.reshape(b, s, -1)
    x = x + _L0_xattn_ref(_layernorm(x, axis=-1), ctx_768, L0_xattn_Wq, L0_xattn_Wk, L0_xattn_Wv, L0_xattn_Wo, L0_xattn_bo)
    x = x + _L0_attn_ref(_layernorm(x, axis=-1), L0_attn_W_q, L0_attn_W_k, L0_attn_W_v, L0_attn_W_o, L0_attn_k_lod1, L0_attn_v_lod1, L0_attn_k_lod2, L0_attn_v_lod2)
    x = x + _L0_ffn_ref(_layernorm(x, axis=-1), L0_ffn_positions, L0_ffn_theta, L0_ffn_gamma1, L0_ffn_gamma2, L0_ffn_q_w, L0_ffn_q_b, L0_ffn_k_w, L0_ffn_k_b, L0_ffn_v_w, L0_ffn_v_b, L0_ffn_o_w, L0_ffn_o_b, L0_ffn_router_w, L0_ffn_router_b, L0_ffn_sh_w1, L0_ffn_sh_b1, L0_ffn_sh_w2, L0_ffn_sh_b2, L0_ffn_re_w1, L0_ffn_re_b1, L0_ffn_re_w2, L0_ffn_re_b2)
    x = x + _L1_xattn_ref(ctx_768, _layernorm(x, axis=-1), mask_BxS2_bk0, L1_xattn_ln_x_g, L1_xattn_ln_x_b, L1_xattn_ln_l_g, L1_xattn_ln_l_b, L1_xattn_qn_g, L1_xattn_kn_g, L1_xattn_Wq, L1_xattn_Wkv, L1_xattn_Wlkv, L1_xattn_Wo, L1_xattn_bo)
    x = x + _L1_attn_ref(_layernorm(x, axis=-1), L1_attn_Wq, L1_attn_bq, L1_attn_Wk, L1_attn_bk, L1_attn_Wv, L1_attn_bv, L1_attn_Wp, L1_attn_bp)
    x = x + _L1_ffn_ref(_layernorm(x, axis=-1), L1_ffn_norm_weight, L1_ffn_router_w, L1_ffn_sw1, L1_ffn_sb1, L1_ffn_sw2, L1_ffn_sb2, L1_ffn_ew1, L1_ffn_eb1, L1_ffn_ew2, L1_ffn_eb2)
    return x

_drawn_inputs = setup_inputs


def setup_inputs(seed=0):
    import zlib

    import numpy as np

    out = dict(_drawn_inputs(seed))
    spreads = {'L0_ffn_gamma1': (1.0, 0.2),
     'L0_ffn_gamma2': (1.0, 0.2),
     'L0_ffn_q_b': (0.0, 0.8),
     'L0_ffn_k_b': (0.0, 0.8),
     'L0_ffn_v_b': (0.0, 0.1),
     'L0_ffn_o_b': (0.0, 0.1),
     'L0_ffn_router_b': (0.0, 0.8),
     'L0_ffn_sh_b1': (0.0, 0.741),
     'L0_ffn_sh_b2': (0.0, 0.1),
     'L0_ffn_re_b1': (0.0, 0.8),
     'L0_ffn_re_b2': (0.0, 0.8),
     'L1_xattn_ln_x_g': (1.0, 0.2),
     'L1_xattn_ln_x_b': (0.0, 0.1),
     'L1_xattn_ln_l_g': (1.0, 0.2),
     'L1_xattn_ln_l_b': (0.0, 0.34),
     'L1_xattn_qn_g': (1.0, 0.6),
     'L1_xattn_kn_g': (1.0, 0.6),
     'L1_xattn_bo': (0.0, 0.1),
     'L1_attn_bq': (0.0, 0.484),
     'L1_attn_bk': (0.0, 0.8),
     'L1_attn_bv': (0.0, 0.1),
     'L1_attn_bp': (0.0, 0.1),
     'L1_ffn_norm_weight': (1.0, 0.2),
     'L1_ffn_sb1': (0.0, 0.393),
     'L1_ffn_sb2': (0.0, 0.284),
     'L1_ffn_eb1': (0.0, 0.575),
     'L1_ffn_eb2': (0.0, 0.385)}
    factors = {'L0_xattn_bo': 3.074,
     'L0_attn_W_q': 8.0,
     'L0_attn_W_k': 8.0,
     'L0_ffn_theta': 8.0,
     'L0_ffn_q_w': 8.0,
     'L0_ffn_k_w': 8.0,
     'L0_ffn_router_w': 8.0,
     'L0_ffn_sh_w1': 3.794,
     'L0_ffn_sh_w2': 3.722,
     'L0_ffn_re_w1': 8.0,
     'L0_ffn_re_w2': 8.0}
    for name, (base, spread) in spreads.items():
        noise = np.random.default_rng([zlib.crc32(name.encode()), seed]).standard_normal(out[name].shape)
        drawn = base * np.exp(spread * noise) if base else spread * noise
        out[name] = jnp.asarray(drawn.astype(out[name].dtype))
    for name, factor in factors.items():
        out[name] = (out[name] * factor).astype(out[name].dtype)
    return out
```

```python
from contextlib import ExitStack

import concourse.bass as bass
from concourse import mybir

F32 = mybir.dt.float32
BF16 = mybir.dt.bfloat16
U8 = mybir.dt.uint8
ALU = mybir.AluOpType
ACT = mybir.ActivationFunctionType
AX = mybir.AxisListType

P = 128
BATCHES = 16
S = 64
PAIRS = BATCHES // 2
ROWS = BATCHES * S
D = 128
CTX = 1601
DC = 96
FULL = CTX // P
KT = FULL + 1
REST = CTX - FULL * P
BANK = 512
NEG = -1.0e30


def rows_of(k):
    return P if k < FULL else REST


class Core:
    pass


class Tally:

    def __init__(self, sem):
        self.sem, self.base = sem, 0

    def wait(self, eng, n):
        eng.wait_ge(self.sem, n + self.base)

    def close(self, n):
        self.base += n


class Chain:

    def __init__(self, eng, sem, base=0):
        self.eng, self.sem, self.base, self.n = eng, sem, base, 0

    def mark(self, ins):
        self.n += 1
        ins.then_inc(self.sem, 1)

    def settle(self):
        self.eng.wait_ge(self.sem, self.base + self.n)

    def link(self, ins):
        self.mark(ins)
        self.settle()


def load_stage(nc, m, dram):
    loaded = m.sem("inputs_loaded")
    zeroed = m.sem("buffers_set")
    casted = m.sem("constants_cast")
    n_loads = [0]
    with nc.Block() as block:
        @block.sync
        def _(sp):
            def load(dst, src):
                sp.dma_start(dst, src).then_inc(loaded, 16)
                n_loads[0] += 1
            load(m.X[:], dram["x"].rearrange("(t b) s d -> (b s) t d", b=2))
            for dst, src in m.loads:
                load(dst, src)
            sp.wait_ge(loaded, 16 * n_loads[0])

        @block.gpsimd
        def _(pool):
            nc.gpsimd.memset(m.nhalf[:], -0.5).then_inc(zeroed, 1)
            nc.gpsimd.memset(m.half[:], 0.5).then_inc(zeroed, 1)
            nc.gpsimd.memset(m.ones[:], 1.0).then_inc(zeroed, 1)
            nc.gpsimd.memset(m.ones_bf[:], 1.0).then_inc(zeroed, 1)
            nc.gpsimd.memset(m.ctx_nat[:], 0.0).then_inc(zeroed, 1)
            pool.wait_ge(zeroed, 5)
            nc.gpsimd.memset(m.ctx_nat[:, :, :, DC:DC + 1], 1.0).then_inc(zeroed, 1)
            pool.wait_ge(zeroed, 6)

        @block.vector
        def _(dve):
            dve.wait_ge(loaded, 16 * (1 + len(m.loads)))
            nc.vector.tensor_copy(m.ident_bf[:], m.ident[:]).then_inc(casted, 1)
            nc.vector.tensor_copy(m.causal_bf[:], m.causal[:]).then_inc(casted, 1)
            nc.vector.tensor_copy(m.strided_bf[:], m.strided[:]).then_inc(casted, 1)
            dve.wait_ge(casted, 3)


def norm_stage(nc, m, name, src, nat, natT, passes):
    stats_ready, rstd_ready, own, nat_ready, turned, natT_ready = (m.tally(n) for n in (
        "norm_stats_ready", "norm_rstd_ready", "norm_dve_steps", "norm_rows_ready", "norm_turned", "norm_copied"))
    with ExitStack() as ctx:
        sb = m.scoped(ctx, name)
        st6, mv = sb("st6", [P, PAIRS, 6]), sb("mv", [P, PAIRS, 2])
        ve, rstd = sb("ve", [P, PAIRS]), sb("rstd", [P, PAIRS])
        with nc.Block() as block:
            @block.vector
            def _(dve):
                chain = Chain(dve, own.sem, own.base)
                cur = src
                for i, (kind, eps, gain, shift) in enumerate(passes):
                    for t in range(PAIRS):
                        chain.mark(nc.vector.bn_stats(st6[:, t, :], cur[:, t, :]))
                    chain.settle()
                    for t in range(PAIRS):
                        chain.mark(nc.vector.bn_aggr(mv[:, t, :], st6[:, t, :]))
                    chain.settle()
                    if kind == "rms":
                        chain.link(nc.vector.tensor_tensor(ve[:], mv[:, :, 0], mv[:, :, 0], ALU.mult))
                        chain.link(nc.vector.tensor_tensor(ve[:], ve[:], mv[:, :, 1], ALU.add))
                        nc.vector.tensor_scalar(ve[:], ve[:], eps, None, ALU.add).then_inc(stats_ready.sem, 1)
                    else:
                        nc.vector.tensor_scalar(ve[:], mv[:, :, 1], eps, None, ALU.add).then_inc(stats_ready.sem, 1)
                    rstd_ready.wait(dve, i + 1)
                    for t in range(PAIRS):
                        if kind == "rms":
                            chain.mark(nc.vector.tensor_scalar(nat[:, t, :], cur[:, t, :], rstd[:, t:t + 1], None,
                                                               ALU.mult))
                        else:
                            chain.mark(nc.vector.tensor_scalar(nat[:, t, :], cur[:, t, :], mv[:, t, 0:1],
                                                               rstd[:, t:t + 1], ALU.subtract, ALU.mult))
                    for table, op in ((gain, ALU.mult), (shift, ALU.add)):
                        if table is not None:
                            chain.settle()
                            both = table[:].unsqueeze(1).broadcast_to([P, PAIRS, D])
                            chain.mark(nc.vector.tensor_tensor(nat[:], nat[:], both, op))
                    chain.settle()
                    cur = nat
                own.close(chain.n)
                nc.vector.tensor_copy(ve[:, 0:1], nat[:, 0, 0:1]).then_inc(nat_ready.sem, 1)

            @block.gpsimd
            def _(pool):
                for i in range(len(passes)):
                    stats_ready.wait(pool, i + 1)
                    nc.gpsimd.tensor_tensor(rstd[:], ve[:], m.nhalf[:, 0:PAIRS], ALU.pow).then_inc(rstd_ready.sem, 1)

            @block.tensor
            def _(pe):
                nat_ready.wait(pe, 1)
                for t in range(PAIRS):
                    out = m.ps[:, t // 4, (t % 4) * P:(t % 4 + 1) * P]
                    ins = nc.tensor.transpose(out, nat[:, t, :], m.ident[:])
                    if t % 4 == 3:
                        ins.then_inc(turned.sem, 1)

            @block.scalar
            def _(act):
                for h in range(2):
                    turned.wait(act, h + 1)
                    nc.scalar.copy(natT[:, h * BANK:(h + 1) * BANK], m.ps[:, h, :]).then_inc(natT_ready.sem, 1)
                natT_ready.wait(act, 2)
    for tally, n in ((stats_ready, len(passes)), (rstd_ready, len(passes)), (nat_ready, 1), (turned, 2),
                     (natT_ready, 2)):
        tally.close(n)


def l0_fold_stage(nc, m):
    folded, copied = m.sem("l0_folded"), m.sem("l0_fold_copied")
    nv_copied, ub_cast = m.sem("l0_nv_copied"), m.sem("l0_ub_cast")
    u_made, u_copied = m.sem("l0_u_made"), m.sem("l0_u_copied")
    H = m.H0
    with nc.Block() as block:
        @block.tensor
        def _(pe):
            for h in range(H):
                ins = nc.tensor.matmul(m.ps[:, h // 4, (h % 4) * P:(h % 4) * P + DC], m.wqT0[:, h, :],
                                       m.wkT0[:, h, :], start=True, stop=True)
            ins.then_inc(folded, 1)
            for h in range(H):
                ins = nc.tensor.matmul(m.ps[0:DC, 2 + h // 4, (h % 4) * P:(h % 4 + 1) * P], m.wvT0[:, h, :],
                                       m.wo0[:, h, :], start=True, stop=True)
            ins.then_inc(folded, 1)
            pe.wait_ge(copied, 1)
            for n in range(2 * H):
                h, half = n // 2, n % 2
                if n >= 4:
                    pe.wait_ge(u_copied, n - 3)
                nc.tensor.matmul(m.ps[0:DC, 4 + n % 4, :], m.mq0[:, h, 0:DC],
                                 m.xT[:, half * BANK:(half + 1) * BANK], start=True, stop=True).then_inc(u_made, 1)

        @block.scalar
        def _(act):
            act.wait_ge(folded, 1)
            nc.scalar.copy(m.mq0[:, :, 0:DC], m.ps[:, 0:2, :].rearrange("p b (h d) -> p (b h) d", d=P)[:, :, 0:DC]
                           ).then_inc(copied, 1)
            for n in range(0, 2 * H):
                h, half = n // 2, n % 2
                act.wait_ge(u_made, n + 1)
                nc.scalar.activation(m.U[0:DC, 8 * half:8 * half + 8, h, :],
                                     m.ps[0:DC, 4 + n % 4, :].rearrange("p (b i) -> p b i", i=S), ACT.Copy,
                                     scale=float(64) ** -0.5).then_inc(u_copied, 1)
            act.wait_ge(u_copied, 2 * H)

        @block.vector
        def _(dve):
            dve.wait_ge(folded, 2)
            nc.vector.tensor_copy(m.nv0[:], m.ps[0:DC, 2:4, :].rearrange("p b (h d) -> p (b h) d", d=P)
                                  ).then_inc(nv_copied, 1)
            dve.wait_ge(nv_copied, 1)
            dve.wait_ge(u_copied, 2 * H)
            for half in range(2):
                nc.vector.tensor_copy(m.Ub[:, 8 * half:8 * half + 8], m.U[0:DC, 8 * half:8 * half + 8]
                                      ).then_inc(ub_cast, 1)
            dve.wait_ge(ub_cast, 2)


def l0_cross_stage(nc, m, dram):
    H = m.H0
    HS = H * S
    ps = m.ps
    MAXB, SB, OB, YB = 0, 4, 6, 7
    ctx_loaded = [m.sem("l0_ctx_loaded_even"), m.sem("l0_ctx_loaded_odd")]
    ctxb_cast = m.sem("l0_ctx_cast")
    rough_ready, rough_used = m.sem("l0_rough_scores_ready"), m.sem("l0_rough_scores_used")
    maxrow_turned, maxrow_written = m.sem("l0_max_turned"), m.sem("l0_max_row_written")
    scores_ready, probs_ready, probs_used = m.sem("l0_scores_ready"), m.sem("l0_probs_ready"), m.sem("l0_probs_used")
    o_copied, recip_ready = m.sem("l0_output_copied"), m.sem("l0_reciprocal_ready")
    spread_ready, o_scaled = m.sem("l0_reciprocal_spread"), m.sem("l0_output_scaled")
    y_ready, x_updated = m.sem("l0_y_ready"), m.sem("l0_x_updated")
    with ExitStack() as ctx:
        sb = m.scoped(ctx, "l0")
        ctxT = sb("ctxT", [DC + 1, 2, CTX])
        ctxTb = sb("ctxTb", [DC, 2, CTX], BF16)
        probs = sb("probs", [P, 2, HS])
        mx = sb("mx", [P, 2, 4])
        osum = sb("osum", [DC + 1, HS])
        recip = sb("recip", [1, HS])
        on = sb("on", [DC, H, P])
        ones_set = m.sem("l0_ones_row_set")

        with nc.Block() as block:
            @block.sync
            def _(sp):
                def load(b, j):
                    jj = bass.ds(j, 1)
                    sp.dma_start(ctxT[0:DC, b, :], dram["ctxT"][jj].rearrange("o d k -> (o d) k")
                                 ).then_inc(ctx_loaded[b], 16)
                    sp.dma_start(m.ctx_nat[:, b, 0:FULL, 0:DC],
                                 dram["ctx"][jj, 0:FULL * P, :].rearrange("o (k p) d -> (o p) k d", p=P)
                                 ).then_inc(ctx_loaded[b], 16)
                    sp.dma_start(m.ctx_nat[0:REST, b, FULL, 0:DC],
                                 dram["ctx"][jj, FULL * P:CTX, :].rearrange("o p d -> (o p) d")
                                 ).then_inc(ctx_loaded[b], 16)
                load(0, 0)
                load(1, 1)
                with sp.Fori(0, PAIRS - 1) as t:
                    for b in range(2):
                        sp.wait_ge(probs_used, 2 + KT * (2 * t + b + 1))
                        load(b, 2 * t + 2 + b)

            @block.gpsimd
            def _(pool):
                nc.gpsimd.memset(ctxT[DC:DC + 1, :, :], 1.0).then_inc(ones_set, 1)

                def cast(b, t):
                    pool.wait_ge(ctx_loaded[b], 48 * (t + 1))
                    pool.sem_inc(m.turns_pool, 1)
                    nc.gpsimd.tensor_copy(ctxTb[:, b, :], ctxT[0:DC, b, :]).then_inc(ctxb_cast, 1)
                cast(0, 0)
                cast(1, 0)
                with pool.Fori(1, PAIRS) as t:
                    for b in range(2):
                        pool.wait_ge(rough_ready, 4 * (2 * t + b - 1))
                        cast(b, t)

            def rough(pe, b, j, r):
                if r == 0:
                    pe.wait_ge(ctxb_cast, j + 1)
                pe.wait_ge(rough_used, 1 + 4 * j + r)
                for c in range(4):
                    n = min(BANK, CTX - c * BANK)
                    ins = nc.tensor.matmul(
                        ps[:, MAXB + c, 0:n],
                        m.Ub[:, bass.ds(j, 1), 2 * r:2 * r + 2, :].rearrange("p o h i -> p (o h i)"),
                        ctxTb[:, b, c * BANK:c * BANK + n], start=True, stop=True)
                ins.then_inc(rough_ready, 1)

            def turn_max(pe, b, j):
                pe.wait_ge(rough_used, 1 + 4 * (j + 1))
                for r in range(4):
                    ins = nc.tensor.matmul(ps[0:1, YB, r * P:(r + 1) * P], mx[:, b, r:r + 1], m.ident[:],
                                           start=True, stop=True)
                ins.then_inc(maxrow_turned, 1)

            def pe_pair(pe, t, last):
                for b in range(2):
                    j = 2 * t + b
                    lastb = last and b == 1
                    pe.wait_ge(maxrow_written, j + 1)

                    def scores(k):
                        r = rows_of(k)
                        nc.tensor.matmul(ps[0:r, SB + (KT * b + k) % 2, :], ctxT[:, b, k * P:k * P + r],
                                         m.U[:, bass.ds(j, 1), :, :].rearrange("p o h i -> p (o h i)"),
                                         start=True, stop=True).then_inc(scores_ready, 1)
                    scores(0)
                    for k in range(KT):
                        if k + 1 < KT:
                            scores(k + 1)
                        if not lastb and k in (1, 3, 6, 9):
                            rough(pe, 1 - b, j + 1, (1, 3, 6, 9).index(k))
                        pe.wait_ge(probs_ready, KT * j + k + 1)
                        if k == 0:
                            pe.wait_ge(o_copied, 1 + j)
                        r = rows_of(k)
                        nc.tensor.matmul(ps[0:DC + 1, OB, :], m.ctx_nat[0:r, b, k, :], probs[0:r, (KT * b + k) % 2, :],
                                         start=(k == 0), stop=(k == KT - 1)).then_inc(probs_used, 1)
                    if not lastb:
                        if b == 0:
                            pe.wait_ge(x_updated, 1 + t)
                        else:
                            pe.wait_ge(o_scaled, 1 + 2 * t + 1)
                        turn_max(pe, 1 - b, j + 1)
                    pe.wait_ge(recip_ready, j + 1)
                    if lastb:
                        pe.wait_ge(o_scaled, 1 + j)
                    else:
                        pe.wait_ge(maxrow_written, j + 2)
                    nc.tensor.matmul(ps[0:DC, YB, :], m.ones[0:1, 0:DC], recip[:], start=True, stop=True
                                     ).then_inc(spread_ready, 1)
                pe.wait_ge(o_scaled, 1 + 2 * t + 2)
                for h in range(H):
                    nc.tensor.matmul(ps[:, YB, 0:D], on[:, h, :], m.nv0[:, h, :], start=(h == 0), stop=False)
                nc.tensor.matmul(ps[:, YB, 0:D], m.ones[0:1, 0:P], m.bo0[:], start=False, stop=True
                                 ).then_inc(y_ready, 1)

            @block.tensor
            def _(pe):
                pe.sem_inc(probs_used, 2)
                pe.wait_ge(ones_set, 1)
                pe.wait_ge(ctx_loaded[0], 48)
                for r in range(4):
                    rough(pe, 0, 0, r)
                turn_max(pe, 0, 0)
                with pe.Fori(0, PAIRS - 1) as t:
                    pe_pair(pe, t, False)
                pe_pair(pe, PAIRS - 1, True)

            def act_pair(act, t):
                for b in range(2):
                    j = 2 * t + b
                    for k in range(KT):
                        act.wait_ge(scores_ready, KT * j + k + 1)
                        act.wait_ge(probs_used, KT * j + k + 1)
                        r = rows_of(k)
                        nc.scalar.activation(probs[0:r, (KT * b + k) % 2, :], ps[0:r, SB + (KT * b + k) % 2, :], ACT.Exp
                                             ).then_inc(probs_ready, 1)
                    act.wait_ge(probs_used, 2 + KT * (j + 1))
                    act.wait_ge(o_scaled, 1 + j)
                    nc.scalar.copy(osum[:], ps[0:DC + 1, OB, :]).then_inc(o_copied, 1)

            @block.scalar
            def _(act):
                act.sem_inc(o_copied, 1)
                with act.Fori(0, PAIRS) as t:
                    act_pair(act, t)

            def take_max(dve, b, j):
                for r in range(4):
                    dve.wait_ge(rough_ready, 4 * j + r + 1)
                    nc.vector.tensor_reduce(mx[:, b, r:r + 1],
                                            ps[:, MAXB:MAXB + 4, :].rearrange("p c n -> p (c n)")[:, 0:CTX],
                                            axis=AX.X, op=ALU.max).then_inc(rough_used, 1)
                dve.wait_ge(maxrow_turned, j + 1)
                nc.vector.tensor_scalar(m.U[DC:DC + 1, bass.ds(j, 1), :, :].rearrange("p o h i -> p (o h i)"),
                                        ps[0:1, YB, :], -1.0, None, ALU.mult).then_inc(maxrow_written, 1)

            def dve_pair(dve, t, last):
                for b in range(2):
                    j = 2 * t + b
                    if not (last and b == 1):
                        take_max(dve, 1 - b, j + 1)
                    dve.wait_ge(o_copied, 2 + j)
                    nc.vector.reciprocal(recip[:], osum[DC:DC + 1, :]).then_inc(recip_ready, 1)
                    dve.wait_ge(spread_ready, j + 1)
                    nc.vector.tensor_tensor(on[:, :, S * b:S * b + S],
                                            osum[0:DC, :].rearrange("p (h i) -> p h i", i=S),
                                            ps[0:DC, YB, :].rearrange("p (h i) -> p h i", i=S), ALU.mult
                                            ).then_inc(o_scaled, 1)
                dve.wait_ge(y_ready, t + 1)
                xt = m.X[:, bass.ds(t, 1), :].rearrange("p o d -> p (o d)")
                nc.vector.tensor_tensor(xt, xt, ps[:, YB, 0:D], ALU.add).then_inc(x_updated, 1)

            @block.vector
            def _(dve):
                dve.sem_inc(rough_used, 1)
                dve.sem_inc(x_updated, 1)
                dve.sem_inc(o_scaled, 1)
                take_max(dve, 0, 0)
                with dve.Fori(0, PAIRS - 1) as t:
                    dve_pair(dve, t, False)
                dve_pair(dve, PAIRS - 1, True)


HP = 8


def project_small_heads_stage(nc, m, name, w, rope, bias):
    made, copied = m.sem(name + "_made"), m.sem(name + "_copied")
    own = m.sem(name + "_dve_steps")
    ps = m.ps
    n_qk = 4 if rope else 2
    with ExitStack() as ctx:
        sb = m.scoped(ctx, name)
        a, b = sb("a", [P, ROWS]), sb("b", [P, ROWS])
        with nc.Block() as block:
            @block.tensor
            def _(pe):
                for n in range(n_qk):
                    for half in range(2):
                        ins = nc.tensor.matmul(ps[:, 2 * n + half, :], w[n][:],
                                               m.xT[:, half * BANK:(half + 1) * BANK], start=True, stop=True)
                    ins.then_inc(made, 1)
                pe.wait_ge(copied if bias else own, 1 if bias else 3)
                if bias:
                    pe.wait_ge(copied, 2)
                for j in range(BATCHES):
                    ins = nc.tensor.matmul(ps[0:S, j // 4, (j % 4) * P:(j % 4 + 1) * P], m.xT[:, j * S:(j + 1) * S],
                                           w[-1][:], start=True, stop=True)
                ins.then_inc(made, 1)

            if bias:
                @block.scalar
                def _(act):
                    for n, dst in ((0, m.qT), (1, m.kT)):
                        act.wait_ge(made, n + 1)
                        nc.scalar.activation(dst[:], ps[:, 2 * n:2 * n + 2, :].rearrange("p b n -> p (b n)"),
                                             ACT.Identity, bias=bias[n][:]).then_inc(copied, 1)
                    act.wait_ge(copied, 2)

            @block.vector
            def _(dve):
                chain = Chain(dve, own)
                if rope:
                    cos = m.cosb[:].unsqueeze(1).broadcast_to([P, BATCHES, S])
                    sin = m.sinb[:].unsqueeze(1).broadcast_to([P, BATCHES, S])
                    for n, dst in ((0, m.qT), (2, m.kT)):
                        for i, (tmp, table) in enumerate(((a, cos), (b, sin))):
                            dve.wait_ge(made, n + i + 1)
                            src = ps[:, 2 * (n + i):2 * (n + i) + 2, :].rearrange("p c (b i) -> p (c b) i", i=S)
                            chain.mark(nc.vector.tensor_tensor(tmp[:].rearrange("p (b i) -> p b i", i=S), src, table,
                                                               ALU.mult))
                        chain.settle()
                        chain.link(nc.vector.tensor_tensor(dst[:], a[:], b[:], ALU.add))
                dve.wait_ge(made, n_qk + 1)
                src = ps[0:S, 0:4, :].rearrange("p b (j d) -> p (b j) d", d=D)
                if bias:
                    chain.link(nc.vector.tensor_tensor(m.V[:], src, bias[2][:].unsqueeze(1).broadcast_to([S, BATCHES, D]),
                                                       ALU.add))
                else:
                    chain.link(nc.vector.tensor_copy(m.V[:], src))


class Softmax:

    def __init__(self, nc, m, name, sb, scale):
        self.nc, self.m, self.scale = nc, m, scale
        self.less, self.exps, self.probs = (sb(n, [P, 2, BANK]) for n in ("less", "exps", "probs"))
        self.probsT = sb("probsT", [S, 2, HP * P])
        self.mx, self.sums, self.recip = (sb(n, [P, 2, HP]) for n in ("mx", "sums", "recip"))
        self.signals = {n: m.tally("softmax_" + n) for n in (
            "scores_ready", "mx_ready", "less_ready", "exps_ready", "sums_ready", "recip_ready", "probs_ready",
            "turned", "probsT_ready")}
        (self.scores_ready, self.mx_ready, self.less_ready, self.exps_ready, self.sums_ready, self.recip_ready,
         self.probs_ready, self.turned, self.probsT_ready) = self.signals.values()

    def close(self):
        for tally in self.signals.values():
            tally.close(BATCHES)

    @staticmethod
    def by_head(ap):
        return ap.rearrange("p (h k) -> p h k", k=S)

    def less_max(self, dve, b, j):
        nc = self.nc
        scores = self.by_head(self.m.ps[:, b, :])
        self.scores_ready.wait(dve, j + 1)
        nc.vector.tensor_reduce(self.mx[:, b, :], scores, axis=AX.X, op=ALU.max).then_inc(self.mx_ready.sem, 1)
        self.mx_ready.wait(dve, j + 1)
        nc.vector.tensor_tensor(self.by_head(self.less[:, b, :]), scores,
                                self.mx[:, b, :].unsqueeze(2).broadcast_to([P, HP, S]), ALU.subtract
                                ).then_inc(self.less_ready.sem, 1)

    def exp(self, act, b, j):
        self.less_ready.wait(act, j + 1)
        self.nc.scalar.activation(self.exps[:, b, :], self.less[:, b, :], ACT.Exp, scale=self.scale
                                  ).then_inc(self.exps_ready.sem, 1)

    def sum(self, dve, b, j):
        nc = self.nc
        self.exps_ready.wait(dve, j + 1)
        nc.vector.tensor_reduce(self.sums[:, b, :], self.by_head(self.exps[:, b, :]), axis=AX.X, op=ALU.add
                                ).then_inc(self.sums_ready.sem, 1)
        self.sums_ready.wait(dve, j + 1)
        nc.vector.reciprocal(self.recip[:, b, :], self.sums[:, b, :]).then_inc(self.recip_ready.sem, 1)

    def divide(self, pool, b, j):
        self.recip_ready.wait(pool, j + 1)
        self.nc.gpsimd.tensor_tensor(self.by_head(self.probs[:, b, :]), self.by_head(self.exps[:, b, :]),
                                     self.recip[:, b, :].unsqueeze(2).broadcast_to([P, HP, S]), ALU.mult
                                     ).then_inc(self.probs_ready.sem, 1)

    def turn(self, pe, b, j):
        self.probs_ready.wait(pe, j + 1)
        pe.sem_inc(self.m.turns_pe, 1)
        for hp in range(HP):
            ins = self.nc.tensor.transpose(self.m.ps[0:S, 2 + 2 * b + hp // 4, (hp % 4) * P:(hp % 4 + 1) * P],
                                           self.probs[:, b, hp * S:(hp + 1) * S], self.m.ident[:])
        ins.then_inc(self.turned.sem, 1)

    def copy_turned(self, act, b, j):
        self.turned.wait(act, j + 1)
        self.nc.scalar.copy(self.probsT[:, b, :], self.m.ps[0:S, 2 + 2 * b:4 + 2 * b, :].rearrange("p c n -> p (c n)")
                            ).then_inc(self.probsT_ready.sem, 1)


def small_heads_stage(nc, m, name, mask_bf, wo, bo):
    ps = m.ps
    per_y = 1 if bo is None else 2
    signals = [m.tally("heads_" + n) for n in ("operands_ready", "pv_ready", "o_copied", "o_turned", "oT_copied",
                                               "y_ready", "x_updated")]
    operands_ready, pv_ready, o_copied, o_turned, oT_copied, y_ready, x_updated = signals
    with ExitStack() as ctx:
        sb = m.scoped(ctx, name)
        sm = Softmax(nc, m, name, sb, float(8) ** -0.5)
        q2, kb = sb("q2", [P, 2, 2, S]), sb("kb", [P, 2, HP, S])
        o, oT = sb("o", [P, HP, 2, 8]), sb("oT", [P, P])
        with nc.Block() as block:
            @block.tensor
            def _(pe):
                with pe.Fori(0, PAIRS) as t:
                    for b in range(2):
                        operands_ready.wait(pe, 2 * (2 * t + b) + 2)
                        nc.tensor.matmul(ps[:, b, :], m.ident_bf[:], mask_bf[:], start=True, stop=False)
                        nc.tensor.matmul(ps[:, b, :], q2[:, b].rearrange("p h i -> p (h i)"),
                                         kb[:, b].rearrange("p h k -> p (h k)"), start=False, stop=True
                                         ).then_inc(sm.scores_ready.sem, 1)
                    for b in range(2):
                        j = 2 * t + b
                        sm.turn(pe, b, j)
                        sm.probsT_ready.wait(pe, j + 1)
                        for hp in range(HP):
                            ins = nc.tensor.matmul(
                                ps[:, 6 + b, 16 * hp:16 * (hp + 1)], sm.probsT[:, b, hp * P:(hp + 1) * P],
                                m.V[:, bass.ds(j, 1), 16 * hp:16 * (hp + 1)].rearrange("p o d -> p (o d)"),
                                start=True, stop=True)
                        ins.then_inc(pv_ready.sem, 1)
                    o_copied.wait(pe, 4 * t + 4)
                    nc.tensor.transpose(ps[:, 7, 2 * P:3 * P], o[:].rearrange("p a b d -> p (a b d)"), m.ident[:]
                                        ).then_inc(o_turned.sem, 1)
                    oT_copied.wait(pe, t + 1)
                    nc.tensor.matmul(ps[:, 6, P:2 * P], oT[:], wo[:], start=True, stop=bo is None
                                     ).then_inc(y_ready.sem, 1)
                    if bo is not None:
                        nc.tensor.matmul(ps[:, 6, P:2 * P], m.ones[0:1, 0:P], bo[:], start=False, stop=True
                                         ).then_inc(y_ready.sem, 1)
            @block.scalar
            def _(act):
                with act.Fori(0, PAIRS) as t:
                    for b in range(2):
                        sm.exp(act, b, 2 * t + b)
                    for b in range(2):
                        sm.copy_turned(act, b, 2 * t + b)
                    o_turned.wait(act, t + 1)
                    nc.scalar.copy(oT[:], ps[:, 7, 2 * P:3 * P]).then_inc(oT_copied.sem, 1)

            @block.gpsimd
            def _(pool):
                with pool.Fori(0, PAIRS) as t:
                    for b in range(2):
                        sm.divide(pool, b, 2 * t + b)

            @block.vector
            def _(dve):
                with dve.Fori(0, PAIRS) as t:
                    for b in range(2):
                        cols = bass.ds((2 * t + b) * S, S)
                        nc.vector.tensor_tensor(q2[:, b], m.qT[:, cols].unsqueeze(1).broadcast_to([P, 2, S]),
                                                m.qmask[:].unsqueeze(2).broadcast_to([P, 2, S]), ALU.mult
                                                ).then_inc(operands_ready.sem, 1)
                        nc.vector.tensor_tensor(kb[:, b], m.kT[:, cols].unsqueeze(1).broadcast_to([P, HP, S]),
                                                m.kmask[:].unsqueeze(2).broadcast_to([P, HP, S]), ALU.mult
                                                ).then_inc(operands_ready.sem, 1)
                    for b in range(2):
                        sm.less_max(dve, b, 2 * t + b)
                    for b in range(2):
                        sm.sum(dve, b, 2 * t + b)
                    for b in range(2):
                        pv_ready.wait(dve, 2 * t + b + 1)
                        for h2 in range(2):
                            src = ps[S * h2:S * h2 + S, 6 + b, 0:P].rearrange("p (h c) -> p h c", c=16)
                            nc.vector.tensor_copy(o[S * b:S * b + S, :, h2, :], src[:, :, 8 * h2:8 * h2 + 8]
                                                  ).then_inc(o_copied.sem, 1)
                    y_ready.wait(dve, per_y * (t + 1))
                    xt = m.X[:, bass.ds(t, 1), :].rearrange("p o d -> p (o d)")
                    nc.vector.tensor_tensor(xt, xt, ps[:, 6, P:2 * P], ALU.add).then_inc(x_updated.sem, 1)
    for tally, per_pair in zip(signals, (4, 2, 4, 1, 1, per_y, 1)):
        tally.close(per_pair * PAIRS)
    sm.close()


def angles_stage(nc, m):
    own, pool_steps, done = m.sem("angles_dve_steps"), m.sem("angles_pool_steps"), m.sem("angles_done")
    ready = m.sem("angles_ready")
    TWO_PI, PI = 6.283185307179586, 3.1415925
    C1 = 6.28125
    C2 = 0.0019350051879882812
    C3 = TWO_PI - C1 - C2
    ROUND = 12582912.0
    with ExitStack() as ctx:
        sb = m.scoped(ctx, "angles")
        a, n, r = sb("a", [P, P]), sb("n", [P, P]), sb("r", [P, P])
        with nc.Block() as block:
            @block.vector
            def _(dve):
                chain = Chain(dve, own)
                chain.link(nc.vector.tensor_scalar(a[:], m.pos[:], m.theta[:], None, ALU.mult))
                chain.link(nc.vector.tensor_scalar(n[:], a[:], 1.0 / TWO_PI, ROUND, ALU.mult, ALU.add))
                chain.link(nc.vector.tensor_scalar(n[:], n[:], -ROUND, None, ALU.add))
                for c in (C1, C2, C3):
                    chain.link(nc.vector.scalar_tensor_tensor(out=a[:], in0=n[:], scalar=-c, in1=a[:], op0=ALU.mult,
                                                              op1=ALU.add))
                chain.link(nc.vector.tensor_scalar(a[:], a[:], PI, -PI, ALU.min, ALU.max))
                chain.link(nc.vector.tensor_scalar(r[:], a[:], -1.0, None, ALU.mult))
                chain.link(nc.vector.tensor_tensor(r[:], r[:], a[:], ALU.max))
                chain.link(nc.vector.tensor_scalar(r[:], r[:], -1.0, TWO_PI / 4, ALU.mult, ALU.add))
                nc.vector.tensor_copy(n[:, 0:1], r[:, 0:1]).then_inc(ready, 1)
                dve.wait_ge(done, 2)
                chain.link(nc.vector.tensor_scalar(m.sinc[:], m.sinc[:], m.rope_sign[:], None, ALU.mult))

            @block.scalar
            def _(act):
                act.wait_ge(ready, 1)
                nc.scalar.activation(m.sinc[:], a[:], ACT.Sin).then_inc(done, 1)
                nc.scalar.activation(m.cosc[:], r[:], ACT.Sin).then_inc(done, 1)
                act.wait_ge(done, 2)


def wide_heads_stage(nc, m):
    ps = m.ps
    name = "wide"
    xs_ready = m.sem("wide_x_staged")
    proj_ready, proj_used = m.sem("wide_projected"), m.sem("wide_projection_used")
    rot_ready = m.sem("wide_rotated")
    v_made, v_copied = m.sem("wide_v_made"), m.sem("wide_v_copied")
    pv_ready, o_copied = m.sem("wide_pv_ready"), m.sem("wide_o_copied")
    y_ready, ao_ready = m.sem("wide_y_ready"), m.sem("wide_attn_out_ready")
    qbd_zeroed = m.sem("wide_qbd_zeroed")
    with ExitStack() as ctx:
        sb = m.scoped(ctx, name)
        sm = Softmax(nc, m, name, sb, float(64) ** -0.5)
        xs = sb("xs", [P, P])
        ta, tb = sb("ta", [P, 2, HP, P]), sb("tb", [P, 2, HP, P])
        qbd = sb("qbd", [P, 2, HP, P])
        kr = sb("kr", [P, HP, P])
        V = sb("v", [S, 2, HP * P])
        oT = sb("oT", [P, HP, P])
        with nc.Block() as block:
            @block.tensor
            def _(pe):
                pe.wait_ge(qbd_zeroed, 1)
                with pe.Fori(0, PAIRS) as t:
                    pe.wait_ge(xs_ready, t + 1)
                    for n in range(4):
                        if n >= 2:
                            pe.wait_ge(proj_used, 4 * t + n - 1)
                        for hp in range(HP):
                            ins = nc.tensor.matmul(ps[:, 2 + 2 * (n % 2) + hp // 4, (hp % 4) * P:(hp % 4 + 1) * P],
                                                   m.wqk[n][:, hp * P:(hp + 1) * P], xs[:], start=True, stop=True)
                        ins.then_inc(proj_ready, 1)
                    for b in range(2):
                        pe.wait_ge(proj_used, 4 * t + 3 + b)
                        for c in range(2):
                            nc.tensor.matmul(ps[0:S, 2 + 2 * b + c, :], xs[:, b * S:(b + 1) * S],
                                             m.wv_c[:, c * BANK:(c + 1) * BANK], start=True, stop=False)
                            ins = nc.tensor.matmul(ps[0:S, 2 + 2 * b + c, :], m.ones[0:1, 0:S],
                                                   m.bv_c[:, c * BANK:(c + 1) * BANK], start=False, stop=True)
                        ins.then_inc(v_made, 1)
                    pe.wait_ge(rot_ready, 3 * t + 3)
                    pe.wait_ge(ao_ready, t + 1)
                    for b in range(2):
                        nc.tensor.matmul(ps[:, b, :], m.ident_bf[:], m.causal_bf[:], start=True, stop=False)
                        for hp in range(HP):
                            ins = nc.tensor.matmul(ps[:, b, hp * S:(hp + 1) * S], qbd[:, b, hp, :],
                                                   kr[:, hp, b * S:(b + 1) * S], start=False, stop=(hp == HP - 1))
                        ins.then_inc(sm.scores_ready.sem, 1)
                    for b in range(2):
                        j = 2 * t + b
                        pe.wait_ge(v_copied, j + 1)
                        sm.turn(pe, b, j)
                        sm.probsT_ready.wait(pe, j + 1)
                        if b == 1:
                            pe.wait_ge(o_copied, 4 * t + 2)
                        for hp in range(HP):
                            ins = nc.tensor.matmul(ps[:, 6 + hp // 4, (hp % 4) * P:(hp % 4 + 1) * P],
                                                   V[:, b, hp * P:(hp + 1) * P], sm.probsT[:, b, hp * P:(hp + 1) * P],
                                                   start=True, stop=True)
                        ins.then_inc(pv_ready, 1)
                    pe.wait_ge(o_copied, 4 * t + 4)
                    for hp in range(HP):
                        nc.tensor.matmul(ps[:, 0, 0:D], oT[:, hp, :], m.wo_c[:, hp, :], start=(hp == 0), stop=False)
                    nc.tensor.matmul(ps[:, 0, 0:D], m.ones[0:1, 0:P], m.bo_c[:], start=False, stop=True
                                     ).then_inc(y_ready, 1)

            @block.scalar
            def _(act):
                with act.Fori(0, PAIRS) as t:
                    for b in range(2):
                        act.wait_ge(v_made, 2 * t + b + 1)
                        nc.scalar.copy(V[:, b, :], ps[0:S, 2 + 2 * b:4 + 2 * b, :].rearrange("p c n -> p (c n)")
                                       ).then_inc(v_copied, 1)
                    for b in range(2):
                        sm.exp(act, b, 2 * t + b)
                    for b in range(2):
                        sm.copy_turned(act, b, 2 * t + b)

            @block.gpsimd
            def _(pool):
                nc.gpsimd.memset(qbd[:], 0.0).then_inc(qbd_zeroed, 1)
                pool.wait_ge(qbd_zeroed, 1)
                with pool.Fori(0, PAIRS) as t:
                    pool.wait_ge(proj_used, 4 * t + 2)
                    for h2 in range(2):
                        rows = slice(S * h2, S * h2 + S)
                        nc.gpsimd.tensor_tensor(qbd[rows, :, :, S * h2:S * h2 + S],
                                                ta[rows, 0].rearrange("p h (b i) -> p b h i", b=2),
                                                tb[rows, 0].rearrange("p h (b i) -> p b h i", b=2), ALU.add
                                                ).then_inc(rot_ready, 1)
                    pool.wait_ge(rot_ready, 3 * t + 2)
                    pool.wait_ge(proj_used, 4 * t + 4)
                    nc.gpsimd.tensor_tensor(kr[:], ta[:, 1], tb[:, 1], ALU.add).then_inc(rot_ready, 1)
                    for b in range(2):
                        sm.divide(pool, b, 2 * t + b)

            @block.vector
            def _(dve):
                dve.sem_inc(ao_ready, 1)
                with dve.Fori(0, PAIRS) as t:
                    nc.vector.tensor_copy(xs[:], m.xT[:, bass.ds(t * P, P)]).then_inc(xs_ready, 1)
                    for n in range(4):
                        dve.wait_ge(proj_ready, 4 * t + n + 1)
                        dst, table = ((ta, m.cosc), (tb, m.sinc))[n % 2]
                        for hp in range(HP):
                            ins = nc.vector.scalar_tensor_tensor(
                                out=dst[:, n // 2, hp, :],
                                in0=ps[:, 2 + 2 * (n % 2) + hp // 4, (hp % 4) * P:(hp % 4 + 1) * P],
                                scalar=m.bqk[:, n, hp:hp + 1], in1=table[:], op0=ALU.add, op1=ALU.mult)
                        ins.then_inc(proj_used, 1)
                    for b in range(2):
                        sm.less_max(dve, b, 2 * t + b)
                    for b in range(2):
                        sm.sum(dve, b, 2 * t + b)
                    for b in range(2):
                        dve.wait_ge(pv_ready, 2 * t + b + 1)
                        for h2 in range(2):
                            rows = slice(S * h2, S * h2 + S)
                            src = ps[rows, 6:8, :].rearrange("p c (h i) -> p (c h) i", i=P)
                            nc.vector.tensor_copy(oT[rows, :, S * b:S * b + S], src[:, :, S * h2:S * h2 + S]
                                                  ).then_inc(o_copied, 1)
                    dve.wait_ge(y_ready, t + 1)
                    tt = bass.ds(t, 1)
                    nc.vector.tensor_tensor(m.AO[:, tt, :].rearrange("p o d -> p (o d)"), ps[:, 0, 0:D],
                                            m.Y[:, tt, :].rearrange("p o d -> p (o d)"), ALU.add
                                            ).then_inc(ao_ready, 1)
    sm.close()


LAT = S
KEYS = CTX + LAT
EPS_RMS = 1e-8


def l1_prepare_stage(nc, m):
    ps = m.ps
    shift_made, shift_copied = m.sem("l1_shift_made"), m.sem("l1_shift_copied")
    q_made, squared, powered = m.sem("l1_q_made"), m.sem("l1_q_squared"), m.sem("l1_q_norms")
    own, ss_ready, q_ready = m.sem("l1_prep_dve_steps"), m.sem("l1_q_squares_summed"), m.sem("l1_q_normed")
    q_turned, qbd_zeroed = m.sem("l1_q_turned"), m.sem("l1_qbd_zeroed")
    with ExitStack() as ctx:
        sb = m.scoped(ctx, "l1p")
        sq, qn = sb("sq", [P, PAIRS, D]), sb("qn", [P, PAIRS, D])
        ss, nrm, gain = sb("ss", [P, 16]), sb("nrm", [P, 16]), sb("gain", [P, D])
        with nc.Block() as block:
            @block.tensor
            def _(pe):
                nc.tensor.matmul(ps[0:1, 0, 0:2 * P], m.ln_x_b[:], m.wkv1[:], start=True, stop=True
                                 ).then_inc(shift_made, 1)
                for t in range(PAIRS):
                    ins = nc.tensor.matmul(ps[:, 2 + t // 4, (t % 4) * P:(t % 4 + 1) * P], m.xT[:, t * P:(t + 1) * P],
                                           m.wq1[:], start=True, stop=True)
                ins.then_inc(q_made, 1)
                pe.wait_ge(q_ready, 1)
                for t in range(PAIRS):
                    ins = nc.tensor.transpose(ps[:, 4 + t // 4, (t % 4) * P:(t % 4 + 1) * P], qn[:, t, :], m.ident[:])
                ins.then_inc(q_turned, 1)

            @block.scalar
            def _(act):
                act.wait_ge(shift_made, 1)
                nc.scalar.copy(m.WA[DC:DC + 1, :], ps[0:1, 0, 0:2 * P]).then_inc(shift_copied, 1)
                act.wait_ge(q_made, 1)
                nc.scalar.activation(sq[:], ps[:, 2:4, :].rearrange("p b (t d) -> p (b t) d", d=D), ACT.Square
                                     ).then_inc(squared, 1)
                act.wait_ge(shift_copied, 1)

            @block.gpsimd
            def _(pool):
                nc.gpsimd.memset(m.qbd1[:], 0.0).then_inc(qbd_zeroed, 1)
                pool.wait_ge(ss_ready, 1)
                nc.gpsimd.tensor_tensor(nrm[:], ss[:], m.half[:, 0:16], ALU.pow).then_inc(powered, 1)

            @block.vector
            def _(dve):
                chain, V = Chain(dve, own), nc.vector
                chain.mark(V.tensor_scalar(m.WA[0:DC, :], m.wkv1[:], m.ln_x_g[:], None, ALU.mult))
                chain.link(V.tensor_tensor(gain[:], m.qn_g[:], m.kn_g[:], ALU.mult))
                chain.link(V.tensor_scalar(gain[:], gain[:], float(64) ** -0.5, None, ALU.mult))
                dve.wait_ge(squared, 1)
                V.tensor_reduce(ss[:], sq[:].rearrange("p t (h d) -> p (t h) d", d=64), axis=AX.X, op=ALU.add
                                ).then_inc(ss_ready, 1)
                dve.wait_ge(powered, 1)
                chain.link(V.tensor_scalar(nrm[:], nrm[:], float(64) ** -0.5, EPS_RMS, ALU.mult, ALU.max))
                chain.link(V.reciprocal(nrm[:], nrm[:]))
                chain.link(V.tensor_tensor(qn[:].rearrange("p t (h d) -> p (t h) d", d=64),
                                           ps[:, 2:4, :].rearrange("p b (t d) -> p (b t) d", d=64),
                                           nrm[:].unsqueeze(2).broadcast_to([P, 16, 64]), ALU.mult))
                V.tensor_tensor(qn[:], qn[:], gain[:].unsqueeze(1).broadcast_to([P, PAIRS, D]), ALU.mult
                                ).then_inc(q_ready, 1)
                dve.wait_ge(q_turned, 1)
                dve.wait_ge(qbd_zeroed, 1)
                for h in range(2):
                    rows = slice(64 * h, 64 * h + 64)
                    chain.mark(V.tensor_copy(m.qbd1[rows, :, h, :],
                                             ps[rows, 4:6, :].rearrange("p c (b i) -> p (c b) i", i=S)))
                chain.settle()


def l1_cross_stage(nc, m, dram):
    ps = m.ps
    TILES = KT * P
    loaded = [m.sem("l1_ctx_loaded_even"), m.sem("l1_ctx_loaded_odd")]
    sums, means = m.sem("l1_row_sums"), m.sem("l1_means")
    centered, squared = m.sem("l1_centered"), m.sem("l1_centered_squared")
    sqsums, variances, rstd_ready = m.sem("l1_square_sums"), m.sem("l1_variances"), m.sem("l1_rstd_ready")
    xh_ready, mask_ready = m.sem("l1_context_normed"), m.sem("l1_mask_row_ready")
    xh_turned, xhT_ready = m.sem("l1_context_turned"), m.sem("l1_contextT_ready")
    staged = m.sem("l1_pair_staged")
    k_made, k_squared, kss_ready, knorm_ready = (m.sem(n) for n in (
        "l1_keys_made", "l1_keys_squared", "l1_key_squares_summed", "l1_key_norms"))
    rk_steps, kn_ready = m.sem("l1_key_scale_steps"), m.sem("l1_keys_normed")
    vlat_ready = m.sem("l1_latent_values_ready")
    kn_turned, knT_ready = m.sem("l1_keys_turned"), m.sem("l1_keysT_ready")
    scores_ready, mx_steps, exps_ready = m.sem("l1_scores_ready"), m.sem("l1_max_steps"), m.sem("l1_exps_ready")
    recip_ready = m.sem("l1_recip_ready")
    p_turned, pT_ready = m.sem("l1_probs_turned"), m.sem("l1_probsT_ready")
    pT_tail_ready = m.sem("l1_probsT_tail_ready")
    oT_made, oT_copied, o_made, o_copied = (m.sem("l1_" + n) for n in (
        "oT_made", "oT_copied", "o_made", "o_copied"))
    a_turned, aT_copied, y_made, x_updated = (m.sem("l1_" + n) for n in (
        "attn_turned", "attnT_copied", "y_made", "x_updated"))
    set_once = m.sem("l1_buffers_set")
    with ExitStack() as ctx:
        sb = m.scoped(ctx, "l1")
        mask_u8, mask_bf = sb("mask_u8", [1, 2, CTX], U8), sb("mask_bf", [1, KEYS], BF16)
        xh = sb("xh", [P, 2, KT, DC + 1])
        sq, stat = sb("sq", [P, KT, P]), sb("stat", [P, 4, KT])
        lat, qs = sb("lat", [P, P]), sb("qs", [P, 2, P])
        ksq, kss = sb("ksq", [P, KT + 1, P]), sb("kss", [P, KT + 1, 2])
        kn = sb("kn", [P, KT + 1, P])
        vlat = sb("vlat", [S, P])
        xhT, knT, probs = sb("xhT", [DC + 1, TILES]), sb("knT", [P, KEYS]), sb("probs", [P, KEYS])
        pT = sb("pT", [P, KT + 1, P])
        negm, total, recip = sb("negm", [P, 1]), sb("total", [P, 1]), sb("recip", [P, 1])
        mxp = sb("mxp", [P, 1])
        oT, attn, attnT = sb("oT", [DC + 1, P]), sb("attn", [P, P]), sb("attnT", [P, P])

        def half_tiles(h):
            return (0, 8) if h == 0 else (8, KT)

        with nc.Block() as block:
            @block.sync
            def _(sp):
                def load(b, j):
                    jj = bass.ds(j, 1)
                    sp.dma_start(m.ctx_nat[:, b, 0:FULL, 0:DC],
                                 dram["ctx"][jj, 0:FULL * P, :].rearrange("o (k p) d -> (o p) k d", p=P)
                                 ).then_inc(loaded[b], 16)
                    sp.dma_start(m.ctx_nat[0:REST, b, FULL, 0:DC],
                                 dram["ctx"][jj, FULL * P:CTX, :].rearrange("o p d -> (o p) d")
                                 ).then_inc(loaded[b], 16)
                    sp.dma_start(mask_u8[:, b, :], dram["mask"][jj]).then_inc(loaded[b], 16)
                load(0, 0)
                load(1, 1)
                with sp.Fori(0, PAIRS - 1) as t:
                    for b in range(2):
                        sp.wait_ge(mask_ready, 2 * t + b + 1)
                        load(b, 2 * t + 2 + b)

            def normalise_dve(dve, b, j, t_load):
                dve.wait_ge(loaded[b], 48 * t_load)
                nc.vector.tensor_reduce(stat[:, 0, :], m.ctx_nat[:, b, :, 0:DC], axis=AX.X, op=ALU.add
                                        ).then_inc(sums, 1)
                dve.wait_ge(sums, j + 1)
                nc.vector.tensor_scalar(stat[:, 1, :], stat[:, 0, :], 1.0 / DC, None, ALU.mult).then_inc(means, 1)

            def variance_dve(dve, b, j):
                dve.wait_ge(squared, j + 1)
                nc.vector.tensor_reduce(stat[:, 2, :], sq[:, :, 0:DC], axis=AX.X, op=ALU.add).then_inc(sqsums, 1)
                dve.wait_ge(sqsums, j + 1)
                nc.vector.tensor_scalar(stat[:, 2, :], stat[:, 2, :], 1.0 / DC, 1e-5, ALU.mult, ALU.add
                                        ).then_inc(variances, 1)

            @block.gpsimd
            def _(pool):
                nc.gpsimd.memset(xh[:, :, :, DC:DC + 1], 1.0).then_inc(set_once, 1)
                nc.gpsimd.memset(mask_bf[:], 0.0).then_inc(set_once, 1)
                nc.gpsimd.memset(kss[:], 1.0).then_inc(set_once, 1)
                pool.wait_ge(set_once, 3)

                def normalise(b, j):
                    pool.wait_ge(oT_made, 2 + j - 1)
                    pool.wait_ge(means, j + 1)
                    nc.gpsimd.tensor_tensor(xh[:, b, :, 0:DC], m.ctx_nat[:, b, :, 0:DC],
                                            stat[:, 1, :].unsqueeze(2).broadcast_to([P, KT, DC]), ALU.subtract
                                            ).then_inc(centered, 1)
                    pool.wait_ge(scores_ready, 1 + j)
                    pool.sem_inc(m.turns_pool, 1)
                    nc.gpsimd.tensor_scalar(mask_bf[:, 0:CTX], mask_u8[:, b, :], -NEG, NEG, ALU.mult, ALU.add
                                            ).then_inc(mask_ready, 1)
                    pool.wait_ge(variances, j + 1)
                    nc.gpsimd.tensor_tensor(stat[:, 3, :], stat[:, 2, :], m.nhalf[:, 0:KT], ALU.pow
                                            ).then_inc(rstd_ready, 1)
                    pool.wait_ge(rstd_ready, j + 1)
                    nc.gpsimd.tensor_tensor(xh[:, b, :, 0:DC], xh[:, b, :, 0:DC],
                                            stat[:, 3, :].unsqueeze(2).broadcast_to([P, KT, DC]), ALU.mult
                                            ).then_inc(xh_ready, 1)

                def key_norms(j):
                    for h in range(2):
                        lo, hi = half_tiles(h)
                        hi += h
                        pool.wait_ge(kss_ready, 3 * j + (1 if h == 0 else 3))
                        nc.gpsimd.tensor_tensor(kss[:, lo:hi, :], kss[:, lo:hi, :],
                                                m.half[:, 0:2 * (hi - lo)].rearrange("p (t h) -> p t h", h=2), ALU.pow
                                                ).then_inc(knorm_ready, 1)
                normalise(0, 0)
                with pool.Fori(0, PAIRS - 1) as t:
                    for b in range(2):
                        key_norms(2 * t + b)
                        normalise(1 - b, 2 * t + b + 1)
                key_norms(BATCHES - 2)
                normalise(1, BATCHES - 1)
                key_norms(BATCHES - 1)

            def turn_context(pe, b, j):
                pe.wait_ge(xh_ready, j + 1)
                pe.sem_inc(m.turns_pe, 1)
                for k in range(KT):
                    ins = nc.tensor.transpose(ps[0:DC + 1, k // 4, (k % 4) * P:(k % 4 + 1) * P], xh[:, b, k, :],
                                              m.ident[:])
                    if k % 4 == 3 or k == KT - 1:
                        ins.then_inc(xh_turned, 1)

            def keys(pe, b, j):
                pe.wait_ge(oT_copied, 1 + j)
                pe.wait_ge(o_copied, 2 + 2 * j)
                for k in range(KT):
                    if k % 4 == 0:
                        pe.wait_ge(xhT_ready, 4 * j + k // 4 + 1)
                    ins = nc.tensor.matmul(ps[:, 4 + k // 4, (k % 4) * P:(k % 4 + 1) * P], xhT[:, k * P:(k + 1) * P],
                                           m.WA[:, 0:P], start=True, stop=True)
                    if k == 7:
                        ins.then_inc(k_made, 1)
                nc.tensor.matmul(ps[0:S, 7, P:3 * P], lat[:, b * S:(b + 1) * S], m.wlkv1[:], start=True, stop=True
                                 ).then_inc(k_made, 1)

            def turn_keys(pe, b, j):
                pe.wait_ge(xhT_ready, 4 * j + 4)
                for k in range(KT):
                    if k in (0, 8):
                        pe.wait_ge(kn_ready, 3 * j + (1 if k == 0 else 3))
                        pe.sem_inc(m.turns_pe, 1)
                    r = rows_of(k)
                    ins = nc.tensor.transpose(ps[:, k // 4, (k % 4) * P:(k % 4) * P + r], kn[0:r, k, :],
                                              m.ident[0:r, 0:r])
                    if k % 4 == 3:
                        ins.then_inc(kn_turned, 1)
                nc.tensor.transpose(ps[:, 3, REST:REST + LAT], kn[0:LAT, KT, :], m.ident[0:LAT, 0:LAT]
                                    ).then_inc(kn_turned, 1)

            def scores(pe, b, j):
                pe.wait_ge(vlat_ready, j + 1)
                pe.wait_ge(mask_ready, j + 1)
                for c in range(4):
                    n = min(BANK, KEYS - c * BANK)
                    pe.wait_ge(knT_ready, 4 * j + c + 1)
                    nc.tensor.matmul(ps[:, 4 + c, 0:n], m.ones_bf[:], mask_bf[:, c * BANK:c * BANK + n],
                                     start=True, stop=False)
                    ins = nc.tensor.matmul(ps[:, 4 + c, 0:n], qs[:, b, :], knT[:, c * BANK:c * BANK + n],
                                           start=False, stop=True)
                ins.then_inc(scores_ready, 1)

            def turn_probs(pe, b, j):
                pe.wait_ge(exps_ready, j + 1)
                pe.sem_inc(m.turns_pe, 1)
                for k in range(KT):
                    r = rows_of(k)
                    ins = nc.tensor.transpose(ps[0:r, k // 4, (k % 4) * P:(k % 4 + 1) * P], probs[:, k * P:k * P + r],
                                              m.ident[:])
                    if k % 4 == 3:
                        ins.then_inc(p_turned, 1)
                nc.tensor.transpose(ps[0:LAT, 3, P:2 * P], probs[:, CTX:KEYS], m.ident[:]).then_inc(p_turned, 1)

            def output(pe, b, j):
                for k in range(KT):
                    if k % 4 == 0:
                        if k < FULL:
                            pe.wait_ge(pT_ready, 3 * j + k // 4 + 1)
                        else:
                            pe.wait_ge(pT_tail_ready, 2 * j + 2)
                    r = rows_of(k)
                    ins = nc.tensor.matmul(ps[0:DC + 1, 4, 0:P], xh[0:r, b, k, :], pT[0:r, k, :], start=(k == 0),
                                           stop=(k == KT - 1))
                ins.then_inc(oT_made, 1)
                nc.tensor.matmul(ps[:, 5, 0:P], pT[0:LAT, KT, :], vlat[:], start=True, stop=False)
                pe.wait_ge(oT_copied, j + 2)
                nc.tensor.matmul(ps[:, 5, 0:P], oT[:], m.WA[:, P:2 * P], start=False, stop=True).then_inc(o_made, 1)

            def pe_pair(pe, t, last):
                pe.wait_ge(staged, 3 * t + 3)
                for b in range(2):
                    j = 2 * t + b
                    keys(pe, b, j)
                    turn_keys(pe, b, j)
                    scores(pe, b, j)
                    if not (last and b == 1):
                        turn_context_after(pe, 1 - b, j + 1)
                    turn_probs_after(pe, b, j, last and b == 1)
                    output(pe, b, j)
                pe.wait_ge(o_copied, 2 + 2 * (2 * t + 2))
                pe.sem_inc(m.turns_pe, 1)
                nc.tensor.transpose(ps[:, 6, 0:P], attn[:], m.ident[:]).then_inc(a_turned, 1)
                pe.wait_ge(aT_copied, t + 1)
                nc.tensor.matmul(ps[:, 7, 0:D], attnT[:], m.wo1[:], start=True, stop=False)
                nc.tensor.matmul(ps[:, 7, 0:D], m.ones[0:1, 0:P], m.bo1[:], start=False, stop=True
                                 ).then_inc(y_made, 1)

            def turn_context_after(pe, b, j):
                pe.wait_ge(knT_ready, 4 * j)
                turn_context(pe, b, j)

            def turn_probs_after(pe, b, j, last):
                if not last:
                    pe.wait_ge(xhT_ready, 4 * (j + 2))
                turn_probs(pe, b, j)

            @block.tensor
            def _(pe):
                pe.sem_inc(oT_made, 2)
                pe.sem_inc(scores_ready, 1)
                pe.wait_ge(set_once, 3)
                turn_context(pe, 0, 0)
                with pe.Fori(0, PAIRS - 1) as t:
                    pe_pair(pe, t, False)
                pe_pair(pe, PAIRS - 1, True)

            def copy_context(act, j):
                for c in range(4):
                    n = min(BANK, TILES - c * BANK)
                    act.wait_ge(xh_turned, 4 * j + c + 1)
                    if c == 0:
                        act.wait_ge(k_made, 2 * j)
                    nc.scalar.copy(xhT[:, c * BANK:c * BANK + n], ps[0:DC + 1, c, 0:n]).then_inc(xhT_ready, 1)

            def square_context(act, b, j):
                act.wait_ge(centered, j + 1)
                nc.scalar.activation(sq[:, :, 0:DC], xh[:, b, :, 0:DC], ACT.Square).then_inc(squared, 1)

            def act_pair(act, t, last):
                for b in range(2):
                    j = 2 * t + b
                    lastb = last and b == 1
                    for h in range(2):
                        lo, hi = half_tiles(h)
                        act.wait_ge(k_made, 2 * j + h + 1)
                        nc.scalar.activation(ksq[:, lo:hi, :],
                                             ps[:, 4:8, :].rearrange("p c (k d) -> p (c k) d", d=P)[:, lo:hi, :],
                                             ACT.Square).then_inc(k_squared, 1)
                    nc.scalar.activation(ksq[0:S, KT, :], ps[0:S, 7, P:2 * P], ACT.Square).then_inc(k_squared, 1)
                    nc.scalar.copy(vlat[:], ps[0:S, 7, 2 * P:3 * P]).then_inc(vlat_ready, 1)
                    for c in range(4):
                        n = min(BANK, KEYS - c * BANK)
                        act.wait_ge(kn_turned, 4 * j + c + 1)
                        nc.scalar.copy(knT[:, c * BANK:c * BANK + n], ps[:, c, 0:n]).then_inc(knT_ready, 1)
                    if not lastb:
                        square_context(act, 1 - b, j + 1)
                        copy_context_late(act, j + 1)
                    act.wait_ge(mx_steps, 2 * j + 2)
                    nc.scalar.activation(probs[:], ps[:, 4:8, :].rearrange("p c n -> p (c n)")[:, 0:KEYS], ACT.Exp,
                                         bias=negm[:], accum_out=total[:]).then_inc(exps_ready, 1)
                    act.wait_ge(oT_made, 2 + j + 1)
                    nc.scalar.copy(oT[:], ps[0:DC + 1, 4, 0:P]).then_inc(oT_copied, 1)
                act.wait_ge(a_turned, t + 1)
                nc.scalar.copy(attnT[:], ps[:, 6, 0:P]).then_inc(aT_copied, 1)

            def copy_context_late(act, j):
                copy_context(act, j)

            @block.scalar
            def _(act):
                act.sem_inc(oT_copied, 1)
                square_context(act, 0, 0)
                for c in range(4):
                    n = min(BANK, TILES - c * BANK)
                    act.wait_ge(xh_turned, c + 1)
                    nc.scalar.copy(xhT[:, c * BANK:c * BANK + n], ps[0:DC + 1, c, 0:n]).then_inc(xhT_ready, 1)
                with act.Fori(0, PAIRS - 1) as t:
                    act_pair(act, t, False)
                act_pair(act, PAIRS - 1, True)

            def dve_pair(dve, t, last):
                V = nc.vector
                V.tensor_copy(lat[:], m.xT[:, bass.ds(t * P, P)]).then_inc(staged, 1)
                for b in range(2):
                    V.tensor_copy(qs[:, b, :], m.qbd1[:, bass.ds(2 * t + b, 1), :, :].rearrange(
                        "p o h i -> p (o h i)")).then_inc(staged, 1)
                for b in range(2):
                    j = 2 * t + b
                    for h in range(2):
                        lo, hi = half_tiles(h)
                        dve.wait_ge(k_squared, 3 * j + h + 1)
                        V.tensor_reduce(kss[:, lo:hi, :].rearrange("p k h -> p (k h)"),
                                        ksq[:, lo:hi, :].rearrange("p k (h d) -> p (k h) d", d=64), axis=AX.X,
                                        op=ALU.add).then_inc(kss_ready, 1)
                    dve.wait_ge(k_squared, 3 * j + 3)
                    V.tensor_reduce(kss[0:S, KT, :], ksq[0:S, KT, :].rearrange("p (h d) -> p h d", d=64), axis=AX.X,
                                    op=ALU.add).then_inc(kss_ready, 1)
                    for h in range(2):
                        lo, hi = half_tiles(h)
                        dve.wait_ge(knorm_ready, 2 * j + h + 1)
                        V.tensor_scalar(kss[:, lo:hi + h, :], kss[:, lo:hi + h, :], float(64) ** -0.5, EPS_RMS,
                                        ALU.mult, ALU.max).then_inc(rk_steps, 1)
                        dve.wait_ge(rk_steps, 4 * j + 2 * h + 1)
                        V.reciprocal(kss[:, lo:hi + h, :], kss[:, lo:hi + h, :]).then_inc(rk_steps, 1)
                        dve.wait_ge(rk_steps, 4 * j + 2 * h + 2)
                        if h == 1:
                            dve.wait_ge(vlat_ready, j + 1)
                        V.tensor_tensor(
                            kn[:, lo:hi, :].rearrange("p k (h d) -> p (k h) d", d=64),
                            ps[:, 4:8, :].rearrange("p c (k d) -> p (c k) d", d=64)[:, 2 * lo:2 * hi, :],
                            kss[:, lo:hi, :].rearrange("p k h -> p (k h)").unsqueeze(2).broadcast_to(
                                [P, 2 * (hi - lo), 64]), ALU.mult).then_inc(kn_ready, 1)
                    V.tensor_tensor(kn[0:S, KT, :].rearrange("p (h d) -> p h d", d=64),
                                    ps[0:S, 7, P:2 * P].rearrange("p (h d) -> p h d", d=64),
                                    kss[0:S, KT, :].unsqueeze(2).broadcast_to([S, 2, 64]), ALU.mult
                                    ).then_inc(kn_ready, 1)
                    if not (last and b == 1):
                        normalise_dve(dve, 1 - b, j + 1, t + 1 + b)
                        variance_dve(dve, 1 - b, j + 1)
                    dve.wait_ge(scores_ready, 1 + j + 1)
                    V.tensor_reduce(mxp[:], ps[:, 4:8, :].rearrange("p c n -> p (c n)")[:, 0:KEYS], axis=AX.X,
                                    op=ALU.max).then_inc(mx_steps, 1)
                    dve.wait_ge(mx_steps, 2 * j + 1)
                    V.tensor_scalar(negm[:], mxp[:], -1.0, None, ALU.mult).then_inc(mx_steps, 1)
                    dve.wait_ge(exps_ready, j + 1)
                    V.reciprocal(recip[:], total[:]).then_inc(recip_ready, 1)
                    for c in range(3):
                        dve.wait_ge(p_turned, 4 * j + c + 1)
                        V.tensor_copy(pT[:, 4 * c:4 * c + 4, :], ps[:, c, :].rearrange("p (k q) -> p k q", q=P)
                                      ).then_inc(pT_ready, 1)
                    dve.wait_ge(p_turned, 4 * j + 4)
                    V.tensor_copy(pT[0:REST, FULL, :], ps[0:REST, 3, 0:P]).then_inc(pT_tail_ready, 1)
                    V.tensor_copy(pT[0:LAT, KT, :], ps[0:LAT, 3, P:2 * P]).then_inc(pT_tail_ready, 1)
                    dve.wait_ge(o_made, j + 1)
                    for h in range(2):
                        rows = slice(64 * h, 64 * h + 64)
                        V.tensor_scalar(attn[S * b:S * b + S, 64 * h:64 * h + 64], ps[rows, 5, 64 * h:64 * h + 64],
                                        recip[rows, :], None, ALU.mult).then_inc(o_copied, 1)
                dve.wait_ge(y_made, t + 1)
                xt = m.X[:, bass.ds(t, 1), :].rearrange("p o d -> p (o d)")
                V.tensor_tensor(xt, xt, ps[:, 7, 0:D], ALU.add).then_inc(x_updated, 1)

            @block.vector
            def _(dve):
                dve.sem_inc(o_copied, 2)
                dve.wait_ge(set_once, 3)
                normalise_dve(dve, 0, 0, 1)
                variance_dve(dve, 0, 0)
                with dve.Fori(0, PAIRS - 1) as t:
                    dve_pair(dve, t, False)
                dve_pair(dve, PAIRS - 1, True)


def router_stage(nc, m, name, E, top, wr, br, b2, soft, extra):
    ps = m.ps
    made, exps_ready, own, less_ready, gates_ready, turned, gT_ready, b_made = (m.tally("router_" + n) for n in (
        "logits_made", "exps_ready", "dve_steps", "less_ready", "gates_ready", "gates_turned", "gT_ready",
        "bias_made"))
    with ExitStack() as ctx:
        sb = m.scoped(ctx, name)
        a, w_, sel, eq = (sb(n, [P, PAIRS, E]) for n in ("a", "work", "sel", "eq"))
        one = sb("one", [P, PAIRS])
        tot = sb("tot", [P, PAIRS])
        gT = sb("gT", [E + 1, ROWS])
        def over(t):
            return t[:].unsqueeze(2).broadcast_to([P, PAIRS, E])
        with nc.Block() as block:
            @block.tensor
            def _(pe):
                for t in range(PAIRS):
                    out = ps[:, 0, 32 * t:32 * t + E]
                    ins = nc.tensor.matmul(out, m.xT[:, t * P:(t + 1) * P], wr[:], start=True, stop=br is None)
                    if br is not None:
                        ins = nc.tensor.matmul(out, m.ones[0:1, 0:P], br[:], start=False, stop=True)
                ins.then_inc(made.sem, 1)
                gates_ready.wait(pe, 1)
                for t in range(PAIRS):
                    ins = nc.tensor.transpose(ps[0:E + 1, 2 + t // 4, (t % 4) * P:(t % 4 + 1) * P],
                                              m.gates[:, t, 0:E + 1], m.ident[:])
                ins.then_inc(turned.sem, 1)
                gT_ready.wait(pe, 1)
                for t in range(PAIRS):
                    ins = nc.tensor.matmul(ps[:, 4 + t // 4, (t % 4) * P:(t % 4 + 1) * P], gT[:, t * P:(t + 1) * P],
                                           b2[:], start=True, stop=True)
                ins.then_inc(b_made.sem, 1)

            @block.scalar
            def _(act):
                less_ready.wait(act, 1)
                nc.scalar.activation(a[:], w_[:], ACT.Exp, scale=1.0 if soft else -1.0).then_inc(exps_ready.sem, 1)
                turned.wait(act, 1)
                nc.scalar.copy(gT[:], ps[0:E + 1, 2:4, :].rearrange("p b n -> p (b n)")).then_inc(gT_ready.sem, 1)
                gT_ready.wait(act, 1)

            @block.vector
            def _(dve):
                chain = Chain(dve, own.sem, own.base)
                logits = ps[:, 0, 0:32 * PAIRS].rearrange("p (t e) -> p t e", e=32)[:, :, 0:E]
                V = nc.vector
                made.wait(dve, 1)
                if soft:
                    chain.link(V.tensor_reduce(one[:], logits, axis=AX.X, op=ALU.max))
                    V.tensor_tensor(w_[:], logits, over(one), ALU.subtract).then_inc(less_ready.sem, 1)
                    exps_ready.wait(dve, 1)
                    chain.link(V.tensor_reduce(one[:], a[:], axis=AX.X, op=ALU.add))
                    chain.link(V.reciprocal(tot[:], one[:]))
                    chain.link(V.tensor_tensor(a[:], a[:], over(tot), ALU.mult))
                else:
                    V.tensor_copy(w_[:], logits).then_inc(less_ready.sem, 1)
                    exps_ready.wait(dve, 1)
                    chain.link(V.tensor_scalar(a[:], a[:], 1.0, None, ALU.add))
                    chain.link(V.reciprocal(a[:], a[:]))
                chain.link(V.tensor_copy(w_[:], a[:]))
                chain.link(V.memset(m.gates[:, :, 0:E], 0.0))
                chain.link(V.memset(m.gates[:, :, E:E + 1], 1.0))
                gates = m.gates[:, :, 0:E]
                for i in range(top):
                    chain.link(V.tensor_reduce(one[:], w_[:], axis=AX.X, op=ALU.max))
                    chain.link(V.tensor_tensor(eq[:], w_[:], over(one), ALU.is_equal))
                    chain.link(V.tensor_tensor(eq[:], eq[:], m.down[:, 32 - E:32].unsqueeze(1).broadcast_to(
                        [P, PAIRS, E]), ALU.mult))
                    chain.link(V.tensor_reduce(one[:], eq[:], axis=AX.X, op=ALU.max))
                    chain.link(V.tensor_tensor(sel[:], eq[:], over(one), ALU.is_equal))
                    chain.link(V.scalar_tensor_tensor(out=w_[:], in0=sel[:], scalar=-4.0, in1=w_[:], op0=ALU.mult,
                                                      op1=ALU.add))
                    chain.link(V.tensor_tensor(sel[:], sel[:], a[:], ALU.mult))
                    chain.link(V.tensor_tensor(gates, gates, sel[:], ALU.add))
                if not soft:
                    chain.link(V.tensor_reduce(one[:], gates, axis=AX.X, op=ALU.add))
                    chain.link(V.tensor_scalar(one[:], one[:], 1e-6, None, ALU.add))
                    chain.link(V.reciprocal(tot[:], one[:]))
                    chain.link(V.tensor_tensor(gates, gates, over(tot), ALU.mult))
                V.tensor_copy(one[:, 0:1], m.gates[:, 0, 0:1]).then_inc(gates_ready.sem, 1)
                for e in extra:
                    chain.link(V.tensor_tensor(m.X[:], m.X[:], e[:], ALU.add))
                b_made.wait(dve, 1)
                chain.link(V.tensor_tensor(m.X[:], m.X[:], ps[:, 4:6, :].rearrange("p b (t d) -> p (b t) d", d=D),
                                           ALU.add))
                own.close(chain.n)
    for tally in (made, exps_ready, less_ready, gates_ready, turned, gT_ready, b_made):
        tally.close(1)


def experts_stage(nc, m, name, n_experts, chunks, func, unroll, w1, w2, b1):
    ps = m.ps
    loaded = [m.sem(f"{name}_weights_loaded_{i}") for i in range(unroll)]
    up_made, h_ready = m.sem(name + "_up_made"), m.sem(name + "_hidden_ready")
    down_made, gated = m.sem(name + "_down_made"), m.sem(name + "_gated")
    gate_staged = m.sem(name + "_gate_staged")
    turns = n_experts // unroll
    assert turns * unroll == n_experts
    even = unroll % 2 == 0
    with ExitStack() as ctx:
        sb = m.scoped(ctx, name)
        W1, W2 = sb("w1", [P, unroll, chunks * P]), sb("w2", [P, unroll, chunks, D])
        B1 = sb("b1", [P, unroll, chunks])
        hid = sb("hid", [P, 2, chunks, ROWS])
        gate = sb("gate", [P, 2, PAIRS])
        with nc.Block() as block:
            @block.sync
            def _(sp):
                def load(i, e):
                    ee = bass.ds(e, 1)
                    sp.dma_start(W1[:, i, :], w1[ee].rearrange("o p h -> (o p) h")).then_inc(loaded[i], 16)
                    sp.dma_start(W2[:, i], w2[ee].rearrange("o (c p) d -> p (o c) d", p=P)).then_inc(loaded[i], 16)
                    sp.dma_start(B1[:, i, :], b1[ee].rearrange("o p c -> (o p) c")).then_inc(loaded[i], 16)
                for i in range(unroll):
                    load(i, i)
                with sp.Fori(1, turns) as t:
                    for i in range(unroll):
                        sp.wait_ge(down_made, 2 + (t - 1) * unroll + i + 1)
                        load(i, t * unroll + i)

            @block.tensor
            def _(pe):
                pe.sem_inc(down_made, 2)

                def up(i, e, t):
                    pe.wait_ge(loaded[i], 48 * (t + 1))
                    for c in range(chunks):
                        pe.wait_ge(h_ready, 2 + chunks * e + c - 1)
                        for half in range(2):
                            ins = nc.tensor.matmul(ps[:, 2 * (((i * chunks) + c) % 2) + half, :],
                                                   W1[:, i, c * P:(c + 1) * P],
                                                   m.xT[:, half * BANK:(half + 1) * BANK], start=True, stop=True)
                        ins.then_inc(up_made, 1)

                def down(i, e):
                    pe.wait_ge(gated, 2 + PAIRS + PAIRS * ((e - 1) if (even or i) else e))
                    for tile in range(PAIRS):
                        for c in range(chunks):
                            if tile == 0:
                                pe.wait_ge(h_ready, 2 + chunks * e + c + 1)
                            ins = nc.tensor.matmul(ps[:, 4 + 2 * (i % 2) + tile // 4, (tile % 4) * P:(tile % 4 + 1) * P],
                                                   hid[:, i % 2, c, tile * P:(tile + 1) * P], W2[:, i, c, :],
                                                   start=(c == 0), stop=(c == chunks - 1))
                    ins.then_inc(down_made, 1)

                with pe.Fori(0, turns) as t:
                    up(0, t * unroll, t)
                    for i in range(1, unroll):
                        up(i, t * unroll + i, t)
                        down(i - 1, t * unroll + i - 1)
                    down(unroll - 1, t * unroll + unroll - 1)

            @block.scalar
            def _(act):
                act.sem_inc(h_ready, 2)
                with act.Fori(0, turns) as t:
                    for i in range(unroll):
                        e = t * unroll + i
                        for c in range(chunks):
                            act.wait_ge(up_made, chunks * e + c + 1)
                            act.wait_ge(down_made, 2 + ((e - 1) if (even or i) else e))
                            nc.scalar.activation(hid[:, i % 2, c, :],
                                                 ps[:, 2 * (((i * chunks) + c) % 2):2 * (((i * chunks) + c) % 2) + 2, :]
                                                 .rearrange("p b n -> p (b n)"), func, bias=B1[:, i, c:c + 1]
                                                 ).then_inc(h_ready, 1)

            @block.vector
            def _(dve):
                dve.sem_inc(gated, 2 + PAIRS)
                with dve.Fori(0, turns) as t:
                    for i in range(unroll):
                        e = t * unroll + i
                        dve.wait_ge(gated, 2 + PAIRS + PAIRS * e)
                        nc.vector.tensor_copy(gate[:, i % 2, :], m.gates[:, :, bass.ds(e, 1)].rearrange(
                            "p t o -> p (t o)")).then_inc(gate_staged, 1)
                        dve.wait_ge(gate_staged, e + 1)
                        dve.wait_ge(down_made, 2 + e + 1)
                        for tile in range(PAIRS):
                            nc.vector.scalar_tensor_tensor(
                                out=m.X[:, tile, :],
                                in0=ps[:, 4 + 2 * (i % 2) + tile // 4, (tile % 4) * P:(tile % 4 + 1) * P],
                                scalar=gate[:, i % 2, tile:tile + 1], in1=m.X[:, tile, :], op0=ALU.mult, op1=ALU.add
                                ).then_inc(gated, 1)
                dve.wait_ge(gated, 2 + PAIRS + PAIRS * n_experts)


def store_stage(nc, m, src, out):
    stored = m.sem("output_stored")
    with nc.Block() as block:
        @block.sync
        def _(sp):
            sp.dma_start(out.rearrange("(t b) s d -> (b s) t d", b=2), src[:]).then_inc(stored, 16)
            sp.wait_ge(stored, 16)


def build(nc, dram, out):
    with ExitStack() as ctx:
        def sb(name, shape, dt=F32):
            return ctx.enter_context(nc.sbuf_tensor(name, shape, dt))

        m = Core()
        m.H0 = 8
        m.sem = lambda name: ctx.enter_context(nc.semaphore(name))
        tallies = {}

        def tally(name):
            if name not in tallies:
                tallies[name] = Tally(m.sem(name))
            return tallies[name]
        m.tally = tally
        m.scoped = lambda c, tag: (lambda name, shape, dt=F32:
                                   c.enter_context(nc.sbuf_tensor(tag + "_" + name, shape, dt)))
        m.ps = ctx.enter_context(nc.psum_tensor("ps", [P, 8, BANK], F32))
        m.X = sb("X", [P, PAIRS, D])
        m.xT = sb("xT", [P, ROWS])
        m.Y = sb("Y", [P, PAIRS, D])
        m.nhalf, m.half = sb("nhalf", [P, 32]), sb("half", [P, 32])
        m.ones, m.ones_bf = sb("ones", [1, BANK]), sb("ones_bf", [1, P], BF16)
        m.ident_bf = sb("ident_bf", [P, P], BF16)
        m.causal_bf, m.strided_bf = sb("causal_bf", [P, BANK], BF16), sb("strided_bf", [P, BANK], BF16)
        m.ctx_nat = sb("ctx_nat", [P, 2, KT, DC + 1])
        m.turns_pool = m.sem("turns_pool")
        m.turns_act, m.turns_pe, m.turns_dve = m.sem("turns_act"), m.sem("turns_pe"), m.sem("turns_dve")
        m.loads = []

        def resident(attr, shape, source):
            t = sb(attr, shape)
            m.loads.append((t[:], source))
            return t

        m.ident = resident("ident", [P, P], dram["ident"])
        m.causal = resident("causal", [P, BANK], dram["causal"])
        m.strided = resident("strided", [P, BANK], dram["strided"])
        m.wqT0 = resident("wqT0", [S, 8, D], dram["wqT0"].rearrange("(h e) d -> e h d", h=8))
        m.wkT0 = resident("wkT0", [S, 8, DC], dram["wkT0"].rearrange("(h e) d -> e h d", h=8))
        m.wvT0 = resident("wvT0", [S, 8, DC], dram["wvT0"].rearrange("(h e) d -> e h d", h=8))
        m.wo0 = resident("wo0", [S, 8, D], dram["L0_xattn_Wo"].rearrange("(h e) d -> e h d", h=8))
        m.bo0 = resident("bo0", [1, D], dram["L0_xattn_bo"].rearrange("(o d) -> o d", o=1))
        m.qmask = resident("qmask", [P, 2], dram["qmask"])
        m.kmask = resident("kmask", [P, HP], dram["kmask"])
        m.cosb = resident("cosb", [P, S], dram["cosb"])
        m.sinb = resident("sinb", [P, S], dram["sinb"])
        m.pos = resident("pos", [P, P], dram["pos"])
        m.down = resident("down", [P, 32], dram["down"])
        m.rope_sign = resident("rope_sign", [P, 1], dram["rope_sign"])
        m.small0 = []
        for n in ("wqB", "wqBs", "wkB", "wkBs", "wvB", "woB"):
            m.small0.append(resident(n, [P, P], dram[n]))
        m.wqk = []
        for n in ("wqC", "wqCs", "wkC", "wkCs"):
            m.wqk.append(resident(n, [P, HP * P], dram[n]))
        m.bqk = resident("bqk", [P, 4, HP], dram["bqkC"])
        m.wv_c = resident("wv_c", [P, HP * P], dram["L0_ffn_v_w"])
        m.bv_c = resident("bv_c", [1, HP * P], dram["L0_ffn_v_b"].rearrange("(o d) -> o d", o=1))
        m.wo_c = resident("wo_c", [P, HP, D], dram["L0_ffn_o_w"].rearrange("(h p) d -> p h d", p=P))
        m.bo_c = resident("bo_c", [1, D], dram["L0_ffn_o_b"].rearrange("(o d) -> o d", o=1))
        m.theta = sb("theta", [P, 1])
        for q in range(4):
            m.loads.append((m.theta[32 * q:32 * q + 32, :], dram["L0_ffn_theta"].rearrange("(p o) -> p o", o=1)))
        m.gain1 = resident("gain1", [P, D], dram["L0_ffn_gamma1"].partition_broadcast(P))
        m.gain2 = resident("gain2", [P, D], dram["L0_ffn_gamma2"].partition_broadcast(P))
        m.wr0 = resident("wr0", [P, 31], dram["L0_ffn_router_w"])
        m.br0 = resident("br0", [1, 31], dram["L0_ffn_router_b"].rearrange("(o d) -> o d", o=1))
        m.b2_0 = resident("b2_0", [32, D], dram["b2_0"])
        def column(source):
            return source.rearrange("(p o) -> p o", o=1)

        def row(source):
            return source.rearrange("(o d) -> o d", o=1)
        m.ln_l_g = resident("ln_l_g", [P, D], dram["L1_xattn_ln_l_g"].partition_broadcast(P))
        m.ln_l_b = resident("ln_l_b", [P, D], dram["L1_xattn_ln_l_b"].partition_broadcast(P))
        m.ln_x_g = resident("ln_x_g", [DC, 1], column(dram["L1_xattn_ln_x_g"]))
        m.ln_x_b = resident("ln_x_b", [DC, 1], column(dram["L1_xattn_ln_x_b"]))
        m.qn_g, m.kn_g = sb("qn_g", [P, D]), sb("kn_g", [P, D])
        for h in range(2):
            for t, n in ((m.qn_g, "L1_xattn_qn_g"), (m.kn_g, "L1_xattn_kn_g")):
                m.loads.append((t[:, 64 * h:64 * h + 64], dram[n].partition_broadcast(P)))
        m.wq1 = resident("wq1", [P, P], dram["wq1"])
        m.wkv1 = resident("wkv1", [DC, 2 * P], dram["wkv1"])
        m.wlkv1 = resident("wlkv1", [P, 2 * P], dram["wlkv1"])
        m.wo1 = resident("wo1", [P, P], dram["wo1"])
        m.bo1 = resident("bo1", [1, P], row(dram["L1_xattn_bo"]))
        m.wq_e, m.wk_e, m.wv_e = (resident(f"w{n}_e", [P, P], dram[f"L1_attn_W{n}"]) for n in "qkv")
        m.wo_e = resident("wo_e", [P, P], dram["L1_attn_Wp"])
        m.bq_e = resident("bq_e", [P, 1], column(dram["L1_attn_bq"]))
        m.bk_e = resident("bk_e", [P, 1], column(dram["L1_attn_bk"]))
        m.bv_e = resident("bv_e", [S, D], dram["L1_attn_bv"].partition_broadcast(S))
        m.bo_e = resident("bo_e", [1, D], row(dram["L1_attn_bp"]))
        m.gain6 = resident("gain6", [P, D], dram["L1_ffn_norm_weight"].partition_broadcast(P))
        m.wr1 = resident("wr1", [P, 8], dram["wr1"])
        m.b2_1 = resident("b2_1", [9, D], dram["b2_1"])
        m.gates = sb("gates", [P, PAIRS, 32])
        m.cosc, m.sinc = sb("cosc", [P, P]), sb("sinc", [P, P])
        load_stage(nc, m, dram)
        ln = [("ln", 1e-5, None, None)]

        def scope():
            c = ExitStack()
            return c, lambda name, shape, dt=F32: c.enter_context(nc.sbuf_tensor(name, shape, dt))
        c0, s0 = scope()
        with c0:
            m.mq0, m.nv0 = s0("mq0", [P, 8, P]), s0("nv0", [DC, 8, D])
            m.U, m.Ub = s0("U", [DC + 1, BATCHES, 8, S]), s0("Ub", [DC, BATCHES, 8, S], BF16)
            norm_stage(nc, m, "n0", m.X, m.Y, m.xT, ln)
            l0_fold_stage(nc, m)
            l0_cross_stage(nc, m, dram)
        c0, s0 = scope()
        with c0:
            m.qT, m.kT, m.V = s0("qT", [P, ROWS]), s0("kT", [P, ROWS]), s0("V", [S, BATCHES, D])
            norm_stage(nc, m, "n1", m.X, m.Y, m.xT, ln)
            project_small_heads_stage(nc, m, "p1", m.small0[:5], True, None)
            small_heads_stage(nc, m, "a1", m.causal_bf, m.small0[5], None)
        c0, s0 = scope()
        with c0:
            m.AO = s0("AO", [P, PAIRS, D])
            norm_stage(nc, m, "n2", m.X, m.Y, m.xT, ln + [("rms", 1e-5, m.gain1, None)])
            angles_stage(nc, m)
            wide_heads_stage(nc, m)
            norm_stage(nc, m, "n3", m.AO, m.Y, m.xT, [("rms", 1e-5, m.gain2, None)])
            router_stage(nc, m, "r0", 31, 3, m.wr0, m.br0, m.b2_0, True, [m.AO, m.Y])
            experts_stage(nc, m, "e0", 32, 1, ACT.Gelu, 4, dram["w1_0"], dram["w2_0"], dram["b1_0"])
        c0, s0 = scope()
        with c0:
            m.qbd1, m.WA = s0("qbd1", [P, BATCHES, 2, S]), s0("WA", [DC + 1, 2 * P])
            norm_stage(nc, m, "n4", m.X, m.Y, m.xT, ln + [("ln", 1e-5, m.ln_l_g, m.ln_l_b)])
            l1_prepare_stage(nc, m)
            l1_cross_stage(nc, m, dram)
        c0, s0 = scope()
        with c0:
            m.qT, m.kT, m.V = s0("qT1", [P, ROWS]), s0("kT1", [P, ROWS]), s0("V1", [S, BATCHES, D])
            norm_stage(nc, m, "n5", m.X, m.Y, m.xT, ln)
            project_small_heads_stage(nc, m, "p5", [m.wq_e, m.wk_e, m.wv_e], False, [m.bq_e, m.bk_e, m.bv_e])
            small_heads_stage(nc, m, "a5", m.strided_bf, m.wo_e, m.bo_e)
        norm_stage(nc, m, "n6", m.X, m.Y, m.xT, ln + [("rms", 1e-8, m.gain6, None)])
        router_stage(nc, m, "r1", 8, 2, m.wr1, None, m.b2_1, False, [])
        experts_stage(nc, m, "e1", 9, 4, ACT.Relu, 3, dram["w1_1"], dram["w2_1"], dram["b1_1"])
        store_stage(nc, m, m.X, out)


def kernel(**inputs):
    import numpy as np
    import concourse.bacc as bacc
    from concourse.bass_utils import run_bass_kernel_spmd

    arrays = {n: np.ascontiguousarray(a) for n, a in inputs.items()}
    arrays["ctx"] = arrays.pop("ctx_768")
    arrays["ctxT"] = np.ascontiguousarray(arrays["ctx"].transpose(0, 2, 1))
    for new, old in (("wqT0", "L0_xattn_Wq"), ("wkT0", "L0_xattn_Wk"), ("wvT0", "L0_xattn_Wv")):
        arrays[new] = np.ascontiguousarray(arrays[old].T)
    i, key = np.arange(128)[:, None] % 64, np.arange(512)[None, :] % 64
    arrays["ident"] = np.eye(128, dtype=np.float32)
    arrays["causal"] = np.where(key <= i, 0.0, NEG).astype(np.float32)
    arrays["strided"] = np.where((key <= i) & (key % 4 != 3), 0.0, NEG).astype(np.float32)

    h, feature = np.arange(128) // 8, np.arange(128) % 8
    arrays["qmask"] = (h[:, None] % 2 == np.arange(2)).astype(np.float32)
    arrays["kmask"] = (h[:, None] // 2 == np.arange(8)).astype(np.float32)
    inv = (1.0 / 10000.0 ** (np.arange(0, 8, 2, dtype=np.float32) / 8)).astype(np.float32)
    angle = (np.arange(64, dtype=np.float32)[None, :] * inv[feature % 4][:, None]).astype(np.float32)
    arrays["cosb"] = np.cos(angle)
    arrays["sinb"] = np.sin(angle) * np.where(feature < 4, -1, 1).astype(np.float32)[:, None]
    arrays["pos"] = np.tile(np.arange(64, dtype=np.float32), (128, 2))
    arrays["rope_sign"] = np.where(np.arange(128) % 64 < 32, -1, 1).astype(np.float32)[:, None]
    arrays["down"] = np.tile(np.arange(32, 0, -1).astype(np.float32), (128, 1))
    swap8 = (np.arange(16)[:, None] * 8 + (np.arange(8) + 4) % 8).reshape(-1)
    for new, old in (("wqB", "L0_attn_W_q"), ("wkB", "L0_attn_W_k"), ("wvB", "L0_attn_W_v"), ("woB", "L0_attn_W_o")):
        arrays[new] = np.ascontiguousarray(arrays[old].T)
    for n in ("wqB", "wkB"):
        arrays[n + "s"] = np.ascontiguousarray(arrays[n][:, swap8])
    halves = np.concatenate([np.arange(0, 64, 2), np.arange(1, 64, 2)])
    split = (np.arange(16)[:, None] * 64 + halves).reshape(-1)
    swapped = (np.arange(16)[:, None] * 64 + np.roll(halves, 32)).reshape(-1)
    biases = []
    for q in "qk":
        w, bias = arrays[f"L0_ffn_{q}_w"], arrays[f"L0_ffn_{q}_b"]
        for tag, order in (("", split), ("s", swapped)):
            arrays[f"w{q}C{tag}"] = np.ascontiguousarray(w[:, order])
            biases.append(bias[order].reshape(8, 128).T)
    arrays["bqkC"] = np.ascontiguousarray(np.stack(biases, 1))
    arrays["w1_0"] = np.concatenate([arrays["L0_ffn_re_w1"], arrays["L0_ffn_sh_w1"][None]])
    arrays["w2_0"] = np.concatenate([arrays["L0_ffn_re_w2"], arrays["L0_ffn_sh_w2"][None]])
    arrays["b1_0"] = np.concatenate([arrays["L0_ffn_re_b1"], arrays["L0_ffn_sh_b1"][None]])[:, :, None]
    arrays["b2_0"] = np.concatenate([arrays["L0_ffn_re_b2"], arrays["L0_ffn_sh_b2"][None]])
    arrays["mask"] = arrays["mask_BxS2_bk0"]
    for new, old in (("wq1", "Wq"), ("wkv1", "Wkv"), ("wlkv1", "Wlkv"), ("wo1", "Wo")):
        arrays[new] = np.ascontiguousarray(arrays["L1_xattn_" + old].T)
    arrays["wr1"] = np.ascontiguousarray(arrays["L1_ffn_router_w"].T)
    for new, old in (("w1_1", "w1"), ("w2_1", "w2"), ("b1_1", "b1"), ("b2_1", "b2")):
        arrays[new] = np.concatenate([arrays["L1_ffn_e" + old], arrays["L1_ffn_s" + old][None]])
    arrays["b1_1"] = np.ascontiguousarray(arrays["b1_1"].reshape(9, 4, 128).transpose(0, 2, 1))

    nc = bacc.Bacc("TRN2", target_bir_lowering=False, num_devices=1)
    dram = {}
    for n in USED:
        a = arrays[n]
        dram[n] = nc.dram_tensor("in_" + n, a.shape, mybir.dt.from_np(a.dtype), kind="ExternalInput").ap()
    out = nc.dram_tensor("out", (BATCHES, S, D), F32, kind="ExternalOutput").ap()
    build(nc, dram, out)
    got = run_bass_kernel_spmd(nc, [{"in_" + n: arrays[n] for n in USED}], core_ids=[0])
    return got.results[0]["out"]


USED = ["x", "ctx", "ctxT", "ident", "causal", "strided", "wqT0", "wkT0", "wvT0", "L0_xattn_Wo", "L0_xattn_bo",
        "qmask", "kmask", "cosb", "sinb", "pos", "down", "rope_sign", "wqB", "wqBs", "wkB", "wkBs", "wvB", "woB",
        "wqC", "wqCs", "wkC", "wkCs", "bqkC", "L0_ffn_v_w", "L0_ffn_v_b", "L0_ffn_o_w", "L0_ffn_o_b", "L0_ffn_theta",
        "L0_ffn_gamma1", "L0_ffn_gamma2", "L0_ffn_router_w", "L0_ffn_router_b", "b2_0", "w1_0", "w2_0", "b1_0",
        "mask", "L1_xattn_ln_l_g", "L1_xattn_ln_l_b", "L1_xattn_ln_x_g", "L1_xattn_ln_x_b", "L1_xattn_qn_g",
        "L1_xattn_kn_g", "wq1", "wkv1", "wlkv1", "wo1", "L1_xattn_bo", "L1_attn_Wq", "L1_attn_Wk", "L1_attn_Wv",
        "L1_attn_Wp", "L1_attn_bq", "L1_attn_bk", "L1_attn_bv", "L1_attn_bp", "L1_ffn_norm_weight", "wr1", "b2_1",
        "w1_1", "w2_1", "b1_1"]
```

```python
from contextlib import ExitStack

import concourse.bass as bass
from concourse import mybir

F32 = mybir.dt.float32
BF16 = mybir.dt.bfloat16
U8 = mybir.dt.uint8
ALU = mybir.AluOpType
ACT = mybir.ActivationFunctionType
AX = mybir.AxisListType

P = 128
BATCHES = 16
S = 64
PAIRS = BATCHES // 2
ROWS = BATCHES * S
D = 128
CTX = 1601
DC = 96
FULL = CTX // P
KT = FULL + 1
REST = CTX - FULL * P
BANK = 512
NEG = -1.0e30


def rows_of(k):
    return P if k < FULL else REST


class Core:
    pass


class Tally:

    def __init__(self, sem):
        self.sem, self.base = sem, 0

    def wait(self, eng, n):
        eng.wait_ge(self.sem, n + self.base)

    def close(self, n):
        self.base += n


class Chain:

    def __init__(self, eng, sem, base=0):
        self.eng, self.sem, self.base, self.n = eng, sem, base, 0

    def mark(self, ins):
        self.n += 1
        ins.then_inc(self.sem, 1)

    def settle(self):
        self.eng.wait_ge(self.sem, self.base + self.n)

    def link(self, ins):
        self.mark(ins)
        self.settle()


def load_stage(nc, m, dram):
    loaded = m.sem("inputs_loaded")
    zeroed = m.sem("buffers_set")
    casted = m.sem("constants_cast")
    n_loads = [0]
    with nc.Block() as block:
        @block.sync
        def _(sp):
            def load(dst, src):
                sp.dma_start(dst, src).then_inc(loaded, 16)
                n_loads[0] += 1
            load(m.X[:], dram["x"].rearrange("(t b) s d -> (b s) t d", b=2))
            for dst, src in m.loads:
                load(dst, src)
            sp.wait_ge(loaded, 16 * n_loads[0])

        @block.gpsimd
        def _(pool):
            nc.gpsimd.memset(m.nhalf[:], -0.5).then_inc(zeroed, 1)
            nc.gpsimd.memset(m.half[:], 0.5).then_inc(zeroed, 1)
            nc.gpsimd.memset(m.ones[:], 1.0).then_inc(zeroed, 1)
            nc.gpsimd.memset(m.ones_bf[:], 1.0).then_inc(zeroed, 1)
            nc.gpsimd.memset(m.ctx_nat[:], 0.0).then_inc(zeroed, 1)
            pool.wait_ge(zeroed, 5)
            nc.gpsimd.memset(m.ctx_nat[:, :, :, DC:DC + 1], 1.0).then_inc(zeroed, 1)
            pool.wait_ge(zeroed, 6)

        @block.vector
        def _(dve):
            dve.wait_ge(loaded, 16 * (1 + len(m.loads)))
            nc.vector.tensor_copy(m.ident_bf[:], m.ident[:]).then_inc(casted, 1)
            nc.vector.tensor_copy(m.causal_bf[:], m.causal[:]).then_inc(casted, 1)
            nc.vector.tensor_copy(m.strided_bf[:], m.strided[:]).then_inc(casted, 1)
            dve.wait_ge(casted, 3)


def norm_stage(nc, m, name, src, nat, natT, passes):
    stats_ready, rstd_ready, own, nat_ready, turned, natT_ready = (m.tally(n) for n in (
        "norm_stats_ready", "norm_rstd_ready", "norm_dve_steps", "norm_rows_ready", "norm_turned", "norm_copied"))
    with ExitStack() as ctx:
        sb = m.scoped(ctx, name)
        st6, mv = sb("st6", [P, PAIRS, 6]), sb("mv", [P, PAIRS, 2])
        ve, rstd = sb("ve", [P, PAIRS]), sb("rstd", [P, PAIRS])
        with nc.Block() as block:
            @block.vector
            def _(dve):
                chain = Chain(dve, own.sem, own.base)
                cur = src
                for i, (kind, eps, gain, shift) in enumerate(passes):
                    for t in range(PAIRS):
                        chain.mark(nc.vector.bn_stats(st6[:, t, :], cur[:, t, :]))
                    chain.settle()
                    for t in range(PAIRS):
                        chain.mark(nc.vector.bn_aggr(mv[:, t, :], st6[:, t, :]))
                    chain.settle()
                    if kind == "rms":
                        chain.link(nc.vector.tensor_tensor(ve[:], mv[:, :, 0], mv[:, :, 0], ALU.mult))
                        chain.link(nc.vector.tensor_tensor(ve[:], ve[:], mv[:, :, 1], ALU.add))
                        nc.vector.tensor_scalar(ve[:], ve[:], eps, None, ALU.add).then_inc(stats_ready.sem, 1)
                    else:
                        nc.vector.tensor_scalar(ve[:], mv[:, :, 1], eps, None, ALU.add).then_inc(stats_ready.sem, 1)
                    rstd_ready.wait(dve, i + 1)
                    for t in range(PAIRS):
                        if kind == "rms":
                            chain.mark(nc.vector.tensor_scalar(nat[:, t, :], cur[:, t, :], rstd[:, t:t + 1], None,
                                                               ALU.mult))
                        else:
                            chain.mark(nc.vector.tensor_scalar(nat[:, t, :], cur[:, t, :], mv[:, t, 0:1],
                                                               rstd[:, t:t + 1], ALU.subtract, ALU.mult))
                    for table, op in ((gain, ALU.mult), (shift, ALU.add)):
                        if table is not None:
                            chain.settle()
                            both = table[:].unsqueeze(1).broadcast_to([P, PAIRS, D])
                            chain.mark(nc.vector.tensor_tensor(nat[:], nat[:], both, op))
                    chain.settle()
                    cur = nat
                own.close(chain.n)
                nc.vector.tensor_copy(ve[:, 0:1], nat[:, 0, 0:1]).then_inc(nat_ready.sem, 1)

            @block.gpsimd
            def _(pool):
                for i in range(len(passes)):
                    stats_ready.wait(pool, i + 1)
                    nc.gpsimd.tensor_tensor(rstd[:], ve[:], m.nhalf[:, 0:PAIRS], ALU.pow).then_inc(rstd_ready.sem, 1)

            @block.tensor
            def _(pe):
                nat_ready.wait(pe, 1)
                for t in range(PAIRS):
                    out = m.ps[:, t // 4, (t % 4) * P:(t % 4 + 1) * P]
                    ins = nc.tensor.transpose(out, nat[:, t, :], m.ident[:])
                    if t % 4 == 3:
                        ins.then_inc(turned.sem, 1)

            @block.scalar
            def _(act):
                for h in range(2):
                    turned.wait(act, h + 1)
                    nc.scalar.copy(natT[:, h * BANK:(h + 1) * BANK], m.ps[:, h, :]).then_inc(natT_ready.sem, 1)
                natT_ready.wait(act, 2)
    for tally, n in ((stats_ready, len(passes)), (rstd_ready, len(passes)), (nat_ready, 1), (turned, 2),
                     (natT_ready, 2)):
        tally.close(n)


def l0_fold_stage(nc, m):
    folded, copied = m.sem("l0_folded"), m.sem("l0_fold_copied")
    nv_copied, ub_cast = m.sem("l0_nv_copied"), m.sem("l0_ub_cast")
    u_made, u_copied = m.sem("l0_u_made"), m.sem("l0_u_copied")
    H = m.H0
    with nc.Block() as block:
        @block.tensor
        def _(pe):
            for h in range(H):
                ins = nc.tensor.matmul(m.ps[:, h // 4, (h % 4) * P:(h % 4) * P + DC], m.wqT0[:, h, :],
                                       m.wkT0[:, h, :], start=True, stop=True)
            ins.then_inc(folded, 1)
            for h in range(H):
                ins = nc.tensor.matmul(m.ps[0:DC, 2 + h // 4, (h % 4) * P:(h % 4 + 1) * P], m.wvT0[:, h, :],
                                       m.wo0[:, h, :], start=True, stop=True)
            ins.then_inc(folded, 1)
            pe.wait_ge(copied, 1)
            for n in range(2 * H):
                h, half = n // 2, n % 2
                if n >= 4:
                    pe.wait_ge(u_copied, n - 3)
                nc.tensor.matmul(m.ps[0:DC, 4 + n % 4, :], m.mq0[:, h, 0:DC],
                                 m.xT[:, half * BANK:(half + 1) * BANK], start=True, stop=True).then_inc(u_made, 1)

        @block.scalar
        def _(act):
            act.wait_ge(folded, 1)
            nc.scalar.copy(m.mq0[:, :, 0:DC], m.ps[:, 0:2, :].rearrange("p b (h d) -> p (b h) d", d=P)[:, :, 0:DC]
                           ).then_inc(copied, 1)
            for n in range(0, 2 * H):
                h, half = n // 2, n % 2
                act.wait_ge(u_made, n + 1)
                nc.scalar.activation(m.U[0:DC, 8 * half:8 * half + 8, h, :],
                                     m.ps[0:DC, 4 + n % 4, :].rearrange("p (b i) -> p b i", i=S), ACT.Copy,
                                     scale=float(64) ** -0.5).then_inc(u_copied, 1)
            act.wait_ge(u_copied, 2 * H)

        @block.vector
        def _(dve):
            dve.wait_ge(folded, 2)
            nc.vector.tensor_copy(m.nv0[:], m.ps[0:DC, 2:4, :].rearrange("p b (h d) -> p (b h) d", d=P)
                                  ).then_inc(nv_copied, 1)
            dve.wait_ge(nv_copied, 1)
            dve.wait_ge(u_copied, 2 * H)
            for half in range(2):
                nc.vector.tensor_copy(m.Ub[:, 8 * half:8 * half + 8], m.U[0:DC, 8 * half:8 * half + 8]
                                      ).then_inc(ub_cast, 1)
            dve.wait_ge(ub_cast, 2)


def l0_cross_stage(nc, m, dram):
    H = m.H0
    HS = H * S
    ps = m.ps
    MAXB, SB, OB, YB = 0, 4, 6, 7
    ctx_loaded = [m.sem("l0_ctx_loaded_even"), m.sem("l0_ctx_loaded_odd")]
    ctxb_cast = m.sem("l0_ctx_cast")
    rough_ready, rough_used = m.sem("l0_rough_scores_ready"), m.sem("l0_rough_scores_used")
    maxrow_turned, maxrow_written = m.sem("l0_max_turned"), m.sem("l0_max_row_written")
    scores_ready, probs_ready, probs_used = m.sem("l0_scores_ready"), m.sem("l0_probs_ready"), m.sem("l0_probs_used")
    o_copied, recip_ready = m.sem("l0_output_copied"), m.sem("l0_reciprocal_ready")
    spread_ready, o_scaled = m.sem("l0_reciprocal_spread"), m.sem("l0_output_scaled")
    y_ready, x_updated = m.sem("l0_y_ready"), m.sem("l0_x_updated")
    with ExitStack() as ctx:
        sb = m.scoped(ctx, "l0")
        ctxT = sb("ctxT", [DC + 1, 2, CTX])
        ctxTb = sb("ctxTb", [DC, 2, CTX], BF16)
        probs = sb("probs", [P, 2, HS])
        mx = sb("mx", [P, 2, 4])
        osum = sb("osum", [DC + 1, HS])
        recip = sb("recip", [1, HS])
        on = sb("on", [DC, H, P])
        ones_set = m.sem("l0_ones_row_set")

        with nc.Block() as block:
            @block.sync
            def _(sp):
                def load(b, j):
                    jj = bass.ds(j, 1)
                    sp.dma_start(ctxT[0:DC, b, :], dram["ctxT"][jj].rearrange("o d k -> (o d) k")
                                 ).then_inc(ctx_loaded[b], 16)
                    sp.dma_start(m.ctx_nat[:, b, 0:FULL, 0:DC],
                                 dram["ctx"][jj, 0:FULL * P, :].rearrange("o (k p) d -> (o p) k d", p=P)
                                 ).then_inc(ctx_loaded[b], 16)
                    sp.dma_start(m.ctx_nat[0:REST, b, FULL, 0:DC],
                                 dram["ctx"][jj, FULL * P:CTX, :].rearrange("o p d -> (o p) d")
                                 ).then_inc(ctx_loaded[b], 16)
                load(0, 0)
                load(1, 1)
                with sp.Fori(0, PAIRS - 1) as t:
                    for b in range(2):
                        sp.wait_ge(probs_used, 2 + KT * (2 * t + b + 1))
                        load(b, 2 * t + 2 + b)

            @block.gpsimd
            def _(pool):
                nc.gpsimd.memset(ctxT[DC:DC + 1, :, :], 1.0).then_inc(ones_set, 1)

                def cast(b, t):
                    pool.wait_ge(ctx_loaded[b], 48 * (t + 1))
                    pool.sem_inc(m.turns_pool, 1)
                    nc.gpsimd.tensor_copy(ctxTb[:, b, :], ctxT[0:DC, b, :]).then_inc(ctxb_cast, 1)
                cast(0, 0)
                cast(1, 0)
                with pool.Fori(1, PAIRS) as t:
                    for b in range(2):
                        pool.wait_ge(rough_ready, 4 * (2 * t + b - 1))
                        cast(b, t)

            def rough(pe, b, j, r):
                if r == 0:
                    pe.wait_ge(ctxb_cast, j + 1)
                pe.wait_ge(rough_used, 1 + 4 * j + r)
                for c in range(4):
                    n = min(BANK, CTX - c * BANK)
                    ins = nc.tensor.matmul(
                        ps[:, MAXB + c, 0:n],
                        m.Ub[:, bass.ds(j, 1), 2 * r:2 * r + 2, :].rearrange("p o h i -> p (o h i)"),
                        ctxTb[:, b, c * BANK:c * BANK + n], start=True, stop=True)
                ins.then_inc(rough_ready, 1)

            def turn_max(pe, b, j):
                pe.wait_ge(rough_used, 1 + 4 * (j + 1))
                for r in range(4):
                    ins = nc.tensor.matmul(ps[0:1, YB, r * P:(r + 1) * P], mx[:, b, r:r + 1], m.ident[:],
                                           start=True, stop=True)
                ins.then_inc(maxrow_turned, 1)

            def pe_pair(pe, t, last):
                for b in range(2):
                    j = 2 * t + b
                    lastb = last and b == 1
                    pe.wait_ge(maxrow_written, j + 1)

                    def scores(k):
                        r = rows_of(k)
                        nc.tensor.matmul(ps[0:r, SB + (KT * b + k) % 2, :], ctxT[:, b, k * P:k * P + r],
                                         m.U[:, bass.ds(j, 1), :, :].rearrange("p o h i -> p (o h i)"),
                                         start=True, stop=True).then_inc(scores_ready, 1)
                    scores(0)
                    for k in range(KT):
                        if k + 1 < KT:
                            scores(k + 1)
                        if not lastb and k in (1, 3, 6, 9):
                            rough(pe, 1 - b, j + 1, (1, 3, 6, 9).index(k))
                        pe.wait_ge(probs_ready, KT * j + k + 1)
                        if k == 0:
                            pe.wait_ge(o_copied, 1 + j)
                        r = rows_of(k)
                        nc.tensor.matmul(ps[0:DC + 1, OB, :], m.ctx_nat[0:r, b, k, :], probs[0:r, (KT * b + k) % 2, :],
                                         start=(k == 0), stop=(k == KT - 1)).then_inc(probs_used, 1)
                    if not lastb:
                        if b == 0:
                            pe.wait_ge(x_updated, 1 + t)
                        else:
                            pe.wait_ge(o_scaled, 1 + 2 * t + 1)
                        turn_max(pe, 1 - b, j + 1)
                    pe.wait_ge(recip_ready, j + 1)
                    if lastb:
                        pe.wait_ge(o_scaled, 1 + j)
                    else:
                        pe.wait_ge(maxrow_written, j + 2)
                    nc.tensor.matmul(ps[0:DC, YB, :], m.ones[0:1, 0:DC], recip[:], start=True, stop=True
                                     ).then_inc(spread_ready, 1)
                pe.wait_ge(o_scaled, 1 + 2 * t + 2)
                for h in range(H):
                    nc.tensor.matmul(ps[:, YB, 0:D], on[:, h, :], m.nv0[:, h, :], start=(h == 0), stop=False)
                nc.tensor.matmul(ps[:, YB, 0:D], m.ones[0:1, 0:P], m.bo0[:], start=False, stop=True
                                 ).then_inc(y_ready, 1)

            @block.tensor
            def _(pe):
                pe.sem_inc(probs_used, 2)
                pe.wait_ge(ones_set, 1)
                pe.wait_ge(ctx_loaded[0], 48)
                for r in range(4):
                    rough(pe, 0, 0, r)
                turn_max(pe, 0, 0)
                with pe.Fori(0, PAIRS - 1) as t:
                    pe_pair(pe, t, False)
                pe_pair(pe, PAIRS - 1, True)

            def act_pair(act, t):
                for b in range(2):
                    j = 2 * t + b
                    for k in range(KT):
                        act.wait_ge(scores_ready, KT * j + k + 1)
                        act.wait_ge(probs_used, KT * j + k + 1)
                        r = rows_of(k)
                        nc.scalar.activation(probs[0:r, (KT * b + k) % 2, :], ps[0:r, SB + (KT * b + k) % 2, :], ACT.Exp
                                             ).then_inc(probs_ready, 1)
                    act.wait_ge(probs_used, 2 + KT * (j + 1))
                    act.wait_ge(o_scaled, 1 + j)
                    nc.scalar.copy(osum[:], ps[0:DC + 1, OB, :]).then_inc(o_copied, 1)

            @block.scalar
            def _(act):
                act.sem_inc(o_copied, 1)
                with act.Fori(0, PAIRS) as t:
                    act_pair(act, t)

            def take_max(dve, b, j):
                for r in range(4):
                    dve.wait_ge(rough_ready, 4 * j + r + 1)
                    nc.vector.tensor_reduce(mx[:, b, r:r + 1],
                                            ps[:, MAXB:MAXB + 4, :].rearrange("p c n -> p (c n)")[:, 0:CTX],
                                            axis=AX.X, op=ALU.max).then_inc(rough_used, 1)
                dve.wait_ge(maxrow_turned, j + 1)
                nc.vector.tensor_scalar(m.U[DC:DC + 1, bass.ds(j, 1), :, :].rearrange("p o h i -> p (o h i)"),
                                        ps[0:1, YB, :], -1.0, None, ALU.mult).then_inc(maxrow_written, 1)

            def dve_pair(dve, t, last):
                for b in range(2):
                    j = 2 * t + b
                    if not (last and b == 1):
                        take_max(dve, 1 - b, j + 1)
                    dve.wait_ge(o_copied, 2 + j)
                    nc.vector.reciprocal(recip[:], osum[DC:DC + 1, :]).then_inc(recip_ready, 1)
                    dve.wait_ge(spread_ready, j + 1)
                    nc.vector.tensor_tensor(on[:, :, S * b:S * b + S],
                                            osum[0:DC, :].rearrange("p (h i) -> p h i", i=S),
                                            ps[0:DC, YB, :].rearrange("p (h i) -> p h i", i=S), ALU.mult
                                            ).then_inc(o_scaled, 1)
                dve.wait_ge(y_ready, t + 1)
                xt = m.X[:, bass.ds(t, 1), :].rearrange("p o d -> p (o d)")
                nc.vector.tensor_tensor(xt, xt, ps[:, YB, 0:D], ALU.add).then_inc(x_updated, 1)

            @block.vector
            def _(dve):
                dve.sem_inc(rough_used, 1)
                dve.sem_inc(x_updated, 1)
                dve.sem_inc(o_scaled, 1)
                take_max(dve, 0, 0)
                with dve.Fori(0, PAIRS - 1) as t:
                    dve_pair(dve, t, False)
                dve_pair(dve, PAIRS - 1, True)


HP = 8


def project_small_heads_stage(nc, m, name, w, rope, bias):
    made, copied = m.sem(name + "_made"), m.sem(name + "_copied")
    own = m.sem(name + "_dve_steps")
    ps = m.ps
    n_qk = 4 if rope else 2
    with ExitStack() as ctx:
        sb = m.scoped(ctx, name)
        a, b = sb("a", [P, ROWS]), sb("b", [P, ROWS])
        with nc.Block() as block:
            @block.tensor
            def _(pe):
                for n in range(n_qk):
                    for half in range(2):
                        ins = nc.tensor.matmul(ps[:, 2 * n + half, :], w[n][:],
                                               m.xT[:, half * BANK:(half + 1) * BANK], start=True, stop=True)
                    ins.then_inc(made, 1)
                pe.wait_ge(copied if bias else own, 1 if bias else 3)
                if bias:
                    pe.wait_ge(copied, 2)
                for j in range(BATCHES):
                    ins = nc.tensor.matmul(ps[0:S, j // 4, (j % 4) * P:(j % 4 + 1) * P], m.xT[:, j * S:(j + 1) * S],
                                           w[-1][:], start=True, stop=True)
                ins.then_inc(made, 1)

            if bias:
                @block.scalar
                def _(act):
                    for n, dst in ((0, m.qT), (1, m.kT)):
                        act.wait_ge(made, n + 1)
                        nc.scalar.activation(dst[:], ps[:, 2 * n:2 * n + 2, :].rearrange("p b n -> p (b n)"),
                                             ACT.Identity, bias=bias[n][:]).then_inc(copied, 1)
                    act.wait_ge(copied, 2)

            @block.vector
            def _(dve):
                chain = Chain(dve, own)
                if rope:
                    cos = m.cosb[:].unsqueeze(1).broadcast_to([P, BATCHES, S])
                    sin = m.sinb[:].unsqueeze(1).broadcast_to([P, BATCHES, S])
                    for n, dst in ((0, m.qT), (2, m.kT)):
                        for i, (tmp, table) in enumerate(((a, cos), (b, sin))):
                            dve.wait_ge(made, n + i + 1)
                            src = ps[:, 2 * (n + i):2 * (n + i) + 2, :].rearrange("p c (b i) -> p (c b) i", i=S)
                            chain.mark(nc.vector.tensor_tensor(tmp[:].rearrange("p (b i) -> p b i", i=S), src, table,
                                                               ALU.mult))
                        chain.settle()
                        chain.link(nc.vector.tensor_tensor(dst[:], a[:], b[:], ALU.add))
                dve.wait_ge(made, n_qk + 1)
                src = ps[0:S, 0:4, :].rearrange("p b (j d) -> p (b j) d", d=D)
                if bias:
                    chain.link(nc.vector.tensor_tensor(m.V[:], src, bias[2][:].unsqueeze(1).broadcast_to([S, BATCHES, D]),
                                                       ALU.add))
                else:
                    chain.link(nc.vector.tensor_copy(m.V[:], src))


class Softmax:

    def __init__(self, nc, m, name, sb, scale):
        self.nc, self.m, self.scale = nc, m, scale
        self.less, self.exps, self.probs = (sb(n, [P, 2, BANK]) for n in ("less", "exps", "probs"))
        self.probsT = sb("probsT", [S, 2, HP * P])
        self.mx, self.sums, self.recip = (sb(n, [P, 2, HP]) for n in ("mx", "sums", "recip"))
        self.signals = {n: m.tally("softmax_" + n) for n in (
            "scores_ready", "mx_ready", "less_ready", "exps_ready", "sums_ready", "recip_ready", "probs_ready",
            "turned", "probsT_ready")}
        (self.scores_ready, self.mx_ready, self.less_ready, self.exps_ready, self.sums_ready, self.recip_ready,
         self.probs_ready, self.turned, self.probsT_ready) = self.signals.values()

    def close(self, divided=True):
        for tally in self.signals.values():
            if divided or tally is not self.probs_ready:
                tally.close(BATCHES)

    @staticmethod
    def by_head(ap):
        return ap.rearrange("p (h k) -> p h k", k=S)

    def less_max(self, dve, b, j, bank):
        nc = self.nc
        scores = self.by_head(self.m.ps[:, bank, :])
        self.scores_ready.wait(dve, j + 1)
        nc.vector.tensor_reduce(self.mx[:, b, :], scores, axis=AX.X, op=ALU.max).then_inc(self.mx_ready.sem, 1)
        self.mx_ready.wait(dve, j + 1)
        nc.vector.tensor_tensor(self.by_head(self.less[:, b, :]), scores,
                                self.mx[:, b, :].unsqueeze(2).broadcast_to([P, HP, S]), ALU.subtract
                                ).then_inc(self.less_ready.sem, 1)

    def exp(self, act, b, j):
        self.less_ready.wait(act, j + 1)
        self.nc.scalar.activation(self.exps[:, b, :], self.less[:, b, :], ACT.Exp, scale=self.scale
                                  ).then_inc(self.exps_ready.sem, 1)

    def sum(self, dve, b, j):
        nc = self.nc
        self.exps_ready.wait(dve, j + 1)
        nc.vector.tensor_reduce(self.sums[:, b, :], self.by_head(self.exps[:, b, :]), axis=AX.X, op=ALU.add
                                ).then_inc(self.sums_ready.sem, 1)
        self.sums_ready.wait(dve, j + 1)
        nc.vector.reciprocal(self.recip[:, b, :], self.sums[:, b, :]).then_inc(self.recip_ready.sem, 1)

    def divide(self, pool, b, j):
        self.recip_ready.wait(pool, j + 1)
        self.nc.gpsimd.tensor_tensor(self.by_head(self.probs[:, b, :]), self.by_head(self.exps[:, b, :]),
                                     self.recip[:, b, :].unsqueeze(2).broadcast_to([P, HP, S]), ALU.mult
                                     ).then_inc(self.probs_ready.sem, 1)

    def turn(self, pe, b, j, probs, ready):
        ready.wait(pe, j + 1)
        pe.sem_inc(self.m.turns_pe, 1)
        for hp in range(HP):
            ins = self.nc.tensor.transpose(self.m.ps[0:S, 2 + 2 * b + hp // 4, (hp % 4) * P:(hp % 4 + 1) * P],
                                           probs[:, b, hp * S:(hp + 1) * S], self.m.ident[:])
        ins.then_inc(self.turned.sem, 1)

    def copy_turned(self, act, b, j):
        self.turned.wait(act, j + 1)
        self.nc.scalar.copy(self.probsT[:, b, :], self.m.ps[0:S, 2 + 2 * b:4 + 2 * b, :].rearrange("p c n -> p (c n)")
                            ).then_inc(self.probsT_ready.sem, 1)


def small_heads_stage(nc, m, name, mask_bf, wo, bo):
    ps = m.ps
    per_y = 1 if bo is None else 2
    signals = [m.tally("heads_" + n) for n in ("operands_ready", "pv_ready", "o_copied", "o_turned", "oT_copied",
                                               "y_ready", "x_updated")]
    operands_ready, pv_ready, o_copied, o_turned, oT_copied, y_ready, x_updated = signals
    with ExitStack() as ctx:
        sb = m.scoped(ctx, name)
        sm = Softmax(nc, m, name, sb, float(8) ** -0.5)
        q2, kb = sb("q2", [P, 2, 2, S]), sb("kb", [P, 2, HP, S])
        o, oT = sb("o", [P, HP, 2, 8]), sb("oT", [P, P])
        with nc.Block() as block:
            def pe_scores(pe, t, first):
                for b in range(2):
                    j = 2 * t + b
                    operands_ready.wait(pe, 2 * j + 2)
                    if not first:
                        sm.less_ready.wait(pe, j - 1)
                    nc.tensor.matmul(ps[:, b, :], m.ident_bf[:], mask_bf[:], start=True, stop=False)
                    nc.tensor.matmul(ps[:, b, :], q2[:, b].rearrange("p h i -> p (h i)"),
                                     kb[:, b].rearrange("p h k -> p (h k)"), start=False, stop=True
                                     ).then_inc(sm.scores_ready.sem, 1)

            def pe_turn_output(pe, t, first):
                o_copied.wait(pe, 4 * t + 4)
                if not first:
                    x_updated.wait(pe, t)
                nc.tensor.transpose(ps[:, 7, 0:P], o[:].rearrange("p a b d -> p (a b d)"), m.ident[:]
                                    ).then_inc(o_turned.sem, 1)

            def pe_turn_probs(pe, t, first):
                for b in range(2):
                    j = 2 * t + b
                    if not first:
                        sm.probsT_ready.wait(pe, j - 1)
                    sm.turn(pe, b, j, sm.exps, sm.exps_ready)

            def pe_output(pe, t):
                oT_copied.wait(pe, t + 1)
                nc.tensor.matmul(ps[:, 7, P:2 * P], oT[:], wo[:], start=True, stop=bo is None
                                 ).then_inc(y_ready.sem, 1)
                if bo is not None:
                    nc.tensor.matmul(ps[:, 7, P:2 * P], m.ones[0:1, 0:P], bo[:], start=False, stop=True
                                     ).then_inc(y_ready.sem, 1)

            def pe_values(pe, t, first):
                if not first:
                    o_copied.wait(pe, 4 * t)
                for b in range(2):
                    j = 2 * t + b
                    sm.probsT_ready.wait(pe, j + 1)
                    for hp in range(HP):
                        v = (m.V[:, bass.ds(j, 1), 16 * hp:16 * (hp + 1)].rearrange("p o d -> p (o d)"))
                        ins = nc.tensor.matmul(ps[:, 6, P * b + 16 * hp:P * b + 16 * (hp + 1)],
                                               sm.probsT[:, b, hp * P:(hp + 1) * P], v, start=True, stop=True)
                    ins.then_inc(pv_ready.sem, 1)

            @block.tensor
            def _(pe):
                pe_scores(pe, 0, True)
                pe_scores(pe, 1, False)
                pe_turn_probs(pe, 0, True)
                pe_values(pe, 0, True)
                pe_scores(pe, 2, False)
                pe_turn_output(pe, 0, True)
                pe_turn_probs(pe, 1, False)
                pe_output(pe, 0)
                pe_values(pe, 1, False)
                with pe.Fori(0, PAIRS - 3) as u:
                    pe_scores(pe, u + 3, False)
                    pe_turn_output(pe, u + 1, False)
                    pe_turn_probs(pe, u + 2, False)
                    pe_output(pe, u + 1)
                    pe_values(pe, u + 2, False)
                pe_turn_output(pe, PAIRS - 2, False)
                pe_turn_probs(pe, PAIRS - 1, False)
                pe_output(pe, PAIRS - 2)
                pe_values(pe, PAIRS - 1, False)
                pe_turn_output(pe, PAIRS - 1, False)
                pe_output(pe, PAIRS - 1)

            def act_exp(act, t, first):
                for b in range(2):
                    if not first:
                        sm.sums_ready.wait(act, 2 * t + b - 1)
                    sm.exp(act, b, 2 * t + b)

            def act_copy_output(act, t):
                o_turned.wait(act, t + 1)
                nc.scalar.copy(oT[:], ps[:, 7, 0:P]).then_inc(oT_copied.sem, 1)

            def act_copy_probs(act, t, first):
                for b in range(2):
                    if not first:
                        pv_ready.wait(act, 2 * t + b - 1)
                    sm.copy_turned(act, b, 2 * t + b)

            @block.scalar
            def _(act):
                act_exp(act, 0, True)
                act_copy_probs(act, 0, True)
                act_exp(act, 1, False)
                with act.Fori(0, PAIRS - 2) as u:
                    act_copy_output(act, u)
                    act_copy_probs(act, u + 1, False)
                    act_exp(act, u + 2, False)
                act_copy_output(act, PAIRS - 2)
                act_copy_probs(act, PAIRS - 1, False)
                act_copy_output(act, PAIRS - 1)

            def operands(pool, t, first):
                for b in range(2):
                    if not first:
                        sm.scores_ready.wait(pool, 2 * t + b - 1)
                        pool.sem_inc(m.turns_pool, 1)
                    cols = bass.ds((2 * t + b) * S, S)
                    nc.gpsimd.tensor_tensor(q2[:, b], m.qT[:, cols].unsqueeze(1).broadcast_to([P, 2, S]),
                                            m.qmask[:].unsqueeze(2).broadcast_to([P, 2, S]), ALU.mult
                                            ).then_inc(operands_ready.sem, 1)
                    nc.gpsimd.tensor_tensor(kb[:, b], m.kT[:, cols].unsqueeze(1).broadcast_to([P, HP, S]),
                                            m.kmask[:].unsqueeze(2).broadcast_to([P, HP, S]), ALU.mult
                                            ).then_inc(operands_ready.sem, 1)

            @block.gpsimd
            def _(pool):
                operands(pool, 0, True)
                with pool.Fori(0, PAIRS - 1) as u:
                    operands(pool, u + 1, False)

            def dve_front(dve, t):
                for b in range(2):
                    sm.less_max(dve, b, 2 * t + b, b)

            def dve_sums(dve, t):
                for b in range(2):
                    sm.sum(dve, b, 2 * t + b)

            def dve_output(dve, t):
                y_ready.wait(dve, per_y * (t + 1))
                xt = m.X[:, bass.ds(t, 1), :].rearrange("p o d -> p (o d)")
                nc.vector.tensor_tensor(xt, xt, ps[:, 7, P:2 * P], ALU.add).then_inc(x_updated.sem, 1)

            def dve_divide(dve, t, first):
                if not first:
                    o_turned.wait(dve, t)
                sm.recip_ready.wait(dve, 2 * t + 2)
                pv_ready.wait(dve, 2 * t + 2)
                for b in range(2):
                    for h2 in range(2):
                        rows = slice(S * h2, S * h2 + S)
                        src = ps[rows, 6, P * b:P * b + P].rearrange("p (h c) -> p h c", c=16)
                        nc.vector.tensor_tensor(o[S * b:S * b + S, :, h2, :], src[:, :, 8 * h2:8 * h2 + 8],
                                                sm.recip[rows, b, :].unsqueeze(2).broadcast_to([S, HP, 8]), ALU.mult
                                                ).then_inc(o_copied.sem, 1)

            @block.vector
            def _(dve):
                dve_front(dve, 0)
                dve_sums(dve, 0)
                dve_front(dve, 1)
                dve_divide(dve, 0, True)
                dve_sums(dve, 1)
                with dve.Fori(0, PAIRS - 2) as u:
                    dve_front(dve, u + 2)
                    dve_output(dve, u)
                    dve_divide(dve, u + 1, False)
                    dve_sums(dve, u + 2)
                dve_output(dve, PAIRS - 2)
                dve_divide(dve, PAIRS - 1, False)
                dve_output(dve, PAIRS - 1)
    for tally, per_pair in zip(signals, (4, 2, 4, 1, 1, per_y, 1)):
        tally.close(per_pair * PAIRS)
    sm.close(divided=False)


def angles_stage(nc, m):
    own, pool_steps, done = m.sem("angles_dve_steps"), m.sem("angles_pool_steps"), m.sem("angles_done")
    ready = m.sem("angles_ready")
    TWO_PI, PI = 6.283185307179586, 3.1415925
    C1 = 6.28125
    C2 = 0.0019350051879882812
    C3 = TWO_PI - C1 - C2
    ROUND = 12582912.0
    with ExitStack() as ctx:
        sb = m.scoped(ctx, "angles")
        a, n, r = sb("a", [P, P]), sb("n", [P, P]), sb("r", [P, P])
        with nc.Block() as block:
            @block.vector
            def _(dve):
                chain = Chain(dve, own)
                chain.link(nc.vector.tensor_scalar(a[:], m.pos[:], m.theta[:], None, ALU.mult))
                chain.link(nc.vector.tensor_scalar(n[:], a[:], 1.0 / TWO_PI, ROUND, ALU.mult, ALU.add))
                chain.link(nc.vector.tensor_scalar(n[:], n[:], -ROUND, None, ALU.add))
                for c in (C1, C2, C3):
                    chain.link(nc.vector.scalar_tensor_tensor(out=a[:], in0=n[:], scalar=-c, in1=a[:], op0=ALU.mult,
                                                              op1=ALU.add))
                chain.link(nc.vector.tensor_scalar(a[:], a[:], PI, -PI, ALU.min, ALU.max))
                chain.link(nc.vector.tensor_scalar(r[:], a[:], -1.0, None, ALU.mult))
                chain.link(nc.vector.tensor_tensor(r[:], r[:], a[:], ALU.max))
                chain.link(nc.vector.tensor_scalar(r[:], r[:], -1.0, TWO_PI / 4, ALU.mult, ALU.add))
                nc.vector.tensor_copy(n[:, 0:1], r[:, 0:1]).then_inc(ready, 1)
                dve.wait_ge(done, 2)
                chain.link(nc.vector.tensor_scalar(m.sinc[:], m.sinc[:], m.rope_sign[:], None, ALU.mult))

            @block.scalar
            def _(act):
                act.wait_ge(ready, 1)
                nc.scalar.activation(m.sinc[:], a[:], ACT.Sin).then_inc(done, 1)
                nc.scalar.activation(m.cosc[:], r[:], ACT.Sin).then_inc(done, 1)
                act.wait_ge(done, 2)


def wide_heads_stage(nc, m):
    ps = m.ps
    name = "wide"
    xs_ready = m.sem("wide_x_staged")
    proj_ready, proj_used = m.sem("wide_projected"), m.sem("wide_projection_used")
    rot_ready = m.sem("wide_rotated")
    v_made, v_copied = m.sem("wide_v_made"), m.sem("wide_v_copied")
    pv_ready, o_copied = m.sem("wide_pv_ready"), m.sem("wide_o_copied")
    y_ready, ao_ready = m.sem("wide_y_ready"), m.sem("wide_attn_out_ready")
    qbd_zeroed, bias_steps = m.sem("wide_qbd_zeroed"), m.sem("wide_bias_steps")
    with ExitStack() as ctx:
        sb = m.scoped(ctx, name)
        sm = Softmax(nc, m, name, sb, float(64) ** -0.5)
        xs = sb("xs", [P, P])
        ta, tb = sb("ta", [P, 2, HP, P]), sb("tb", [P, 2, HP, P])
        qbd = sb("qbd", [P, 2, HP, P])
        kr = sb("kr", [P, HP, P])
        V = sb("v", [P, HP * P])
        probs, probsT = sb("pair_probs", [P, HP, 2, S]), sb("pair_probsT", [P, HP, P])
        oT = sb("oT", [P, HP, P])

        def proj_banks(n):
            return 2 * (n % 2)

        with nc.Block() as block:
            def project(pe, t, n):
                x = m.xT[:, bass.ds(t * P, P)]
                for hp in range(HP):
                    ins = nc.tensor.matmul(ps[:, proj_banks(n) + hp // 4, (hp % 4) * P:(hp % 4 + 1) * P],
                                           m.wqk[n][:, hp * P:(hp + 1) * P], x, start=True, stop=True)
                ins.then_inc(proj_ready, 1)

            def output(pe, t, last):
                pe.wait_ge(o_copied, 4 * t + 4)
                if last:
                    pe.wait_ge(ao_ready, t)
                else:
                    sm.less_ready.wait(pe, 2 * t + 4)
                for hp in range(HP):
                    ins = nc.tensor.matmul(ps[:, 4, 0:D], oT[:, hp, :], m.wo_c[:, hp, :], start=(hp == 0),
                                           stop=(hp == HP - 1))
                ins.then_inc(y_ready, 1)

            def turn_probs(pe, t, first):
                sm.probs_ready.wait(pe, 2 * t + 2)
                if not first:
                    pe.wait_ge(ao_ready, t)
                pe.sem_inc(m.turns_pe, 1)
                for hp in range(HP):
                    ins = nc.tensor.transpose(ps[:, 4 + hp // 4, (hp % 4) * P:(hp % 4 + 1) * P],
                                              probs[:, hp].rearrange("p b k -> p (b k)"), m.ident[:])
                    if hp % 4 == 3:
                        ins.then_inc(sm.turned.sem, 1)

            def values_product(pe, t, b):
                for hp in range(HP):
                    if b == 0 and hp % 4 == 0:
                        sm.probsT_ready.wait(pe, 2 * t + hp // 4 + 1)
                    ins = nc.tensor.matmul(ps[:, (6, 0)[b] + hp // 4, (hp % 4) * P:(hp % 4 + 1) * P],
                                           V[S * b:S * b + S, hp * P:(hp + 1) * P], probsT[S * b:S * b + S, hp, :],
                                           start=True, stop=True)
                ins.then_inc(pv_ready, 1)

            def scores(pe, t, first):
                if not first:
                    sm.probsT_ready.wait(pe, 2 * t)
                for b in range(2):
                    pe.wait_ge(rot_ready, 4 * t + 3 + b)
                    nc.tensor.matmul(ps[:, 4 + b, :], m.ident_bf[:], m.causal_bf[:], start=True, stop=False)
                    for hp in range(HP):
                        ins = nc.tensor.matmul(ps[:, 4 + b, hp * S:(hp + 1) * S], qbd[:, b, hp, :],
                                               kr[:, hp, b * S:(b + 1) * S], start=False, stop=(hp == HP - 1))
                    ins.then_inc(sm.scores_ready.sem, 1)

            def values(pe, t, first):
                pe.wait_ge(xs_ready, t + 1)
                if not first:
                    pe.wait_ge(o_copied, 4 * t - 2)
                for c in range(2):
                    ins = nc.tensor.matmul(ps[:, 6 + c, :], xs[:], m.wv_c[:, c * BANK:(c + 1) * BANK],
                                           start=True, stop=True)
                ins.then_inc(v_made, 1)

            def pe_turn(pe, t, front, back, out):
                if front:
                    if back and out:
                        pe.wait_ge(o_copied, 4 * t - 4)
                    project(pe, t, 0)
                    if back:
                        pe.wait_ge(proj_used, 4 * t)
                    project(pe, t, 1)
                if out:
                    output(pe, t - 2, False)
                if front:
                    pe.wait_ge(proj_used, 4 * t + 1)
                    project(pe, t, 2)
                if back:
                    turn_probs(pe, t - 1, not out)
                if front:
                    pe.wait_ge(proj_used, 4 * t + 2)
                    project(pe, t, 3)
                if back:
                    pe.wait_ge(v_copied, t)
                    values_product(pe, t - 1, 0)
                    if front:
                        pe.wait_ge(proj_used, 4 * t + 3)
                    values_product(pe, t - 1, 1)
                if front:
                    scores(pe, t, not back)
                    values(pe, t, not back)

            @block.tensor
            def _(pe):
                pe.wait_ge(bias_steps, 1)
                for hp in range(HP):
                    nc.tensor.matmul(ps[:, 6, 0:D], ta[:, 0, hp, :], m.wo_c[:, hp, :], start=(hp == 0), stop=False)
                nc.tensor.matmul(ps[:, 6, 0:D], m.ones[0:1, 0:P], m.bo_c[:], start=False, stop=True
                                 ).then_inc(y_ready, 1)
                pe.wait_ge(bias_steps, 2)
                pe.wait_ge(qbd_zeroed, 1)
                pe_turn(pe, 0, True, False, False)
                pe_turn(pe, 1, True, True, False)
                with pe.Fori(0, PAIRS - 2) as u:
                    pe_turn(pe, u + 2, True, True, True)
                pe_turn(pe, PAIRS, False, True, True)
                output(pe, PAIRS - 1, True)

            def stage_x(act, t, first):
                if not first:
                    act.wait_ge(v_made, t)
                    act.sem_inc(m.turns_act, 1)
                nc.scalar.copy(xs[:], m.xT[:, bass.ds(t * P, P)]).then_inc(xs_ready, 1)

            def copy_values(act, t, first):
                act.wait_ge(v_made, t + 1)
                if not first:
                    act.wait_ge(pv_ready, 2 * t)
                nc.scalar.copy(V[:], ps[:, 6:8, :].rearrange("p c n -> p (c n)")).then_inc(v_copied, 1)

            def exps(act, t, first):
                for b in range(2):
                    if not first:
                        sm.probs_ready.wait(act, 2 * t + b - 1)
                    sm.exp(act, b, 2 * t + b)

            def copy_turned(act, t, first):
                if not first:
                    act.wait_ge(pv_ready, 2 * t)
                for c in range(2):
                    sm.turned.wait(act, 2 * t + c + 1)
                    nc.scalar.copy(probsT[:, 4 * c:4 * c + 4, :], ps[:, 4 + c, :].rearrange("p (h i) -> p h i", i=P)
                                   ).then_inc(sm.probsT_ready.sem, 1)

            def copy_products(act, t, first):
                if not first:
                    act.wait_ge(y_ready, t + 1)
                for b in range(2):
                    act.wait_ge(pv_ready, 2 * t + b + 1)
                    for h2 in range(2):
                        rows, c = slice(S * h2, S * h2 + S), (6, 0)[b]
                        src = ps[rows, c:c + 2, :].rearrange("p c (h i) -> p (c h) i", i=P)
                        nc.scalar.copy(oT[rows, :, S * b:S * b + S], src[:, :, S * h2:S * h2 + S]
                                       ).then_inc(o_copied, 1)

            @block.scalar
            def _(act):
                stage_x(act, 0, True)
                exps(act, 0, True)
                copy_values(act, 0, True)
                stage_x(act, 1, False)
                copy_turned(act, 0, True)
                copy_products(act, 0, True)
                exps(act, 1, False)
                copy_values(act, 1, False)
                with act.Fori(0, PAIRS - 2) as u:
                    stage_x(act, u + 2, False)
                    copy_turned(act, u + 1, False)
                    copy_products(act, u + 1, False)
                    exps(act, u + 2, False)
                    copy_values(act, u + 2, False)
                copy_turned(act, PAIRS - 1, False)
                copy_products(act, PAIRS - 1, False)

            def divide(pool, t, first):
                pool.wait_ge(rot_ready, 4 * t + 4)
                if not first:
                    sm.turned.wait(pool, 2 * t)
                for b in range(2):
                    sm.recip_ready.wait(pool, 2 * t + b + 1)
                    nc.gpsimd.tensor_tensor(probs[:, :, b, :], sm.by_head(sm.exps[:, b, :]),
                                            sm.recip[:, b, :].unsqueeze(2).broadcast_to([P, HP, S]), ALU.mult
                                            ).then_inc(sm.probs_ready.sem, 1)

            def rotate(pool, t, first):
                if not first:
                    sm.scores_ready.wait(pool, 2 * t)
                    sm.probs_ready.wait(pool, 2 * t)
                pool.wait_ge(proj_used, 4 * t + 2)
                for h2 in range(2):
                    rows = slice(S * h2, S * h2 + S)
                    nc.gpsimd.tensor_tensor(qbd[rows, :, :, S * h2:S * h2 + S],
                                            ta[rows, 0].rearrange("p h (b i) -> p b h i", b=2),
                                            tb[rows, 0].rearrange("p h (b i) -> p b h i", b=2), ALU.add
                                            ).then_inc(rot_ready, 1)
                pool.wait_ge(rot_ready, 4 * t + 2)
                pool.wait_ge(proj_used, 4 * t + 4)
                for b in range(2):
                    cols = slice(S * b, S * b + S)
                    nc.gpsimd.tensor_tensor(kr[:, :, cols], ta[:, 1, :, cols], tb[:, 1, :, cols], ALU.add
                                            ).then_inc(rot_ready, 1)

            @block.gpsimd
            def _(pool):
                nc.gpsimd.memset(qbd[:], 0.0).then_inc(qbd_zeroed, 1)
                pool.wait_ge(qbd_zeroed, 1)
                rotate(pool, 0, True)
                divide(pool, 0, True)
                with pool.Fori(0, PAIRS - 1) as u:
                    rotate(pool, u + 1, False)
                    divide(pool, u + 1, False)

            def bias_turn(dve, t, n, first):
                dve.wait_ge(proj_ready, 4 * t + n + 1)
                if not first and n in (0, 2):
                    dve.wait_ge(rot_ready, 4 * t - (2 if n == 0 else 0))
                dst, table = ((ta, m.cosc), (tb, m.sinc))[n % 2]
                for hp in range(HP):
                    ins = nc.vector.scalar_tensor_tensor(
                        out=dst[:, n // 2, hp, :],
                        in0=ps[:, proj_banks(n) + hp // 4, (hp % 4) * P:(hp % 4 + 1) * P],
                        scalar=m.bqk[:, n, hp:hp + 1], in1=table[:], op0=ALU.add, op1=ALU.mult)
                ins.then_inc(proj_used, 1)

            def attn_out(dve, t):
                dve.wait_ge(y_ready, t + 2)
                tt = bass.ds(t, 1)
                nc.vector.tensor_tensor(m.AO[:, tt, :].rearrange("p o d -> p (o d)"), ps[:, 4, 0:D],
                                        m.Y[:, tt, :].rearrange("p o d -> p (o d)"), ALU.add
                                        ).then_inc(ao_ready, 1)

            def softmax(dve, t):
                for b in range(2):
                    sm.less_max(dve, b, 2 * t + b, 4 + b)
                for b in range(2):
                    sm.sum(dve, b, 2 * t + b)

            @block.vector
            def _(dve):
                nc.vector.tensor_copy(ta[:, 0], m.bv_c[:].unsqueeze(2).broadcast_to([P, HP, P])
                                      ).then_inc(bias_steps, 1)
                dve.wait_ge(y_ready, 1)
                nc.vector.tensor_tensor(m.Y[:], m.Y[:], ps[:, 6, 0:D].unsqueeze(1).broadcast_to([P, PAIRS, D]),
                                        ALU.add).then_inc(bias_steps, 1)
                dve.wait_ge(bias_steps, 2)
                for t in range(2):
                    for n in range(4):
                        bias_turn(dve, t, n, t == 0)
                    softmax(dve, t)
                with dve.Fori(0, PAIRS - 2) as u:
                    for n in range(2):
                        bias_turn(dve, u + 2, n, False)
                    attn_out(dve, u)
                    for n in range(2, 4):
                        bias_turn(dve, u + 2, n, False)
                    softmax(dve, u + 2)
                attn_out(dve, PAIRS - 2)
                attn_out(dve, PAIRS - 1)
    sm.close()


LAT = S
KEYS = CTX + LAT
EPS_RMS = 1e-8


def l1_prepare_stage(nc, m):
    ps = m.ps
    shift_made, shift_copied = m.sem("l1_shift_made"), m.sem("l1_shift_copied")
    q_made, squared, powered = m.sem("l1_q_made"), m.sem("l1_q_squared"), m.sem("l1_q_norms")
    own, ss_ready, q_ready = m.sem("l1_prep_dve_steps"), m.sem("l1_q_squares_summed"), m.sem("l1_q_normed")
    q_turned, qbd_zeroed = m.sem("l1_q_turned"), m.sem("l1_qbd_zeroed")
    with ExitStack() as ctx:
        sb = m.scoped(ctx, "l1p")
        sq, qn = sb("sq", [P, PAIRS, D]), sb("qn", [P, PAIRS, D])
        ss, nrm, gain = sb("ss", [P, 16]), sb("nrm", [P, 16]), sb("gain", [P, D])
        with nc.Block() as block:
            @block.tensor
            def _(pe):
                nc.tensor.matmul(ps[0:1, 0, 0:2 * P], m.ln_x_b[:], m.wkv1[:], start=True, stop=True
                                 ).then_inc(shift_made, 1)
                for t in range(PAIRS):
                    ins = nc.tensor.matmul(ps[:, 2 + t // 4, (t % 4) * P:(t % 4 + 1) * P], m.xT[:, t * P:(t + 1) * P],
                                           m.wq1[:], start=True, stop=True)
                ins.then_inc(q_made, 1)
                pe.wait_ge(q_ready, 1)
                for t in range(PAIRS):
                    ins = nc.tensor.transpose(ps[:, 4 + t // 4, (t % 4) * P:(t % 4 + 1) * P], qn[:, t, :], m.ident[:])
                ins.then_inc(q_turned, 1)

            @block.scalar
            def _(act):
                act.wait_ge(shift_made, 1)
                nc.scalar.copy(m.WA[DC:DC + 1, :], ps[0:1, 0, 0:2 * P]).then_inc(shift_copied, 1)
                act.wait_ge(q_made, 1)
                nc.scalar.activation(sq[:], ps[:, 2:4, :].rearrange("p b (t d) -> p (b t) d", d=D), ACT.Square
                                     ).then_inc(squared, 1)
                act.wait_ge(shift_copied, 1)

            @block.gpsimd
            def _(pool):
                nc.gpsimd.memset(m.qbd1[:], 0.0).then_inc(qbd_zeroed, 1)
                pool.wait_ge(ss_ready, 1)
                nc.gpsimd.tensor_tensor(nrm[:], ss[:], m.half[:, 0:16], ALU.pow).then_inc(powered, 1)

            @block.vector
            def _(dve):
                chain, V = Chain(dve, own), nc.vector
                chain.mark(V.tensor_scalar(m.WA[0:DC, :], m.wkv1[:], m.ln_x_g[:], None, ALU.mult))
                chain.link(V.tensor_tensor(gain[:], m.qn_g[:], m.kn_g[:], ALU.mult))
                chain.link(V.tensor_scalar(gain[:], gain[:], float(64) ** -0.5 * 2 * float(64) ** 0.5, None,
                                           ALU.mult))
                dve.wait_ge(squared, 1)
                V.tensor_reduce(ss[:], sq[:].rearrange("p t (h d) -> p (t h) d", d=64), axis=AX.X, op=ALU.add
                                ).then_inc(ss_ready, 1)
                dve.wait_ge(powered, 1)
                chain.link(V.tensor_scalar(nrm[:], nrm[:], float(64) ** -0.5, EPS_RMS, ALU.mult, ALU.max))
                chain.link(V.reciprocal(nrm[:], nrm[:]))
                chain.link(V.tensor_tensor(qn[:].rearrange("p t (h d) -> p (t h) d", d=64),
                                           ps[:, 2:4, :].rearrange("p b (t d) -> p (b t) d", d=64),
                                           nrm[:].unsqueeze(2).broadcast_to([P, 16, 64]), ALU.mult))
                V.tensor_tensor(qn[:], qn[:], gain[:].unsqueeze(1).broadcast_to([P, PAIRS, D]), ALU.mult
                                ).then_inc(q_ready, 1)
                dve.wait_ge(q_turned, 1)
                dve.wait_ge(qbd_zeroed, 1)
                for h in range(2):
                    rows = slice(64 * h, 64 * h + 64)
                    chain.mark(V.tensor_copy(m.qbd1[rows, :, h, :],
                                             ps[rows, 4:6, :].rearrange("p c (b i) -> p (c b) i", i=S)))
                chain.settle()


def l1_cross_stage(nc, m, dram):
    ps = m.ps
    TILES = KT * P
    loaded = [m.sem("l1_ctx_loaded_even"), m.sem("l1_ctx_loaded_odd")]
    mask_loaded, mask_ready = m.sem("l1_mask_loaded"), m.sem("l1_mask_ready")
    sums, means = m.sem("l1_row_sums"), m.sem("l1_means")
    centered, squared = m.sem("l1_centered"), m.sem("l1_centered_squared")
    sqsums, variances, rstd_ready = m.sem("l1_square_sums"), m.sem("l1_variances"), m.sem("l1_rstd_ready")
    xh_ready = m.sem("l1_context_normed")
    xh_turned, xhT_ready = m.sem("l1_context_turned"), m.sem("l1_contextT_ready")
    staged = m.sem("l1_pair_staged")
    k_made, k_squared, kss_ready, knorm_ready = (m.sem(n) for n in (
        "l1_keys_made", "l1_keys_squared", "l1_key_squares_summed", "l1_key_norms"))
    rk_steps, kn_ready = m.sem("l1_key_scale_steps"), m.sem("l1_keys_normed")
    vlat_ready = m.sem("l1_latent_values_ready")
    kn_turned, knT_ready = m.sem("l1_keys_turned"), m.sem("l1_keysT_ready")
    scores_ready, mx_steps, exps_ready = m.sem("l1_scores_ready"), m.sem("l1_max_steps"), m.sem("l1_exps_ready")
    recip_ready = m.sem("l1_recip_ready")
    p_turned, pT_even_ready, pT_front_ready, pT_back_ready = (m.sem("l1_" + n) for n in (
        "probs_turned", "probsT_even_ready", "probsT_odd_front_ready", "probsT_odd_back_ready"))
    oT_made, oT_copied, o_made, o_copied = (m.sem("l1_" + n) for n in (
        "oT_made", "oT_copied", "o_made", "o_copied"))
    a_turned, aT_copied, y_made, x_updated = (m.sem("l1_" + n) for n in (
        "attn_turned", "attnT_copied", "y_made", "x_updated"))
    set_once = m.sem("l1_buffers_set")
    with ExitStack() as ctx:
        sb = m.scoped(ctx, "l1")
        mask_u8, mask_bf = sb("mask_u8", [BATCHES, CTX], U8), sb("mask_bf", [P, KEYS], BF16)
        pick = sb("pick", [P, BATCHES, P], BF16)
        xh = sb("xh", [P, 4, KT, DC + 1])
        sq, stat = sb("sq", [P, 2, KT, DC]), sb("stat", [P, 2, 4, KT])
        lat, qs = sb("lat", [P, P]), sb("qs", [P, 2, P])
        kss, knorm, krec = (sb(n, [P, 2, KT + 1, 2]) for n in ("kss", "knorm", "krec"))
        vlat = sb("vlat", [S, 2, P])
        ksq = sb("ksq_probs", [P, 2, KT + 1, P])
        kn = sb("kn_probsT", [P, 2, KT + 1, P])
        turned = sb("contextT_keysT", [P, 2, KEYS])
        probs = ksq[:].rearrange("p b k d -> p b (k d)")
        pT = kn
        negm, total, recip, mxp = (sb(n, [P, 2]) for n in ("negm", "total", "recip", "mxp"))
        oT, attn, attnT = sb("oT", [DC + 1, 2, P]), sb("attn", [P, P]), sb("attnT", [P, P])

        def group(b):
            return ps[:, 4 * b:4 * b + 4, :].rearrange("p c n -> p (c n)")

        def half_tiles(h):
            return (0, 8) if h == 0 else (8, KT)

        with nc.Block() as block:
            @block.sync
            def _(sp):
                def load(b, j):
                    jj = bass.ds(j, 1)
                    sp.dma_start(m.ctx_nat[:, b, 0:FULL, 0:DC],
                                 dram["ctx"][jj, 0:FULL * P, :].rearrange("o (k p) d -> (o p) k d", p=P)
                                 ).then_inc(loaded[b], 16)
                    sp.dma_start(m.ctx_nat[0:REST, b, FULL, 0:DC],
                                 dram["ctx"][jj, FULL * P:CTX, :].rearrange("o p d -> (o p) d")
                                 ).then_inc(loaded[b], 16)
                load(0, 0)
                load(1, 1)
                sp.dma_start(mask_u8[:], dram["mask"]).then_inc(mask_loaded, 16)
                with sp.Fori(0, PAIRS - 1) as t:
                    for b in range(2):
                        sp.wait_ge(centered, 2 * t + b + 1)
                        load(b, 2 * t + 2 + b)

            @block.gpsimd
            def _(pool):
                nc.gpsimd.memset(xh[:, :, :, DC:DC + 1], 1.0).then_inc(set_once, 1)
                nc.gpsimd.memset(mask_bf[:], 0.0).then_inc(set_once, 1)
                nc.gpsimd.memset(kss[:], 1.0).then_inc(set_once, 1)
                pool.wait_ge(set_once, 3)

                def center(b, q, j):
                    pool.wait_ge(means, j + 1)
                    nc.gpsimd.tensor_tensor(xh[:, 2 * q + b, :, 0:DC], m.ctx_nat[:, b, :, 0:DC],
                                            stat[:, b, 1, :].unsqueeze(2).broadcast_to([P, KT, DC]), ALU.subtract
                                            ).then_inc(centered, 1)

                def scale(b, q, j):
                    pool.wait_ge(variances, j + 1)
                    nc.gpsimd.tensor_tensor(stat[:, b, 3, :], stat[:, b, 2, :], m.nhalf[:, 0:KT], ALU.pow
                                            ).then_inc(rstd_ready, 1)
                    pool.wait_ge(rstd_ready, j + 1)
                    nc.gpsimd.tensor_tensor(xh[:, 2 * q + b, :, 0:DC], xh[:, 2 * q + b, :, 0:DC],
                                            stat[:, b, 3, :].unsqueeze(2).broadcast_to([P, KT, DC]), ALU.mult
                                            ).then_inc(xh_ready, 1)

                def pool_pair(t, q):
                    for b in range(2):
                        center(b, 1 - q, 2 * t + 2 + b)
                    for b in range(2):
                        scale(b, 1 - q, 2 * t + 2 + b)
                for b in range(2):
                    center(b, 0, b)
                for b in range(2):
                    scale(b, 0, b)
                with pool.Fori(0, PAIRS // 2 - 1) as u:
                    for q in range(2):
                        pool_pair(2 * u + q, q)
                pool_pair(PAIRS - 2, 0)

            def turn_context(pe, b, q, j):
                pe.wait_ge(xh_ready, j + 1)
                pe.sem_inc(m.turns_pe, 1)
                for k in range(KT):
                    ins = nc.tensor.transpose(ps[0:DC + 1, 4 * b + k // 4, (k % 4) * P:(k % 4 + 1) * P],
                                              xh[:, 2 * q + b, k, :], m.ident[:])
                    if k % 4 == 3 or k == KT - 1:
                        ins.then_inc(xh_turned, 1)

            def keys(pe, b, j):
                for k in range(KT):
                    if k % 4 == 0:
                        pe.wait_ge(xhT_ready, 4 * j + k // 4 + 1)
                    ins = nc.tensor.matmul(ps[:, 4 * b + k // 4, (k % 4) * P:(k % 4 + 1) * P],
                                           turned[0:DC + 1, b, k * P:(k + 1) * P], m.WA[:, 0:P],
                                           start=True, stop=True)
                    if k == 7:
                        ins.then_inc(k_made, 1)
                nc.tensor.matmul(ps[0:S, 4 * b + 3, P:3 * P], lat[:, b * S:(b + 1) * S], m.wlkv1[:],
                                 start=True, stop=True).then_inc(k_made, 1)

            def turn_keys(pe, b, j):
                for k in range(KT):
                    if k in (0, 8):
                        pe.wait_ge(kn_ready, 3 * j + (1 if k == 0 else 3))
                        pe.sem_inc(m.turns_pe, 1)
                    r = rows_of(k)
                    ins = nc.tensor.transpose(ps[:, 4 * b + k // 4, (k % 4) * P:(k % 4) * P + r], kn[0:r, b, k, :],
                                              m.ident[0:r, 0:r])
                    if k % 4 == 3:
                        ins.then_inc(kn_turned, 1)
                nc.tensor.transpose(ps[:, 4 * b + 3, REST:REST + LAT], kn[0:LAT, b, KT, :], m.ident[0:LAT, 0:LAT]
                                    ).then_inc(kn_turned, 1)

            def scores(pe, b, j):
                for c in range(4):
                    n = min(BANK, KEYS - c * BANK)
                    pe.wait_ge(knT_ready, 4 * j + c + 1)
                    nc.tensor.matmul(ps[:, 4 * b + c, 0:n], pick[:, bass.ds(j, 1), :].rearrange("p o q -> p (o q)"),
                                     mask_bf[:, c * BANK:c * BANK + n], start=True, stop=False)
                    ins = nc.tensor.matmul(ps[:, 4 * b + c, 0:n], qs[:, b, :], turned[:, b, c * BANK:c * BANK + n],
                                           start=False, stop=True)
                ins.then_inc(scores_ready, 1)

            def turn_probs(pe, b, j):
                pe.wait_ge(exps_ready, j + 1)
                pe.sem_inc(m.turns_pe, 1)
                for k in range(KT):
                    r = rows_of(k)
                    ins = nc.tensor.transpose(ps[0:r, 4 * b + k // 4, (k % 4) * P:(k % 4 + 1) * P],
                                              probs[:, b, k * P:k * P + r], m.ident[:])
                    if k % 4 == 3:
                        ins.then_inc(p_turned, 1)
                nc.tensor.transpose(ps[0:LAT, 4 * b + 3, P:2 * P], probs[:, b, CTX:KEYS], m.ident[:]
                                    ).then_inc(p_turned, 1)

            def output(pe, b, q, t):
                for k in range(KT):
                    if k in (0, 4, 8) and b == 0:
                        pe.wait_ge(pT_even_ready, 5 * t + (1, 2, 5)[k // 4])
                    elif k in (0, 4):
                        pe.wait_ge(pT_front_ready, 2 * t + k // 4 + 1)
                    elif k == 8:
                        pe.wait_ge(pT_back_ready, 3 * t + 3)
                    r = rows_of(k)
                    ins = nc.tensor.matmul(ps[0:DC + 1, 4 * b, 0:P], xh[0:r, 2 * q + b, k, :], pT[0:r, b, k, :],
                                           start=(k == 0), stop=(k == KT - 1))
                ins.then_inc(oT_made, 1)

            def values(pe, b, j):
                nc.tensor.matmul(ps[:, 4 * b + 1, 0:P], pT[0:LAT, b, KT, :], vlat[:, b, :], start=True, stop=False)
                pe.wait_ge(oT_copied, j + 1)
                nc.tensor.matmul(ps[:, 4 * b + 1, 0:P], oT[:, b, :], m.WA[:, P:2 * P], start=False, stop=True
                                 ).then_inc(o_made, 1)

            def pe_pair(pe, t, q):
                turn_context(pe, 0, q, 2 * t)
                pe.wait_ge(x_updated, t + 1)
                turn_context(pe, 1, q, 2 * t + 1)
                pe.wait_ge(staged, 3 * t + 3)
                for b in range(2):
                    keys(pe, b, 2 * t + b)
                for b in range(2):
                    turn_keys(pe, b, 2 * t + b)
                    scores(pe, b, 2 * t + b)
                turn_probs(pe, 0, 2 * t)
                output(pe, 0, q, t)
                turn_probs(pe, 1, 2 * t + 1)
                values(pe, 0, 2 * t)
                output(pe, 1, q, t)
                values(pe, 1, 2 * t + 1)
                pe.wait_ge(o_copied, 4 * t + 4)
                pe.sem_inc(m.turns_pe, 1)
                nc.tensor.transpose(ps[:, 0, 0:P], attn[:], m.ident[:]).then_inc(a_turned, 1)
                pe.wait_ge(aT_copied, t + 1)
                nc.tensor.matmul(ps[:, 4, 0:D], attnT[:], m.wo1[:], start=True, stop=False)
                nc.tensor.matmul(ps[:, 4, 0:D], m.ones[0:1, 0:P], m.bo1[:], start=False, stop=True
                                 ).then_inc(y_made, 1)

            @block.tensor
            def _(pe):
                pe.wait_ge(set_once, 3)
                pe.wait_ge(mask_ready, 2)
                with pe.Fori(0, PAIRS // 2) as u:
                    for q in range(2):
                        pe_pair(pe, 2 * u + q, q)

            def square_context(act, b, q, j):
                act.wait_ge(centered, j + 1)
                nc.scalar.activation(sq[:, b], xh[:, 2 * q + b, :, 0:DC], ACT.Square).then_inc(squared, 1)

            def act_pair(act, t, q, last):
                for b in range(2):
                    for c in range(4):
                        n = min(BANK, TILES - c * BANK)
                        act.wait_ge(xh_turned, 4 * (2 * t + b) + c + 1)
                        nc.scalar.copy(turned[0:DC + 1, b, c * BANK:c * BANK + n], ps[0:DC + 1, 4 * b + c, 0:n]
                                       ).then_inc(xhT_ready, 1)
                for b in range(2):
                    j = 2 * t + b
                    for h in range(2):
                        lo, hi = half_tiles(h)
                        act.wait_ge(k_made, 2 * j + h + 1)
                        nc.scalar.activation(ksq[:, b, lo:hi, :],
                                             group(b)[:, lo * P:hi * P].rearrange("p (k d) -> p k d", d=P),
                                             ACT.Square).then_inc(k_squared, 1)
                    nc.scalar.activation(ksq[0:S, b, KT, :], ps[0:S, 4 * b + 3, P:2 * P], ACT.Square
                                         ).then_inc(k_squared, 1)
                    nc.scalar.copy(vlat[:, b, :], ps[0:S, 4 * b + 3, 2 * P:3 * P]).then_inc(vlat_ready, 1)
                    act.wait_ge(kss_ready, 4 * j + 4)
                    nc.scalar.activation(knorm[:, b], kss[:, b], ACT.Sqrt).then_inc(knorm_ready, 1)

                def copy_keys(b):
                    for c in range(4):
                        n = min(BANK, KEYS - c * BANK)
                        act.wait_ge(kn_turned, 4 * (2 * t + b) + c + 1)
                        nc.scalar.copy(turned[:, b, c * BANK:c * BANK + n], ps[:, 4 * b + c, 0:n]
                                       ).then_inc(knT_ready, 1)

                def exp(b):
                    act.wait_ge(mx_steps, 2 * (2 * t + b) + 2)
                    nc.scalar.activation(probs[:, b, 0:KEYS], group(b)[:, 0:KEYS], ACT.Exp,
                                         bias=negm[:, b:b + 1], accum_out=total[:, b:b + 1]).then_inc(exps_ready, 1)

                def copy_probs(b, first, ready):
                    for c in range(first, 3):
                        act.wait_ge(p_turned, 4 * (2 * t + b) + c + 1)
                        nc.scalar.copy(pT[:, b, 4 * c:4 * c + 4, :],
                                       ps[:, 4 * b + c, :].rearrange("p (k q) -> p k q", q=P)).then_inc(ready, 1)
                    act.wait_ge(p_turned, 4 * (2 * t + b) + 4)
                    nc.scalar.copy(pT[0:REST, b, FULL, :], ps[0:REST, 4 * b + 3, 0:P]).then_inc(ready, 1)
                    nc.scalar.copy(pT[0:LAT, b, KT, :], ps[0:LAT, 4 * b + 3, P:2 * P]).then_inc(ready, 1)
                copy_keys(0)
                if not last:
                    for b in range(2):
                        square_context(act, b, 1 - q, 2 * t + 2 + b)
                copy_keys(1)
                exp(0)
                copy_probs(0, 0, pT_even_ready)
                exp(1)
                act.wait_ge(oT_made, 2 * t + 1)
                nc.scalar.copy(oT[:, 0, :], ps[0:DC + 1, 0, 0:P]).then_inc(oT_copied, 1)
                copy_probs(1, 2, pT_back_ready)
                act.wait_ge(oT_made, 2 * t + 2)
                nc.scalar.copy(oT[:, 1, :], ps[0:DC + 1, 4, 0:P]).then_inc(oT_copied, 1)
                act.wait_ge(a_turned, t + 1)
                nc.scalar.copy(attnT[:], ps[:, 0, 0:P]).then_inc(aT_copied, 1)

            @block.scalar
            def _(act):
                for b in range(2):
                    square_context(act, b, 0, b)
                with act.Fori(0, PAIRS // 2 - 1) as u:
                    for q in range(2):
                        act_pair(act, 2 * u + q, q, False)
                act_pair(act, PAIRS - 2, 0, False)
                act_pair(act, PAIRS - 1, 1, True)

            def mean(dve, b, j, t_load):
                dve.wait_ge(loaded[b], 32 * t_load)
                nc.vector.tensor_reduce(stat[:, b, 0, :], m.ctx_nat[:, b, :, 0:DC], axis=AX.X, op=ALU.add
                                        ).then_inc(sums, 1)
                dve.wait_ge(sums, j + 1)
                nc.vector.tensor_scalar(stat[:, b, 1, :], stat[:, b, 0, :], 1.0 / DC, None, ALU.mult
                                        ).then_inc(means, 1)

            def variance(dve, b, j):
                dve.wait_ge(squared, j + 1)
                nc.vector.tensor_reduce(stat[:, b, 2, :], sq[:, b], axis=AX.X, op=ALU.add).then_inc(sqsums, 1)
                dve.wait_ge(sqsums, j + 1)
                nc.vector.tensor_scalar(stat[:, b, 2, :], stat[:, b, 2, :], 1.0 / DC, 1e-5, ALU.mult, ALU.add
                                        ).then_inc(variances, 1)

            def dve_pair(dve, t, q, last):
                V = nc.vector
                V.tensor_copy(lat[:], m.xT[:, bass.ds(t * P, P)]).then_inc(staged, 1)
                for b in range(2):
                    V.tensor_copy(qs[:, b, :], m.qbd1[:, bass.ds(2 * t + b, 1), :, :].rearrange(
                        "p o h i -> p (o h i)")).then_inc(staged, 1)
                if not last:
                    for b in range(2):
                        mean(dve, b, 2 * t + 2 + b, t + 2)
                for b in range(2):
                    j = 2 * t + b
                    for h in range(2):
                        lo, hi = half_tiles(h)
                        dve.wait_ge(k_squared, 3 * j + h + 1)
                        V.tensor_reduce(kss[:, b, lo:hi, :].rearrange("p k h -> p (k h)"),
                                        ksq[:, b, lo:hi, :].rearrange("p k (h d) -> p (k h) d", d=64), axis=AX.X,
                                        op=ALU.add).then_inc(kss_ready, 1)
                    dve.wait_ge(k_squared, 3 * j + 3)
                    V.tensor_reduce(kss[0:S, b, KT, :], ksq[0:S, b, KT, :].rearrange("p (h d) -> p h d", d=64),
                                    axis=AX.X, op=ALU.add).then_inc(kss_ready, 1)
                    dve.wait_ge(kss_ready, 4 * j + 3)
                    V.tensor_scalar(kss[:, b], kss[:, b], 64 * EPS_RMS ** 2, None, ALU.max).then_inc(kss_ready, 1)
                    dve.wait_ge(knorm_ready, j + 1)
                    V.reciprocal(krec[:, b], knorm[:, b]).then_inc(rk_steps, 1)
                    dve.wait_ge(rk_steps, 4 * j + 1)
                    V.tensor_tensor(krec[:, b], krec[:, b], kss[:, b], ALU.mult).then_inc(rk_steps, 1)
                    dve.wait_ge(rk_steps, 4 * j + 2)
                    V.tensor_tensor(krec[:, b], krec[:, b], knorm[:, b], ALU.add).then_inc(rk_steps, 1)
                    dve.wait_ge(rk_steps, 4 * j + 3)
                    V.reciprocal(krec[:, b], krec[:, b]).then_inc(rk_steps, 1)
                    dve.wait_ge(rk_steps, 4 * j + 4)
                    dve.wait_ge(vlat_ready, j + 1)
                    for h in range(2):
                        lo, hi = half_tiles(h)
                        V.tensor_tensor(
                            kn[:, b, lo:hi, :].rearrange("p k (h d) -> p (k h) d", d=64),
                            group(b)[:, lo * P:hi * P].rearrange("p (k d) -> p k d", d=64),
                            krec[:, b, lo:hi, :].rearrange("p k h -> p (k h)").unsqueeze(2).broadcast_to(
                                [P, 2 * (hi - lo), 64]), ALU.mult).then_inc(kn_ready, 1)
                    V.tensor_tensor(kn[0:S, b, KT, :].rearrange("p (h d) -> p h d", d=64),
                                    ps[0:S, 4 * b + 3, P:2 * P].rearrange("p (h d) -> p h d", d=64),
                                    krec[0:S, b, KT, :].unsqueeze(2).broadcast_to([S, 2, 64]), ALU.mult
                                    ).then_inc(kn_ready, 1)

                def less_max(b):
                    dve.wait_ge(scores_ready, 2 * t + b + 1)
                    V.tensor_reduce(mxp[:, b:b + 1], group(b)[:, 0:KEYS], axis=AX.X, op=ALU.max
                                    ).then_inc(mx_steps, 1)
                    dve.wait_ge(mx_steps, 2 * (2 * t + b) + 1)
                    V.tensor_scalar(negm[:, b:b + 1], mxp[:, b:b + 1], -1.0, None, ALU.mult).then_inc(mx_steps, 1)
                less_max(0)
                if not last:
                    for b in range(2):
                        variance(dve, b, 2 * t + 2 + b)
                less_max(1)
                for b in range(2):
                    dve.wait_ge(exps_ready, 2 * t + b + 1)
                    V.reciprocal(recip[:, b:b + 1], total[:, b:b + 1]).then_inc(recip_ready, 1)
                for c in range(2):
                    dve.wait_ge(p_turned, 4 * (2 * t + 1) + c + 1)
                    V.tensor_copy(pT[:, 1, 4 * c:4 * c + 4, :], ps[:, 4 + c, :].rearrange("p (k q) -> p k q", q=P)
                                  ).then_inc(pT_front_ready, 1)
                dve.wait_ge(recip_ready, 2 * t + 2)
                for b in range(2):
                    dve.wait_ge(o_made, 2 * t + b + 1)
                    for h in range(2):
                        rows = slice(64 * h, 64 * h + 64)
                        V.tensor_scalar(attn[S * b:S * b + S, 64 * h:64 * h + 64],
                                        ps[rows, 4 * b + 1, 64 * h:64 * h + 64], recip[rows, b:b + 1], None, ALU.mult
                                        ).then_inc(o_copied, 1)
                dve.wait_ge(y_made, t + 1)
                xt = m.X[:, bass.ds(t, 1), :].rearrange("p o d -> p (o d)")
                V.tensor_tensor(xt, xt, ps[:, 4, 0:D], ALU.add).then_inc(x_updated, 1)

            @block.vector
            def _(dve):
                dve.sem_inc(x_updated, 1)
                dve.wait_ge(set_once, 3)
                dve.wait_ge(mask_loaded, 16)
                nc.vector.tensor_scalar(mask_bf[0:BATCHES, 0:CTX], mask_u8[:], -NEG, NEG, ALU.mult, ALU.add
                                        ).then_inc(mask_ready, 1)
                nc.vector.tensor_copy(pick[:], m.ident[:, 0:BATCHES].unsqueeze(2).broadcast_to([P, BATCHES, P])
                                      ).then_inc(mask_ready, 1)
                for b in range(2):
                    mean(dve, b, b, 1)
                for b in range(2):
                    variance(dve, b, b)
                with dve.Fori(0, PAIRS // 2 - 1) as u:
                    for q in range(2):
                        dve_pair(dve, 2 * u + q, q, False)
                dve_pair(dve, PAIRS - 2, 0, False)
                dve_pair(dve, PAIRS - 1, 1, True)


def router_stage(nc, m, name, E, top, wr, br, b2, soft, extra):
    ps = m.ps
    made, exps_ready, own, less_ready, gates_ready, turned, gT_ready, b_made = (m.tally("router_" + n) for n in (
        "logits_made", "exps_ready", "dve_steps", "less_ready", "gates_ready", "gates_turned", "gT_ready",
        "bias_made"))
    with ExitStack() as ctx:
        sb = m.scoped(ctx, name)
        a, w_, sel, eq = (sb(n, [P, PAIRS, E]) for n in ("a", "work", "sel", "eq"))
        one = sb("one", [P, PAIRS])
        tot = sb("tot", [P, PAIRS])
        gT = sb("gT", [E + 1, ROWS])
        def over(t):
            return t[:].unsqueeze(2).broadcast_to([P, PAIRS, E])
        with nc.Block() as block:
            @block.tensor
            def _(pe):
                for t in range(PAIRS):
                    out = ps[:, 0, 32 * t:32 * t + E]
                    ins = nc.tensor.matmul(out, m.xT[:, t * P:(t + 1) * P], wr[:], start=True, stop=br is None)
                    if br is not None:
                        ins = nc.tensor.matmul(out, m.ones[0:1, 0:P], br[:], start=False, stop=True)
                ins.then_inc(made.sem, 1)
                gates_ready.wait(pe, 1)
                for t in range(PAIRS):
                    ins = nc.tensor.transpose(ps[0:E + 1, 2 + t // 4, (t % 4) * P:(t % 4 + 1) * P],
                                              m.gates[:, t, 0:E + 1], m.ident[:])
                ins.then_inc(turned.sem, 1)
                gT_ready.wait(pe, 1)
                for t in range(PAIRS):
                    ins = nc.tensor.matmul(ps[:, 4 + t // 4, (t % 4) * P:(t % 4 + 1) * P], gT[:, t * P:(t + 1) * P],
                                           b2[:], start=True, stop=True)
                ins.then_inc(b_made.sem, 1)

            @block.scalar
            def _(act):
                less_ready.wait(act, 1)
                nc.scalar.activation(a[:], w_[:], ACT.Exp, scale=1.0 if soft else -1.0).then_inc(exps_ready.sem, 1)
                turned.wait(act, 1)
                nc.scalar.copy(gT[:], ps[0:E + 1, 2:4, :].rearrange("p b n -> p (b n)")).then_inc(gT_ready.sem, 1)
                gT_ready.wait(act, 1)

            @block.vector
            def _(dve):
                chain = Chain(dve, own.sem, own.base)
                logits = ps[:, 0, 0:32 * PAIRS].rearrange("p (t e) -> p t e", e=32)[:, :, 0:E]
                V = nc.vector
                made.wait(dve, 1)
                if soft:
                    chain.link(V.tensor_reduce(one[:], logits, axis=AX.X, op=ALU.max))
                    V.tensor_tensor(w_[:], logits, over(one), ALU.subtract).then_inc(less_ready.sem, 1)
                    exps_ready.wait(dve, 1)
                    chain.link(V.tensor_reduce(one[:], a[:], axis=AX.X, op=ALU.add))
                    chain.link(V.reciprocal(tot[:], one[:]))
                    chain.link(V.tensor_tensor(a[:], a[:], over(tot), ALU.mult))
                else:
                    V.tensor_copy(w_[:], logits).then_inc(less_ready.sem, 1)
                    exps_ready.wait(dve, 1)
                    chain.link(V.tensor_scalar(a[:], a[:], 1.0, None, ALU.add))
                    chain.link(V.reciprocal(a[:], a[:]))
                chain.link(V.tensor_copy(w_[:], a[:]))
                chain.link(V.memset(m.gates[:, :, 0:E], 0.0))
                chain.link(V.memset(m.gates[:, :, E:E + 1], 1.0))
                gates = m.gates[:, :, 0:E]
                for i in range(top):
                    chain.link(V.tensor_reduce(one[:], w_[:], axis=AX.X, op=ALU.max))
                    chain.link(V.tensor_tensor(eq[:], w_[:], over(one), ALU.is_equal))
                    chain.link(V.tensor_tensor(eq[:], eq[:], m.down[:, 32 - E:32].unsqueeze(1).broadcast_to(
                        [P, PAIRS, E]), ALU.mult))
                    chain.link(V.tensor_reduce(one[:], eq[:], axis=AX.X, op=ALU.max))
                    chain.link(V.tensor_tensor(sel[:], eq[:], over(one), ALU.is_equal))
                    chain.link(V.scalar_tensor_tensor(out=w_[:], in0=sel[:], scalar=-4.0, in1=w_[:], op0=ALU.mult,
                                                      op1=ALU.add))
                    chain.link(V.tensor_tensor(sel[:], sel[:], a[:], ALU.mult))
                    chain.link(V.tensor_tensor(gates, gates, sel[:], ALU.add))
                if not soft:
                    chain.link(V.tensor_reduce(one[:], gates, axis=AX.X, op=ALU.add))
                    chain.link(V.tensor_scalar(one[:], one[:], 1e-6, None, ALU.add))
                    chain.link(V.reciprocal(tot[:], one[:]))
                    chain.link(V.tensor_tensor(gates, gates, over(tot), ALU.mult))
                V.tensor_copy(one[:, 0:1], m.gates[:, 0, 0:1]).then_inc(gates_ready.sem, 1)
                for e in extra:
                    chain.link(V.tensor_tensor(m.X[:], m.X[:], e[:], ALU.add))
                b_made.wait(dve, 1)
                chain.link(V.tensor_tensor(m.X[:], m.X[:], ps[:, 4:6, :].rearrange("p b (t d) -> p (b t) d", d=D),
                                           ALU.add))
                own.close(chain.n)
    for tally in (made, exps_ready, less_ready, gates_ready, turned, gT_ready, b_made):
        tally.close(1)


def experts_stage(nc, m, name, n_experts, chunks, func, unroll, w1, w2, b1):
    ps = m.ps
    loaded = [m.sem(f"{name}_weights_loaded_{i}") for i in range(unroll)]
    up_made, h_ready = m.sem(name + "_up_made"), m.sem(name + "_hidden_ready")
    down_made, gated = m.sem(name + "_down_made"), m.sem(name + "_gated")
    gate_staged = m.sem(name + "_gate_staged")
    turns = n_experts // unroll
    assert turns * unroll == n_experts
    even = unroll % 2 == 0
    with ExitStack() as ctx:
        sb = m.scoped(ctx, name)
        W1, W2 = sb("w1", [P, unroll, chunks * P]), sb("w2", [P, unroll, chunks, D])
        B1 = sb("b1", [P, unroll, chunks])
        hid = sb("hid", [P, 2, chunks, ROWS])
        gate = sb("gate", [P, 2, PAIRS])
        with nc.Block() as block:
            @block.sync
            def _(sp):
                def load(i, e):
                    ee = bass.ds(e, 1)
                    sp.dma_start(W1[:, i, :], w1[ee].rearrange("o p h -> (o p) h")).then_inc(loaded[i], 16)
                    sp.dma_start(W2[:, i], w2[ee].rearrange("o (c p) d -> p (o c) d", p=P)).then_inc(loaded[i], 16)
                    sp.dma_start(B1[:, i, :], b1[ee].rearrange("o p c -> (o p) c")).then_inc(loaded[i], 16)
                for i in range(unroll):
                    load(i, i)
                with sp.Fori(1, turns) as t:
                    for i in range(unroll):
                        sp.wait_ge(down_made, 2 + (t - 1) * unroll + i + 1)
                        load(i, t * unroll + i)

            @block.tensor
            def _(pe):
                pe.sem_inc(down_made, 2)

                def up(i, e, t):
                    pe.wait_ge(loaded[i], 48 * (t + 1))
                    for c in range(chunks):
                        pe.wait_ge(h_ready, 2 + chunks * e + c - 1)
                        for half in range(2):
                            ins = nc.tensor.matmul(ps[:, 2 * (((i * chunks) + c) % 2) + half, :],
                                                   W1[:, i, c * P:(c + 1) * P],
                                                   m.xT[:, half * BANK:(half + 1) * BANK], start=True, stop=True)
                        ins.then_inc(up_made, 1)

                def down(i, e):
                    pe.wait_ge(gated, 2 + PAIRS + PAIRS * ((e - 1) if (even or i) else e))
                    for tile in range(PAIRS):
                        for c in range(chunks):
                            if tile == 0:
                                pe.wait_ge(h_ready, 2 + chunks * e + c + 1)
                            ins = nc.tensor.matmul(ps[:, 4 + 2 * (i % 2) + tile // 4, (tile % 4) * P:(tile % 4 + 1) * P],
                                                   hid[:, i % 2, c, tile * P:(tile + 1) * P], W2[:, i, c, :],
                                                   start=(c == 0), stop=(c == chunks - 1))
                    ins.then_inc(down_made, 1)

                with pe.Fori(0, turns) as t:
                    up(0, t * unroll, t)
                    for i in range(1, unroll):
                        up(i, t * unroll + i, t)
                        down(i - 1, t * unroll + i - 1)
                    down(unroll - 1, t * unroll + unroll - 1)

            @block.scalar
            def _(act):
                act.sem_inc(h_ready, 2)
                with act.Fori(0, turns) as t:
                    for i in range(unroll):
                        e = t * unroll + i
                        for c in range(chunks):
                            act.wait_ge(up_made, chunks * e + c + 1)
                            act.wait_ge(down_made, 2 + ((e - 1) if (even or i) else e))
                            nc.scalar.activation(hid[:, i % 2, c, :],
                                                 ps[:, 2 * (((i * chunks) + c) % 2):2 * (((i * chunks) + c) % 2) + 2, :]
                                                 .rearrange("p b n -> p (b n)"), func, bias=B1[:, i, c:c + 1]
                                                 ).then_inc(h_ready, 1)

            @block.vector
            def _(dve):
                dve.sem_inc(gated, 2 + PAIRS)
                with dve.Fori(0, turns) as t:
                    for i in range(unroll):
                        e = t * unroll + i
                        dve.wait_ge(gated, 2 + PAIRS + PAIRS * e)
                        nc.vector.tensor_copy(gate[:, i % 2, :], m.gates[:, :, bass.ds(e, 1)].rearrange(
                            "p t o -> p (t o)")).then_inc(gate_staged, 1)
                        dve.wait_ge(gate_staged, e + 1)
                        dve.wait_ge(down_made, 2 + e + 1)
                        for tile in range(PAIRS):
                            nc.vector.scalar_tensor_tensor(
                                out=m.X[:, tile, :],
                                in0=ps[:, 4 + 2 * (i % 2) + tile // 4, (tile % 4) * P:(tile % 4 + 1) * P],
                                scalar=gate[:, i % 2, tile:tile + 1], in1=m.X[:, tile, :], op0=ALU.mult, op1=ALU.add
                                ).then_inc(gated, 1)
                dve.wait_ge(gated, 2 + PAIRS + PAIRS * n_experts)


def store_stage(nc, m, src, out):
    stored = m.sem("output_stored")
    with nc.Block() as block:
        @block.sync
        def _(sp):
            sp.dma_start(out.rearrange("(t b) s d -> (b s) t d", b=2), src[:]).then_inc(stored, 16)
            sp.wait_ge(stored, 16)


def build(nc, dram, out):
    with ExitStack() as ctx:
        def sb(name, shape, dt=F32):
            return ctx.enter_context(nc.sbuf_tensor(name, shape, dt))

        m = Core()
        m.H0 = 8
        m.sem = lambda name: ctx.enter_context(nc.semaphore(name))
        tallies = {}

        def tally(name):
            if name not in tallies:
                tallies[name] = Tally(m.sem(name))
            return tallies[name]
        m.tally = tally
        m.scoped = lambda c, tag: (lambda name, shape, dt=F32:
                                   c.enter_context(nc.sbuf_tensor(tag + "_" + name, shape, dt)))
        m.ps = ctx.enter_context(nc.psum_tensor("ps", [P, 8, BANK], F32))
        m.X = sb("X", [P, PAIRS, D])
        m.xT = sb("xT", [P, ROWS])
        m.Y = sb("Y", [P, PAIRS, D])
        m.nhalf, m.half = sb("nhalf", [P, 32]), sb("half", [P, 32])
        m.ones, m.ones_bf = sb("ones", [1, BANK]), sb("ones_bf", [1, P], BF16)
        m.ident_bf = sb("ident_bf", [P, P], BF16)
        m.causal_bf, m.strided_bf = sb("causal_bf", [P, BANK], BF16), sb("strided_bf", [P, BANK], BF16)
        m.ctx_nat = sb("ctx_nat", [P, 2, KT, DC + 1])
        m.turns_pool = m.sem("turns_pool")
        m.turns_act, m.turns_pe, m.turns_dve = m.sem("turns_act"), m.sem("turns_pe"), m.sem("turns_dve")
        m.loads = []

        def resident(attr, shape, source):
            t = sb(attr, shape)
            m.loads.append((t[:], source))
            return t

        m.ident = resident("ident", [P, P], dram["ident"])
        m.causal = resident("causal", [P, BANK], dram["causal"])
        m.strided = resident("strided", [P, BANK], dram["strided"])
        m.wqT0 = resident("wqT0", [S, 8, D], dram["wqT0"].rearrange("(h e) d -> e h d", h=8))
        m.wkT0 = resident("wkT0", [S, 8, DC], dram["wkT0"].rearrange("(h e) d -> e h d", h=8))
        m.wvT0 = resident("wvT0", [S, 8, DC], dram["wvT0"].rearrange("(h e) d -> e h d", h=8))
        m.wo0 = resident("wo0", [S, 8, D], dram["L0_xattn_Wo"].rearrange("(h e) d -> e h d", h=8))
        m.bo0 = resident("bo0", [1, D], dram["L0_xattn_bo"].rearrange("(o d) -> o d", o=1))
        m.qmask = resident("qmask", [P, 2], dram["qmask"])
        m.kmask = resident("kmask", [P, HP], dram["kmask"])
        m.cosb = resident("cosb", [P, S], dram["cosb"])
        m.sinb = resident("sinb", [P, S], dram["sinb"])
        m.pos = resident("pos", [P, P], dram["pos"])
        m.down = resident("down", [P, 32], dram["down"])
        m.rope_sign = resident("rope_sign", [P, 1], dram["rope_sign"])
        m.small0 = []
        for n in ("wqB", "wqBs", "wkB", "wkBs", "wvB", "woB"):
            m.small0.append(resident(n, [P, P], dram[n]))
        m.wqk = []
        for n in ("wqC", "wqCs", "wkC", "wkCs"):
            m.wqk.append(resident(n, [P, HP * P], dram[n]))
        m.bqk = resident("bqk", [P, 4, HP], dram["bqkC"])
        m.wv_c = resident("wv_c", [P, HP * P], dram["L0_ffn_v_w"])
        m.bv_c = resident("bv_c", [P, HP], dram["bvC"])
        m.wo_c = resident("wo_c", [P, HP, D], dram["L0_ffn_o_w"].rearrange("(h p) d -> p h d", p=P))
        m.bo_c = resident("bo_c", [1, D], dram["L0_ffn_o_b"].rearrange("(o d) -> o d", o=1))
        m.theta = sb("theta", [P, 1])
        for q in range(4):
            m.loads.append((m.theta[32 * q:32 * q + 32, :], dram["L0_ffn_theta"].rearrange("(p o) -> p o", o=1)))
        m.gain1 = resident("gain1", [P, D], dram["L0_ffn_gamma1"].partition_broadcast(P))
        m.gain2 = resident("gain2", [P, D], dram["L0_ffn_gamma2"].partition_broadcast(P))
        m.wr0 = resident("wr0", [P, 31], dram["L0_ffn_router_w"])
        m.br0 = resident("br0", [1, 31], dram["L0_ffn_router_b"].rearrange("(o d) -> o d", o=1))
        m.b2_0 = resident("b2_0", [32, D], dram["b2_0"])
        def column(source):
            return source.rearrange("(p o) -> p o", o=1)

        def row(source):
            return source.rearrange("(o d) -> o d", o=1)
        m.ln_l_g = resident("ln_l_g", [P, D], dram["L1_xattn_ln_l_g"].partition_broadcast(P))
        m.ln_l_b = resident("ln_l_b", [P, D], dram["L1_xattn_ln_l_b"].partition_broadcast(P))
        m.ln_x_g = resident("ln_x_g", [DC, 1], column(dram["L1_xattn_ln_x_g"]))
        m.ln_x_b = resident("ln_x_b", [DC, 1], column(dram["L1_xattn_ln_x_b"]))
        m.qn_g, m.kn_g = sb("qn_g", [P, D]), sb("kn_g", [P, D])
        for h in range(2):
            for t, n in ((m.qn_g, "L1_xattn_qn_g"), (m.kn_g, "L1_xattn_kn_g")):
                m.loads.append((t[:, 64 * h:64 * h + 64], dram[n].partition_broadcast(P)))
        m.wq1 = resident("wq1", [P, P], dram["wq1"])
        m.wkv1 = resident("wkv1", [DC, 2 * P], dram["wkv1"])
        m.wlkv1 = resident("wlkv1", [P, 2 * P], dram["wlkv1"])
        m.wo1 = resident("wo1", [P, P], dram["wo1"])
        m.bo1 = resident("bo1", [1, P], row(dram["L1_xattn_bo"]))
        m.wq_e, m.wk_e, m.wv_e = (resident(f"w{n}_e", [P, P], dram[f"L1_attn_W{n}"]) for n in "qkv")
        m.wo_e = resident("wo_e", [P, P], dram["L1_attn_Wp"])
        m.bq_e = resident("bq_e", [P, 1], column(dram["L1_attn_bq"]))
        m.bk_e = resident("bk_e", [P, 1], column(dram["L1_attn_bk"]))
        m.bv_e = resident("bv_e", [S, D], dram["L1_attn_bv"].partition_broadcast(S))
        m.bo_e = resident("bo_e", [1, D], row(dram["L1_attn_bp"]))
        m.gain6 = resident("gain6", [P, D], dram["L1_ffn_norm_weight"].partition_broadcast(P))
        m.wr1 = resident("wr1", [P, 8], dram["wr1"])
        m.b2_1 = resident("b2_1", [9, D], dram["b2_1"])
        m.gates = sb("gates", [P, PAIRS, 32])
        m.cosc, m.sinc = sb("cosc", [P, P]), sb("sinc", [P, P])
        load_stage(nc, m, dram)
        ln = [("ln", 1e-5, None, None)]

        def scope():
            c = ExitStack()
            return c, lambda name, shape, dt=F32: c.enter_context(nc.sbuf_tensor(name, shape, dt))
        c0, s0 = scope()
        with c0:
            m.mq0, m.nv0 = s0("mq0", [P, 8, P]), s0("nv0", [DC, 8, D])
            m.U, m.Ub = s0("U", [DC + 1, BATCHES, 8, S]), s0("Ub", [DC, BATCHES, 8, S], BF16)
            norm_stage(nc, m, "n0", m.X, m.Y, m.xT, ln)
            l0_fold_stage(nc, m)
            l0_cross_stage(nc, m, dram)
        c0, s0 = scope()
        with c0:
            m.qT, m.kT, m.V = s0("qT", [P, ROWS]), s0("kT", [P, ROWS]), s0("V", [S, BATCHES, D])
            norm_stage(nc, m, "n1", m.X, m.Y, m.xT, ln)
            project_small_heads_stage(nc, m, "p1", m.small0[:5], True, None)
            small_heads_stage(nc, m, "a1", m.causal_bf, m.small0[5], None)
        c0, s0 = scope()
        with c0:
            m.AO = s0("AO", [P, PAIRS, D])
            norm_stage(nc, m, "n2", m.X, m.Y, m.xT, ln + [("rms", 1e-5, m.gain1, None)])
            angles_stage(nc, m)
            wide_heads_stage(nc, m)
            norm_stage(nc, m, "n3", m.AO, m.Y, m.xT, [("rms", 1e-5, m.gain2, None)])
            router_stage(nc, m, "r0", 31, 3, m.wr0, m.br0, m.b2_0, True, [m.AO, m.Y])
            experts_stage(nc, m, "e0", 32, 1, ACT.Gelu, 4, dram["w1_0"], dram["w2_0"], dram["b1_0"])
        c0, s0 = scope()
        with c0:
            m.qbd1, m.WA = s0("qbd1", [P, BATCHES, 2, S]), s0("WA", [DC + 1, 2 * P])
            norm_stage(nc, m, "n4", m.X, m.Y, m.xT, ln + [("ln", 1e-5, m.ln_l_g, m.ln_l_b)])
            l1_prepare_stage(nc, m)
            l1_cross_stage(nc, m, dram)
        c0, s0 = scope()
        with c0:
            m.qT, m.kT, m.V = s0("qT1", [P, ROWS]), s0("kT1", [P, ROWS]), s0("V1", [S, BATCHES, D])
            norm_stage(nc, m, "n5", m.X, m.Y, m.xT, ln)
            project_small_heads_stage(nc, m, "p5", [m.wq_e, m.wk_e, m.wv_e], False, [m.bq_e, m.bk_e, m.bv_e])
            small_heads_stage(nc, m, "a5", m.strided_bf, m.wo_e, m.bo_e)
        norm_stage(nc, m, "n6", m.X, m.Y, m.xT, ln + [("rms", 1e-8, m.gain6, None)])
        router_stage(nc, m, "r1", 8, 2, m.wr1, None, m.b2_1, False, [])
        experts_stage(nc, m, "e1", 9, 4, ACT.Relu, 3, dram["w1_1"], dram["w2_1"], dram["b1_1"])
        store_stage(nc, m, m.X, out)


def kernel(**inputs):
    import numpy as np
    import concourse.bacc as bacc
    from concourse.bass_utils import run_bass_kernel_spmd

    arrays = {n: np.ascontiguousarray(a) for n, a in inputs.items()}
    arrays["ctx"] = arrays.pop("ctx_768")
    arrays["ctxT"] = np.ascontiguousarray(arrays["ctx"].transpose(0, 2, 1))
    for new, old in (("wqT0", "L0_xattn_Wq"), ("wkT0", "L0_xattn_Wk"), ("wvT0", "L0_xattn_Wv")):
        arrays[new] = np.ascontiguousarray(arrays[old].T)
    i, key = np.arange(128)[:, None] % 64, np.arange(512)[None, :] % 64
    arrays["ident"] = np.eye(128, dtype=np.float32)
    arrays["causal"] = np.where(key <= i, 0.0, NEG).astype(np.float32)
    arrays["strided"] = np.where((key <= i) & (key % 4 != 3), 0.0, NEG).astype(np.float32)

    h, feature = np.arange(128) // 8, np.arange(128) % 8
    arrays["qmask"] = (h[:, None] % 2 == np.arange(2)).astype(np.float32)
    arrays["kmask"] = (h[:, None] // 2 == np.arange(8)).astype(np.float32)
    inv = (1.0 / 10000.0 ** (np.arange(0, 8, 2, dtype=np.float32) / 8)).astype(np.float32)
    angle = (np.arange(64, dtype=np.float32)[None, :] * inv[feature % 4][:, None]).astype(np.float32)
    arrays["cosb"] = np.cos(angle)
    arrays["sinb"] = np.sin(angle) * np.where(feature < 4, -1, 1).astype(np.float32)[:, None]
    arrays["pos"] = np.tile(np.arange(64, dtype=np.float32), (128, 2))
    arrays["rope_sign"] = np.where(np.arange(128) % 64 < 32, -1, 1).astype(np.float32)[:, None]
    arrays["down"] = np.tile(np.arange(32, 0, -1).astype(np.float32), (128, 1))
    swap8 = (np.arange(16)[:, None] * 8 + (np.arange(8) + 4) % 8).reshape(-1)
    for new, old in (("wqB", "L0_attn_W_q"), ("wkB", "L0_attn_W_k"), ("wvB", "L0_attn_W_v"), ("woB", "L0_attn_W_o")):
        arrays[new] = np.ascontiguousarray(arrays[old].T)
    for n in ("wqB", "wkB"):
        arrays[n + "s"] = np.ascontiguousarray(arrays[n][:, swap8])
    halves = np.concatenate([np.arange(0, 64, 2), np.arange(1, 64, 2)])
    split = (np.arange(16)[:, None] * 64 + halves).reshape(-1)
    swapped = (np.arange(16)[:, None] * 64 + np.roll(halves, 32)).reshape(-1)
    biases = []
    for q in "qk":
        w, bias = arrays[f"L0_ffn_{q}_w"], arrays[f"L0_ffn_{q}_b"]
        for tag, order in (("", split), ("s", swapped)):
            arrays[f"w{q}C{tag}"] = np.ascontiguousarray(w[:, order])
            biases.append(bias[order].reshape(8, 128).T)
    arrays["bvC"] = np.ascontiguousarray(arrays["L0_ffn_v_b"].reshape(8, 128).T)
    arrays["bqkC"] = np.ascontiguousarray(np.stack(biases, 1))
    arrays["w1_0"] = np.concatenate([arrays["L0_ffn_re_w1"], arrays["L0_ffn_sh_w1"][None]])
    arrays["w2_0"] = np.concatenate([arrays["L0_ffn_re_w2"], arrays["L0_ffn_sh_w2"][None]])
    arrays["b1_0"] = np.concatenate([arrays["L0_ffn_re_b1"], arrays["L0_ffn_sh_b1"][None]])[:, :, None]
    arrays["b2_0"] = np.concatenate([arrays["L0_ffn_re_b2"], arrays["L0_ffn_sh_b2"][None]])
    arrays["mask"] = arrays["mask_BxS2_bk0"]
    for new, old in (("wq1", "Wq"), ("wkv1", "Wkv"), ("wlkv1", "Wlkv"), ("wo1", "Wo")):
        arrays[new] = np.ascontiguousarray(arrays["L1_xattn_" + old].T)
    arrays["wr1"] = np.ascontiguousarray(arrays["L1_ffn_router_w"].T)
    for new, old in (("w1_1", "w1"), ("w2_1", "w2"), ("b1_1", "b1"), ("b2_1", "b2")):
        arrays[new] = np.concatenate([arrays["L1_ffn_e" + old], arrays["L1_ffn_s" + old][None]])
    arrays["b1_1"] = np.ascontiguousarray(arrays["b1_1"].reshape(9, 4, 128).transpose(0, 2, 1))

    nc = bacc.Bacc("TRN2", target_bir_lowering=False, num_devices=1)
    dram = {}
    for n in USED:
        a = arrays[n]
        dram[n] = nc.dram_tensor("in_" + n, a.shape, mybir.dt.from_np(a.dtype), kind="ExternalInput").ap()
    out = nc.dram_tensor("out", (BATCHES, S, D), F32, kind="ExternalOutput").ap()
    build(nc, dram, out)
    got = run_bass_kernel_spmd(nc, [{"in_" + n: arrays[n] for n in USED}], core_ids=[0])
    return got.results[0]["out"]


USED = ["x", "ctx", "ctxT", "ident", "causal", "strided", "wqT0", "wkT0", "wvT0", "L0_xattn_Wo", "L0_xattn_bo",
        "qmask", "kmask", "cosb", "sinb", "pos", "down", "rope_sign", "wqB", "wqBs", "wkB", "wkBs", "wvB", "woB",
        "wqC", "wqCs", "wkC", "wkCs", "bqkC", "L0_ffn_v_w", "bvC", "L0_ffn_o_w", "L0_ffn_o_b", "L0_ffn_theta",
        "L0_ffn_gamma1", "L0_ffn_gamma2", "L0_ffn_router_w", "L0_ffn_router_b", "b2_0", "w1_0", "w2_0", "b1_0",
        "mask", "L1_xattn_ln_l_g", "L1_xattn_ln_l_b", "L1_xattn_ln_x_g", "L1_xattn_ln_x_b", "L1_xattn_qn_g",
        "L1_xattn_kn_g", "wq1", "wkv1", "wlkv1", "wo1", "L1_xattn_bo", "L1_attn_Wq", "L1_attn_Wk", "L1_attn_Wv",
        "L1_attn_Wp", "L1_attn_bq", "L1_attn_bk", "L1_attn_bv", "L1_attn_bp", "L1_ffn_norm_weight", "wr1", "b2_1",
        "w1_1", "w2_1", "b1_1"]
```

```python
from contextlib import ExitStack

import concourse.bass as bass
from concourse import mybir

F32 = mybir.dt.float32
F32R = mybir.dt.float32r
BF16 = mybir.dt.bfloat16
U8 = mybir.dt.uint8
ALU = mybir.AluOpType
ACT = mybir.ActivationFunctionType
AX = mybir.AxisListType

P = 128
BATCHES = 16
S = 64
PAIRS = BATCHES // 2
ROWS = BATCHES * S
D = 128
CTX = 1601
DC = 96
FULL = CTX // P
KT = FULL + 1
REST = CTX - FULL * P
BANK = 512
NEG = -1.0e30


def rows_of(k):
    return P if k < FULL else REST


class Core:
    pass


class Tally:

    def __init__(self, sem):
        self.sem, self.base = sem, 0

    def wait(self, eng, n):
        eng.wait_ge(self.sem, n + self.base)

    def close(self, n):
        self.base += n


class Chain:

    def __init__(self, eng, sem, base=0):
        self.eng, self.sem, self.base, self.n = eng, sem, base, 0

    def mark(self, ins):
        self.n += 1
        ins.then_inc(self.sem, 1)

    def settle(self):
        self.eng.wait_ge(self.sem, self.base + self.n)

    def link(self, ins):
        self.mark(ins)
        self.settle()


def load_stage(nc, m, dram):
    loaded = m.sem("first_inputs_loaded")
    zeroed = m.sem("buffers_set")
    casted = m.sem("constants_cast")
    with nc.Block() as block:
        @block.sync
        def _(sp):
            sp.dma_start(m.X[:], dram["x"].rearrange("(t b) s d -> (b s) t d", b=2)).then_inc(loaded, 16)
            for dst, src in m.loads[:m.n_first_loads]:
                sp.dma_start(dst, src).then_inc(loaded, 16)

        @block.gpsimd
        def _(pool):
            nc.gpsimd.memset(m.nhalf[:], -0.5).then_inc(zeroed, 1)
            nc.gpsimd.memset(m.half[:], 0.5).then_inc(zeroed, 1)
            nc.gpsimd.memset(m.ones[:], 1.0).then_inc(zeroed, 1)
            nc.gpsimd.memset(m.ones_bf[:], 1.0).then_inc(zeroed, 1)
            nc.gpsimd.memset(m.ctx_nat[:], 0.0).then_inc(zeroed, 1)
            pool.wait_ge(zeroed, 5)
            nc.gpsimd.memset(m.ctx_nat[:, :, :, DC:DC + 1], 1.0).then_inc(zeroed, 1)
            pool.wait_ge(zeroed, 6)

        @block.vector
        def _(dve):
            dve.wait_ge(loaded, 16 * (1 + m.n_first_loads))
            nc.vector.tensor_copy(m.ident_bf[:], m.ident[:]).then_inc(casted, 1)
            nc.vector.tensor_copy(m.causal_bf[:], m.masks[:, 0:BANK]).then_inc(casted, 1)
            nc.vector.tensor_copy(m.strided_bf[:], m.masks[:, BANK:2 * BANK]).then_inc(casted, 1)
            dve.wait_ge(casted, 3)


def rest_loaded_stage(nc, m):
    with nc.Block() as block:
        @block.sync
        def _(sp):
            sp.wait_ge(m.rest_loaded, 16 * (len(m.loads) - m.n_first_loads))


def norm_stage(nc, m, name, src, nat, natT, passes):
    stats_ready, rstd_ready, own, nat_ready, turned, natT_ready = (m.tally(n) for n in (
        "norm_stats_ready", "norm_rstd_ready", "norm_dve_steps", "norm_rows_ready", "norm_turned", "norm_copied"))
    with ExitStack() as ctx:
        sb = m.scoped(ctx, name)
        st6, mv = sb("st6", [P, PAIRS, 6]), sb("mv", [P, PAIRS, 2])
        ve, rstd = sb("ve", [P, PAIRS]), sb("rstd", [P, PAIRS])
        with nc.Block() as block:
            @block.vector
            def _(dve):
                chain = Chain(dve, own.sem, own.base)
                cur = src
                for i, (kind, eps, gain, shift) in enumerate(passes):
                    for t in range(PAIRS):
                        chain.mark(nc.vector.bn_stats(st6[:, t, :], cur[:, t, :]))
                    chain.settle()
                    for t in range(PAIRS):
                        chain.mark(nc.vector.bn_aggr(mv[:, t, :], st6[:, t, :]))
                    chain.settle()
                    if kind == "rms":
                        chain.link(nc.vector.tensor_tensor(ve[:], mv[:, :, 0], mv[:, :, 0], ALU.mult))
                        chain.link(nc.vector.tensor_tensor(ve[:], ve[:], mv[:, :, 1], ALU.add))
                        nc.vector.tensor_scalar(ve[:], ve[:], eps, None, ALU.add).then_inc(stats_ready.sem, 1)
                    else:
                        nc.vector.tensor_scalar(ve[:], mv[:, :, 1], eps, None, ALU.add).then_inc(stats_ready.sem, 1)
                    rstd_ready.wait(dve, i + 1)
                    tables = [(table, op) for table, op in ((gain, ALU.mult), (shift, ALU.add)) if table is not None]
                    final = i == len(passes) - 1
                    for t in range(PAIRS):
                        if kind == "rms":
                            ins = nc.vector.tensor_scalar(nat[:, t, :], cur[:, t, :], rstd[:, t:t + 1], None, ALU.mult)
                        else:
                            ins = nc.vector.tensor_scalar(nat[:, t, :], cur[:, t, :], mv[:, t, 0:1],
                                                          rstd[:, t:t + 1], ALU.subtract, ALU.mult)
                        if final and not tables:
                            ins.then_inc(nat_ready.sem, 1)
                        else:
                            chain.mark(ins)
                    for n, (table, op) in enumerate(tables):
                        chain.settle()
                        for lo in (0, PAIRS // 2):
                            tiles = nat[:, lo:lo + PAIRS // 2, :]
                            both = table[:].unsqueeze(1).broadcast_to([P, PAIRS // 2, D])
                            ins = nc.vector.tensor_tensor(tiles, tiles, both, op)
                            if final and n == len(tables) - 1:
                                ins.then_inc(nat_ready.sem, PAIRS // 2)
                            else:
                                chain.mark(ins)
                    if not final:
                        chain.settle()
                    cur = nat
                own.close(chain.n)

            @block.gpsimd
            def _(pool):
                for i in range(len(passes)):
                    stats_ready.wait(pool, i + 1)
                    nc.gpsimd.tensor_tensor(rstd[:], ve[:], m.nhalf[:, 0:PAIRS], ALU.pow).then_inc(rstd_ready.sem, 1)

            @block.tensor
            def _(pe):
                for t in range(PAIRS):
                    nat_ready.wait(pe, t + 1)
                    out = m.ps[:, t // 4, (t % 4) * P:(t % 4 + 1) * P]
                    ins = nc.tensor.transpose(out, nat[:, t, :], m.ident[:])
                    if t % 4 == 3:
                        ins.then_inc(turned.sem, 1)

            @block.scalar
            def _(act):
                for h in range(2):
                    turned.wait(act, h + 1)
                    nc.scalar.copy(natT[:, h * BANK:(h + 1) * BANK], m.ps[:, h, :]).then_inc(natT_ready.sem, 1)
                natT_ready.wait(act, 2)
    for tally, n in ((stats_ready, len(passes)), (rstd_ready, len(passes)), (nat_ready, PAIRS), (turned, 2),
                     (natT_ready, 2)):
        tally.close(n)


def l0_fold_stage(nc, m):
    folded, copied = m.sem("l0_folded"), m.sem("l0_fold_copied")
    nv_copied = m.sem("l0_nv_copied")
    u_made, u_copied = m.sem("l0_u_made"), m.sem("l0_u_copied")
    H = m.H0
    m.rest_loaded = m.sem("other_inputs_loaded")
    with nc.Block() as block:
        @block.sync
        def _(sp):
            for dst, src in m.loads[m.n_first_loads:]:
                sp.dma_start(dst, src).then_inc(m.rest_loaded, 16)

        @block.tensor
        def _(pe):
            for h in range(H):
                ins = nc.tensor.matmul(m.ps[:, h // 4, (h % 4) * P:(h % 4) * P + DC], m.wqT0[:, h, :],
                                       m.wkT0[:, h, :], start=True, stop=True)
            ins.then_inc(folded, 1)
            for h in range(H):
                ins = nc.tensor.matmul(m.ps[0:DC, 2 + h // 4, (h % 4) * P:(h % 4 + 1) * P], m.wvT0[:, h, :],
                                       m.wo0[:, h, :], start=True, stop=True)
            ins.then_inc(folded, 1)
            pe.wait_ge(copied, 1)
            for n in range(2 * H):
                h, half = n // 2, n % 2
                if n >= 4:
                    pe.wait_ge(u_copied, n - 3)
                nc.tensor.matmul(m.ps[0:DC, 4 + n % 4, :], m.mq0[:, h, 0:DC],
                                 m.xT[:, half * BANK:(half + 1) * BANK], start=True, stop=True).then_inc(u_made, 1)

        @block.scalar
        def _(act):
            act.wait_ge(folded, 1)
            nc.scalar.copy(m.mq0[:, :, 0:DC], m.ps[:, 0:2, :].rearrange("p b (h d) -> p (b h) d", d=P)[:, :, 0:DC]
                           ).then_inc(copied, 1)
            for n in range(0, 2 * H):
                h, half = n // 2, n % 2
                act.wait_ge(u_made, n + 1)
                nc.scalar.activation(m.U[0:DC, 8 * half:8 * half + 8, h, :],
                                     m.ps[0:DC, 4 + n % 4, :].rearrange("p (b i) -> p b i", i=S), ACT.Copy,
                                     scale=float(64) ** -0.5).then_inc(u_copied, 1)
            act.wait_ge(u_copied, 2 * H)

        @block.vector
        def _(dve):
            dve.wait_ge(folded, 2)
            nc.vector.tensor_copy(m.nv0[:], m.ps[0:DC, 2:4, :].rearrange("p b (h d) -> p (b h) d", d=P)
                                  ).then_inc(nv_copied, 1)
            dve.wait_ge(nv_copied, 1)


def l0_cross_stage(nc, m, dram):
    H = m.H0
    HS = H * S
    AHEAD, SLOTS = 3, 4
    ps = m.ps
    MAXB, SB, OB = 0, 4, 6
    ROUGH_AT = (0, 2, 4, 6)
    TURN_AT, Y_AT = 8, 10
    HALVES = ((0, 896), (896, CTX))
    TILE_HALVES = ((0, 7), (7, KT))
    ctxT_loaded = m.sem("l0_ctxT_loaded")
    nat_loaded = [m.sem("l0_ctx_loaded_even"), m.sem("l0_ctx_loaded_odd")]
    ones_set = m.sem("l0_constants_set")
    ctxT_high, ctxT_low = m.sem("l0_ctxT_high_ready"), m.sem("l0_ctxT_low_ready")
    nat_high, nat_low = m.sem("l0_ctx_high_ready"), m.sem("l0_ctx_low_ready")
    u_high, u_low = m.sem("l0_u_high_ready"), m.sem("l0_u_low_ready")
    rough_ready, rough_used = m.sem("l0_rough_scores_ready"), m.sem("l0_rough_scores_used")
    maxrow_turned, maxrow_written = m.sem("l0_max_turned"), m.sem("l0_max_row_written")
    scores_ready, exps_ready = m.sem("l0_scores_ready"), m.sem("l0_exps_ready")
    probs_high = m.sem("l0_probs_high_ready")
    low_even, low_odd = m.sem("l0_probs_low_even_ready"), m.sem("l0_probs_low_odd_ready")
    probs_used = m.sem("l0_probs_used")
    o_copied, recip_ready = m.sem("l0_output_copied"), m.sem("l0_reciprocal_ready")
    spread_ready, o_scaled = m.sem("l0_reciprocal_spread"), m.sem("l0_output_scaled")
    y_ready, x_updated = m.sem("l0_y_ready"), m.sem("l0_x_updated")
    EVEN, ODD = (KT + 1) // 2, KT // 2
    with ExitStack() as ctx:
        sb = m.scoped(ctx, "l0")
        ctxT = sb("ctxT", [DC, CTX])
        cTh, cTl = (sb(n, [DC + 1, 2, CTX], F32R) for n in ("ctxT_high", "ctxT_low"))
        nh, nl = (sb(n, [P, 2, KT, DC + 1], F32R) for n in ("ctx_high", "ctx_low"))
        Uh, Ul = (sb(n, [DC + 1, 2, HS], F32R) for n in ("u_high", "u_low"))
        probs = sb("probs", [P, SLOTS, HS])
        ph, pl = (sb(n, [P, SLOTS, HS], F32R) for n in ("probs_high", "probs_low"))
        mx = sb("mx", [P, 2, 4])
        osum, recip = m.masks[0:DC + 1, 0:HS], m.masks[0:1, HS:2 * HS]
        on = m.mq0[0:DC]

        def slot(b, k):
            return (KT * b + k) % SLOTS

        def u_of(j):
            return m.U[:, bass.ds(j, 1), :, :].rearrange("p o h i -> p (o h i)")

        def by_pair(eng, body):
            for b in range(2):
                body(eng, 0, b, True, 2)
            with eng.Fori(1, PAIRS - 1) as t:
                for b in range(2):
                    body(eng, t, b, False, 2)
            for b in range(2):
                body(eng, PAIRS - 1, b, False, 1 - b)

        with nc.Block() as block:
            @block.sync
            def _(sp):
                def load_T(j):
                    sp.dma_start(ctxT[:], dram["ctxT"][bass.ds(j, 1)].rearrange("o d k -> (o d) k")
                                 ).then_inc(ctxT_loaded, 16)

                def load_nat(b, j):
                    jj = bass.ds(j, 1)
                    sp.dma_start(m.ctx_nat[:, b, 0:FULL, 0:DC],
                                 dram["ctx"][jj, 0:FULL * P, :].rearrange("o (k p) d -> (o p) k d", p=P)
                                 ).then_inc(nat_loaded[b], 16)
                    sp.dma_start(m.ctx_nat[0:REST, b, FULL, 0:DC],
                                 dram["ctx"][jj, FULL * P:CTX, :].rearrange("o p d -> (o p) d")
                                 ).then_inc(nat_loaded[b], 16)

                def reload_T(j):
                    sp.wait_ge(ctxT_high, 2 * j)
                    sp.wait_ge(ctxT_low, 2 * j)
                    load_T(j)

                def reload_nat(b, j):
                    sp.wait_ge(nat_high, 2 * j - 2)
                    sp.wait_ge(nat_low, 2 * j - 2)
                    load_nat(b, j)
                load_T(0)
                load_nat(0, 0)
                load_nat(1, 1)
                reload_T(1)
                with sp.Fori(1, PAIRS) as t:
                    for b in range(2):
                        reload_T(2 * t + b)
                        reload_nat(b, 2 * t + b)

            def product(out, left, right, start, stop):
                nc.tensor.matmul(out, left[0], right[0], start=start, stop=False)
                nc.tensor.matmul(out, left[1], right[0], start=False, stop=False)
                return nc.tensor.matmul(out, left[0], right[1], start=False, stop=stop)

            def rough(pe, b, j, r, bank=MAXB):
                if r == 0:
                    pe.wait_ge(ctxT_high, 2 * j + 2)
                    pe.wait_ge(u_high, j + 1)
                if isinstance(j, int) and j == 0:
                    if r >= 2:
                        pe.wait_ge(rough_used, r - 1)
                else:
                    pe.wait_ge(rough_used, 4 * j + r)
                    if r == 0:
                        pe.wait_ge(maxrow_written, j)
                for c in range(4):
                    lo = c * BANK if c < 3 else 3 * BANK - 1
                    n = min(BANK, CTX - lo)
                    ins = nc.tensor.matmul(ps[:, bank + c, 0:n], Uh[0:DC, b, r * P:(r + 1) * P],
                                           cTh[0:DC, b, lo:lo + n], start=True, stop=True)
                ins.then_inc(rough_ready, 1)

            def turn_max(pe, b, j):
                pe.wait_ge(rough_used, 4 * j + 4)
                for r in range(4):
                    ins = nc.tensor.matmul(ps[0:1, MAXB, r * P:(r + 1) * P], mx[:, b, r:r + 1], m.ident[:],
                                           start=True, stop=True)
                ins.then_inc(maxrow_turned, 1)

            def scores(pe, b, j, k):
                if k == 0:
                    pe.wait_ge(maxrow_written, j + 1)
                    pe.wait_ge(ctxT_low, 2 * j + 2)
                    pe.wait_ge(u_low, j + 1)
                if not (isinstance(j, int) and j == 0 and k < 2):
                    pe.wait_ge(exps_ready, KT * j + k - 1)
                r, cols = rows_of(k), slice(k * P, k * P + rows_of(k))
                product(ps[0:r, SB + (KT * b + k) % 2, :], (cTh[:, b, cols], cTl[:, b, cols]),
                        (Uh[:, b, :], Ul[:, b, :]), True, True).then_inc(scores_ready, 1)

            def spread(pe, b, j):
                pe.wait_ge(recip_ready, 2 * j + 2)
                nc.tensor.matmul(ps[0:DC, OB + b, :], m.ones[0:1, 0:DC], recip[:], start=True, stop=True
                                 ).then_inc(spread_ready, 1)

            def output(pe, t):
                pe.wait_ge(o_scaled, 2 * t + 2)
                for h in range(H):
                    nc.tensor.matmul(ps[:, OB + 1, 0:D], on[:, h, :], m.nv0[:, h, :], start=(h == 0), stop=False)
                nc.tensor.matmul(ps[:, OB + 1, 0:D], m.ones[0:1, 0:P], m.bo0[:], start=False, stop=True
                                 ).then_inc(y_ready, 1)

            def pe_batch(pe, t, b, first_pair, follow):
                j, first = 2 * t + b, first_pair and b == 0
                for k in range(KT):
                    if k + AHEAD < KT:
                        scores(pe, b, j, k + AHEAD)
                    elif follow:
                        scores(pe, 1 - b, j + 1, k + AHEAD - KT)
                    if follow and k in ROUGH_AT:
                        rough(pe, 1 - b, j + 1, ROUGH_AT.index(k))
                    if k == 0:
                        pe.wait_ge(nat_high, 2 * j + 2)
                        pe.wait_ge(nat_low, 2 * j + 2)
                        if b == 0 and not first:
                            pe.wait_ge(o_scaled, j - 1)
                        if b == 1 and not first_pair:
                            pe.wait_ge(x_updated, t)
                    if k % 2 == 0:
                        pe.wait_ge(low_even, EVEN * j + k // 2 + 1)
                    else:
                        pe.wait_ge(low_odd, ODD * j + k // 2 + 1)
                    r, s = rows_of(k), slot(b, k)
                    product(ps[0:DC + 1, OB + b, :], (nh[0:r, b, k, :], nl[0:r, b, k, :]),
                            (ph[0:r, s, :], pl[0:r, s, :]), k == 0, k == KT - 1).then_inc(probs_used, 1)
                    if k == TURN_AT:
                        if follow:
                            turn_max(pe, 1 - b, j + 1)
                        if not first:
                            spread(pe, 1 - b, j - 1)
                    if k == Y_AT and b == 0 and not first:
                        output(pe, t - 1)

            @block.tensor
            def _(pe):
                pe.sem_inc(probs_used, SLOTS)
                for r in range(4):
                    rough(pe, 0, 0, r, (MAXB, SB)[r % 2])
                turn_max(pe, 0, 0)
                pe.wait_ge(ones_set, 5)
                for k in range(AHEAD):
                    scores(pe, 0, 0, k)
                by_pair(pe, pe_batch)
                spread(pe, 1, BATCHES - 1)
                output(pe, PAIRS - 1)

            def split_T_high(act, b, j, half):
                lo, hi = HALVES[half]
                act.wait_ge(ctxT_loaded, 16 * j + 16)
                nc.scalar.copy(cTh[0:DC, b, lo:hi], ctxT[:, lo:hi]).then_inc(ctxT_high, 1)

            def split_nat_high(act, b, t, half):
                lo, hi = TILE_HALVES[half]
                act.wait_ge(nat_loaded[b], 32 * t + 32)
                nc.scalar.copy(nh[:, b, lo:hi, 0:DC], m.ctx_nat[:, b, lo:hi, 0:DC]).then_inc(nat_high, 1)

            def copy_output(act, b, j, first):
                act.wait_ge(probs_used, SLOTS + KT * (j + 1))
                if not first:
                    act.wait_ge(o_scaled, j)
                nc.scalar.copy(osum[:], ps[0:DC + 1, OB + b, :]).then_inc(o_copied, 1)

            def act_batch(act, t, b, first_pair, follow):
                j, first = 2 * t + b, first_pair and b == 0
                for k in range(KT):
                    act.wait_ge(scores_ready, KT * j + k + 1)
                    act.wait_ge(probs_used, KT * j + k + (SLOTS - 1 if b == 0 and k < 2 else 1))
                    r, s = rows_of(k), slot(b, k)
                    nc.scalar.activation(probs[0:r, s, :], ps[0:r, SB + (KT * b + k) % 2, :], ACT.Exp
                                         ).then_inc(exps_ready, 1)
                    act.wait_ge(exps_ready, KT * j + k + 1)
                    nc.scalar.copy(ph[0:r, s, :], probs[0:r, s, :]).then_inc(probs_high, 1)
                    if k == 2 and not first:
                        copy_output(act, 1 - b, j - 1, first_pair)
                    if follow and k in (5, 7):
                        if not first:
                            act.wait_ge(probs_used, SLOTS + KT * j)
                        split_nat_high(act, 1 - b, t + b, (k - 5) // 2)
                    if follow == 2 and k in (11, 12):
                        act.wait_ge(scores_ready, KT * (j + 1))
                        split_T_high(act, b, j + 2, k - 11)

            @block.scalar
            def _(act):
                for half in range(2):
                    split_T_high(act, 0, 0, half)
                for half in range(2):
                    split_nat_high(act, 0, 0, half)
                for half in range(2):
                    split_T_high(act, 1, 1, half)
                by_pair(act, act_batch)
                copy_output(act, 1, BATCHES - 1, False)

            def minus(out, x, high):
                return nc.gpsimd.tensor_tensor(out, x, high, ALU.subtract)

            def split_T_low(pool, b, j, half):
                lo, hi = HALVES[half]
                pool.wait_ge(ctxT_high, 2 * j + half + 1)
                minus(cTl[0:DC, b, lo:hi], ctxT[:, lo:hi], cTh[0:DC, b, lo:hi]).then_inc(ctxT_low, 1)

            def split_nat_low(pool, b, j, half):
                lo, hi = TILE_HALVES[half]
                pool.wait_ge(nat_high, 2 * j + half + 1)
                minus(nl[:, b, lo:hi, 0:DC], m.ctx_nat[:, b, lo:hi, 0:DC], nh[:, b, lo:hi, 0:DC]).then_inc(nat_low, 1)

            def split_u_low(pool, b, j):
                pool.wait_ge(u_high, j + 1)
                pool.sem_inc(m.turns_pool, 1)
                minus(Ul[0:DC, b, :], u_of(j), Uh[0:DC, b, :]).then_inc(u_low, 1)

            def pool_batch(pool, t, b, first_pair, follow):
                j, first = 2 * t + b, first_pair and b == 0
                for k in range(1, KT, 2):
                    pool.wait_ge(probs_high, KT * j + k + 1)
                    r, s = rows_of(k), slot(b, k)
                    minus(pl[0:r, s, :], probs[0:r, s, :], ph[0:r, s, :]).then_inc(low_odd, 1)
                    if follow:
                        if k in (1, 3):
                            split_T_low(pool, 1 - b, j + 1, k // 2)
                        elif k == 5:
                            split_u_low(pool, 1 - b, j + 1)
                        elif k in (7, 9):
                            split_nat_low(pool, 1 - b, j + 1, (k - 7) // 2)

            @block.gpsimd
            def _(pool):
                row, col = slice(DC, DC + 1), slice(DC, DC + 1)
                nc.gpsimd.memset(cTh[row, :, :].bitcast(F32), 1.0).then_inc(ones_set, 1)
                nc.gpsimd.memset(cTl[row, :, :].bitcast(F32), 0.0).then_inc(ones_set, 1)
                nc.gpsimd.memset(Ul[row, :, :].bitcast(F32), 0.0).then_inc(ones_set, 1)
                pool.wait_ge(ones_set, 3)
                nc.gpsimd.memset(nh[:, :, :, col].bitcast(F32), 1.0).then_inc(ones_set, 1)
                nc.gpsimd.memset(nl[:, :, :, col].bitcast(F32), 0.0).then_inc(ones_set, 1)
                pool.wait_ge(ones_set, 5)
                for half in range(2):
                    split_T_low(pool, 0, 0, half)
                split_u_low(pool, 0, 0)
                for half in range(2):
                    split_nat_low(pool, 0, 0, half)
                by_pair(pool, pool_batch)

            def split_u_high(dve, b, j):
                nc.vector.tensor_copy(Uh[0:DC, b, :], u_of(j)).then_inc(u_high, 1)

            def take_max(dve, b, j, r, bank=MAXB):
                dve.wait_ge(rough_ready, 4 * j + r + 1)
                nc.vector.tensor_reduce(mx[:, b, r:r + 1],
                                        ps[:, bank:bank + 4, :].rearrange("p c n -> p (c n)")[:, 0:CTX + 1],
                                        axis=AX.X, op=ALU.max).then_inc(rough_used, 1)

            def write_max(dve, b, j):
                dve.wait_ge(maxrow_turned, j + 1)
                nc.vector.tensor_scalar(Uh[DC:DC + 1, b, :], ps[0:1, MAXB, :], -1.0, None, ALU.mult
                                        ).then_inc(maxrow_written, 1)

            def reciprocals(dve, j, half):
                cols = slice(half * HS // 2, (half + 1) * HS // 2)
                dve.wait_ge(o_copied, j + 1)
                nc.vector.reciprocal(recip[:, cols], osum[DC:DC + 1, cols]).then_inc(recip_ready, 1)

            def scale_output(dve, b, j):
                dve.wait_ge(spread_ready, j + 1)
                nc.vector.tensor_tensor(on[:, :, S * b:S * b + S],
                                        osum[0:DC, :].rearrange("p (h i) -> p h i", i=S),
                                        ps[0:DC, OB + b, :].rearrange("p (h i) -> p h i", i=S), ALU.mult
                                        ).then_inc(o_scaled, 1)

            def update_x(dve, t):
                dve.wait_ge(y_ready, t + 1)
                xt = m.X[:, bass.ds(t, 1), :].rearrange("p o d -> p (o d)")
                nc.vector.tensor_tensor(xt, xt, ps[:, OB + 1, 0:D], ALU.add).then_inc(x_updated, 1)

            def dve_batch(dve, t, b, first_pair, follow):
                j, first = 2 * t + b, first_pair and b == 0
                for k in range(KT):
                    if k % 2 == 0:
                        dve.wait_ge(probs_high, KT * j + k + 1)
                        r, s = rows_of(k), slot(b, k)
                        nc.vector.tensor_tensor(pl[0:r, s, :], probs[0:r, s, :], ph[0:r, s, :], ALU.subtract
                                                ).then_inc(low_even, 1)
                    if follow and k - 1 in ROUGH_AT:
                        take_max(dve, 1 - b, j + 1, ROUGH_AT.index(k - 1))
                    if k in (4, 6) and not first:
                        reciprocals(dve, j - 1, (k - 4) // 2)
                    if k == TURN_AT:
                        if follow:
                            write_max(dve, 1 - b, j + 1)
                        if not first:
                            scale_output(dve, 1 - b, j - 1)
                    if k == Y_AT and b == 0 and not first:
                        update_x(dve, t - 1)
                    if k == 11 and follow == 2:
                        dve.wait_ge(scores_ready, KT * (j + 1))
                        dve.wait_ge(u_low, j + 1)
                        split_u_high(dve, b, j + 2)

            @block.vector
            def _(dve):
                split_u_high(dve, 0, 0)
                for r in range(4):
                    take_max(dve, 0, 0, r, (MAXB, SB)[r % 2])
                write_max(dve, 0, 0)
                split_u_high(dve, 1, 1)
                by_pair(dve, dve_batch)
                for half in range(2):
                    reciprocals(dve, BATCHES - 1, half)
                scale_output(dve, 1, BATCHES - 1)
                update_x(dve, PAIRS - 1)


HP = 8


def project_small_heads_stage(nc, m, name, w, rope, bias):
    made, copied, own = m.tally("project_made"), m.tally("project_copied"), m.tally("project_dve_steps")
    zeroed = m.tally("project_values_zeroed")
    ps = m.ps
    n_qk = 4 if rope else 2
    with ExitStack() as ctx:
        sb = m.scoped(ctx, name)
        a, b = sb("a", [P, ROWS]), sb("b", [P, ROWS])
        with nc.Block() as block:
            @block.gpsimd
            def _(pool):
                nc.gpsimd.memset(m.V[:], 0.0).then_inc(zeroed.sem, 1)

            @block.tensor
            def _(pe):
                for n in range(n_qk):
                    for half in range(2):
                        ins = nc.tensor.matmul(ps[:, 2 * n + half, :], w[n][:],
                                               m.xT[:, half * BANK:(half + 1) * BANK], start=True, stop=True)
                    ins.then_inc(made.sem, 1)
                if bias:
                    copied.wait(pe, 2)
                else:
                    own.wait(pe, 3)
                for t in range(PAIRS):
                    ins = nc.tensor.matmul(ps[:, t // 4, (t % 4) * P:(t % 4 + 1) * P], m.xT[:, t * P:(t + 1) * P],
                                           w[-1][:], start=True, stop=True)
                ins.then_inc(made.sem, 1)

            if bias:
                @block.scalar
                def _(act):
                    for n, dst in ((0, m.qT), (1, m.kT)):
                        made.wait(act, n + 1)
                        nc.scalar.activation(dst[:], ps[:, 2 * n:2 * n + 2, :].rearrange("p b n -> p (b n)"),
                                             ACT.Identity, bias=bias[n][:]).then_inc(copied.sem, 1)
                    copied.wait(act, 2)

            @block.vector
            def _(dve):
                chain = Chain(dve, own.sem, own.base)
                if rope:
                    cos = m.cosb[:].unsqueeze(1).broadcast_to([P, BATCHES, S])
                    sin = m.sinb[:].unsqueeze(1).broadcast_to([P, BATCHES, S])
                    for n, dst in ((0, m.qT), (2, m.kT)):
                        for i, (tmp, table) in enumerate(((a, cos), (b, sin))):
                            made.wait(dve, n + i + 1)
                            src = ps[:, 2 * (n + i):2 * (n + i) + 2, :].rearrange("p c (b i) -> p (c b) i", i=S)
                            chain.mark(nc.vector.tensor_tensor(tmp[:].rearrange("p (b i) -> p b i", i=S), src, table,
                                                               ALU.mult))
                        chain.settle()
                        chain.link(nc.vector.tensor_tensor(dst[:], a[:], b[:], ALU.add))
                made.wait(dve, n_qk + 1)
                zeroed.wait(dve, 1)
                for batch in range(2):
                    rows = slice(S * batch, S * batch + S)
                    src = ps[rows, 0:2, :].rearrange("p k (t h c) -> p (k t) h c", h=HP, c=16)
                    if bias:
                        table = bias[2][rows, :].rearrange("p (h c) -> p h c", c=16).unsqueeze(1)
                        chain.mark(nc.vector.tensor_tensor(m.V[rows, :, :, batch, :], src,
                                                           table.broadcast_to([S, PAIRS, HP, 16]), ALU.add))
                    else:
                        chain.mark(nc.vector.tensor_copy(m.V[rows, :, :, batch, :], src))
                chain.settle()
    zeroed.close(1)
    made.close(n_qk + 1)
    copied.close(2 if bias else 0)
    own.close(8 if rope else 2)


class Softmax:

    def __init__(self, nc, m, name, sb, scale):
        self.nc, self.m, self.scale = nc, m, scale
        self.less = sb("less", [P, 2, BANK])
        self.exps, self.probsT = sb("exps", [P, HP, 2, S]), sb("probsT", [P, HP, P])
        self.mx, self.sums, self.recip = (sb(n, [P, 2, HP]) for n in ("mx", "sums", "recip"))
        self.signals = {n: m.tally("softmax_" + n) for n in (
            "scores_ready", "mx_ready", "less_ready", "exps_ready", "sums_ready", "recip_ready", "probs_ready",
            "turned", "probsT_ready")}
        (self.scores_ready, self.mx_ready, self.less_ready, self.exps_ready, self.sums_ready, self.recip_ready,
         self.probs_ready, self.turned, self.probsT_ready) = self.signals.values()

    def close(self, divided=True):
        for tally in self.signals.values():
            if divided or tally is not self.probs_ready:
                tally.close(BATCHES)

    @staticmethod
    def by_head(ap):
        return ap.rearrange("p (h k) -> p h k", k=S)

    def less_max(self, dve, b, j, bank):
        nc = self.nc
        scores = self.by_head(self.m.ps[:, bank, :])
        self.scores_ready.wait(dve, j + 1)
        nc.vector.tensor_reduce(self.mx[:, b, :], scores, axis=AX.X, op=ALU.max).then_inc(self.mx_ready.sem, 1)
        self.mx_ready.wait(dve, j + 1)
        nc.vector.tensor_tensor(self.by_head(self.less[:, b, :]), scores,
                                self.mx[:, b, :].unsqueeze(2).broadcast_to([P, HP, S]), ALU.subtract
                                ).then_inc(self.less_ready.sem, 1)

    def exp(self, act, b, j):
        self.less_ready.wait(act, j + 1)
        self.nc.scalar.activation(self.exps[:, :, b, :], self.by_head(self.less[:, b, :]), ACT.Exp, scale=self.scale
                                  ).then_inc(self.exps_ready.sem, 1)

    def sum(self, dve, b, j):
        nc = self.nc
        self.exps_ready.wait(dve, j + 1)
        nc.vector.tensor_reduce(self.sums[:, b, :], self.exps[:, :, b, :], axis=AX.X, op=ALU.add
                                ).then_inc(self.sums_ready.sem, 1)
        self.sums_ready.wait(dve, j + 1)
        nc.vector.reciprocal(self.recip[:, b, :], self.sums[:, b, :]).then_inc(self.recip_ready.sem, 1)

    def turn(self, pe, probs, bank):
        pe.sem_inc(self.m.turns_pe, 1)
        for hp in range(HP):
            ins = self.nc.tensor.transpose(self.m.ps[:, bank + hp // 4, (hp % 4) * P:(hp % 4 + 1) * P],
                                           probs[:, hp].rearrange("p b k -> p (b k)"), self.m.ident[:])
            if hp % 4 == 3:
                ins.then_inc(self.turned.sem, 1)

    def copy_turned(self, act, t, bank):
        for c in range(2):
            self.turned.wait(act, 2 * t + c + 1)
            self.nc.scalar.copy(self.probsT[:, 4 * c:4 * c + 4, :],
                                self.m.ps[:, bank + c, :].rearrange("p (h i) -> p h i", i=P)
                                ).then_inc(self.probsT_ready.sem, 1)


def small_heads_stage(nc, m, name, mask_bf, wo, bo):
    ps = m.ps
    per_y = 1 if bo is None else 2
    signals = [m.tally("heads_" + n) for n in ("operands_ready", "pv_ready", "o_copied", "o_turned", "oT_copied",
                                               "y_ready", "x_updated")]
    operands_ready, pv_ready, o_copied, o_turned, oT_copied, y_ready, x_updated = signals
    with ExitStack() as ctx:
        sb = m.scoped(ctx, name)
        sm = Softmax(nc, m, name, sb, float(8) ** -0.5)
        q2, kb = sb("q2", [P, 2, 2, S]), sb("kb", [P, 2, HP, S])
        o, oT = sb("o", [P, HP, 2, 8]), sb("oT", [P, P])
        with nc.Block() as block:
            def pe_scores(pe, t, first):
                for b in range(2):
                    j = 2 * t + b
                    operands_ready.wait(pe, 2 * j + 2)
                    if not first:
                        sm.less_ready.wait(pe, j - 1)
                    nc.tensor.matmul(ps[:, b, :], m.ident_bf[:], mask_bf[:], start=True, stop=False)
                    nc.tensor.matmul(ps[:, b, :], q2[:, b].rearrange("p h i -> p (h i)"),
                                     kb[:, b].rearrange("p h k -> p (h k)"), start=False, stop=True
                                     ).then_inc(sm.scores_ready.sem, 1)

            def pe_turn_output(pe, t, first):
                o_copied.wait(pe, 4 * t + 4)
                if not first:
                    x_updated.wait(pe, t)
                nc.tensor.transpose(ps[:, 7, 0:P], o[:].rearrange("p a b d -> p (a b d)"), m.ident[:]
                                    ).then_inc(o_turned.sem, 1)

            def pe_turn_probs(pe, t, first):
                sm.exps_ready.wait(pe, 2 * t + 2)
                if not first:
                    sm.probsT_ready.wait(pe, 2 * t)
                sm.turn(pe, sm.exps, 2)

            def pe_output(pe, t):
                oT_copied.wait(pe, t + 1)
                nc.tensor.matmul(ps[:, 7, P:2 * P], oT[:], wo[:], start=True, stop=bo is None
                                 ).then_inc(y_ready.sem, 1)
                if bo is not None:
                    nc.tensor.matmul(ps[:, 7, P:2 * P], m.ones[0:1, 0:P], bo[:], start=False, stop=True
                                     ).then_inc(y_ready.sem, 1)

            def pe_values(pe, t, first):
                if not first:
                    o_copied.wait(pe, 4 * t)
                for hp in range(HP):
                    if hp % 4 == 0:
                        sm.probsT_ready.wait(pe, 2 * t + hp // 4 + 1)
                    v = m.V[:, bass.ds(t, 1), hp].rearrange("p o b c -> p (o b c)")
                    ins = nc.tensor.matmul(ps[:, 6, 32 * hp:32 * hp + 32], sm.probsT[:, hp, :], v,
                                           start=True, stop=True)
                ins.then_inc(pv_ready.sem, 1)

            @block.tensor
            def _(pe):
                pe_scores(pe, 0, True)
                pe_scores(pe, 1, False)
                pe_turn_probs(pe, 0, True)
                pe_values(pe, 0, True)
                pe_scores(pe, 2, False)
                pe_turn_output(pe, 0, True)
                pe_turn_probs(pe, 1, False)
                pe_output(pe, 0)
                pe_values(pe, 1, False)
                with pe.Fori(0, PAIRS - 3) as u:
                    pe_scores(pe, u + 3, False)
                    pe_turn_output(pe, u + 1, False)
                    pe_turn_probs(pe, u + 2, False)
                    pe_output(pe, u + 1)
                    pe_values(pe, u + 2, False)
                pe_turn_output(pe, PAIRS - 2, False)
                pe_turn_probs(pe, PAIRS - 1, False)
                pe_output(pe, PAIRS - 2)
                pe_values(pe, PAIRS - 1, False)
                pe_turn_output(pe, PAIRS - 1, False)
                pe_output(pe, PAIRS - 1)

            def act_exp(act, t, first):
                for b in range(2):
                    if not first:
                        sm.sums_ready.wait(act, 2 * t + b - 1)
                        sm.turned.wait(act, 2 * t)
                    sm.exp(act, b, 2 * t + b)

            def act_copy_output(act, t):
                o_turned.wait(act, t + 1)
                nc.scalar.copy(oT[:], ps[:, 7, 0:P]).then_inc(oT_copied.sem, 1)

            def act_copy_probs(act, t, first):
                if not first:
                    pv_ready.wait(act, t)
                sm.copy_turned(act, t, 2)

            @block.scalar
            def _(act):
                act_exp(act, 0, True)
                act_copy_probs(act, 0, True)
                act_exp(act, 1, False)
                with act.Fori(0, PAIRS - 2) as u:
                    act_copy_output(act, u)
                    act_copy_probs(act, u + 1, False)
                    act_exp(act, u + 2, False)
                act_copy_output(act, PAIRS - 2)
                act_copy_probs(act, PAIRS - 1, False)
                act_copy_output(act, PAIRS - 1)

            def operands(pool, t, first):
                for b in range(2):
                    if not first:
                        sm.scores_ready.wait(pool, 2 * t + b - 1)
                        pool.sem_inc(m.turns_pool, 1)
                    cols = bass.ds((2 * t + b) * S, S)
                    nc.gpsimd.tensor_tensor(q2[:, b], m.qT[:, cols].unsqueeze(1).broadcast_to([P, 2, S]),
                                            m.qmask[:].unsqueeze(2).broadcast_to([P, 2, S]), ALU.mult
                                            ).then_inc(operands_ready.sem, 1)
                    nc.gpsimd.tensor_tensor(kb[:, b], m.kT[:, cols].unsqueeze(1).broadcast_to([P, HP, S]),
                                            m.kmask[:].unsqueeze(2).broadcast_to([P, HP, S]), ALU.mult
                                            ).then_inc(operands_ready.sem, 1)

            @block.gpsimd
            def _(pool):
                operands(pool, 0, True)
                with pool.Fori(0, PAIRS - 1) as u:
                    operands(pool, u + 1, False)

            def dve_front(dve, t):
                for b in range(2):
                    sm.less_max(dve, b, 2 * t + b, b)

            def dve_sums(dve, t):
                for b in range(2):
                    sm.sum(dve, b, 2 * t + b)

            def dve_output(dve, t):
                y_ready.wait(dve, per_y * (t + 1))
                xt = m.X[:, bass.ds(t, 1), :].rearrange("p o d -> p (o d)")
                nc.vector.tensor_tensor(xt, xt, ps[:, 7, P:2 * P], ALU.add).then_inc(x_updated.sem, 1)

            def dve_divide(dve, t, first):
                if not first:
                    o_turned.wait(dve, t)
                sm.recip_ready.wait(dve, 2 * t + 2)
                pv_ready.wait(dve, t + 1)
                for b in range(2):
                    for h2 in range(2):
                        rows = slice(S * h2, S * h2 + S)
                        src = ps[rows, 6, 0:32 * HP].rearrange("p (h b c) -> p h b c", b=2, c=16)
                        nc.vector.tensor_tensor(o[S * b:S * b + S, :, h2, :], src[:, :, b, 8 * h2:8 * h2 + 8],
                                                sm.recip[rows, b, :].unsqueeze(2).broadcast_to([S, HP, 8]), ALU.mult
                                                ).then_inc(o_copied.sem, 1)

            @block.vector
            def _(dve):
                dve_front(dve, 0)
                dve_sums(dve, 0)
                dve_front(dve, 1)
                dve_divide(dve, 0, True)
                dve_sums(dve, 1)
                with dve.Fori(0, PAIRS - 2) as u:
                    dve_front(dve, u + 2)
                    dve_output(dve, u)
                    dve_divide(dve, u + 1, False)
                    dve_sums(dve, u + 2)
                dve_output(dve, PAIRS - 2)
                dve_divide(dve, PAIRS - 1, False)
                dve_output(dve, PAIRS - 1)
    for tally, per_pair in zip(signals, (4, 1, 4, 1, 1, per_y, 1)):
        tally.close(per_pair * PAIRS)
    sm.close(divided=False)


def angles_stage(nc, m):
    own, pool_steps, done = m.sem("angles_dve_steps"), m.sem("angles_pool_steps"), m.sem("angles_done")
    ready = m.sem("angles_ready")
    TWO_PI, PI = 6.283185307179586, 3.1415925
    C1 = 6.28125
    C2 = 0.0019350051879882812
    C3 = TWO_PI - C1 - C2
    ROUND = 12582912.0
    with ExitStack() as ctx:
        sb = m.scoped(ctx, "angles")
        a, n, r = sb("a", [P, P]), sb("n", [P, P]), sb("r", [P, P])
        with nc.Block() as block:
            @block.vector
            def _(dve):
                chain = Chain(dve, own)
                chain.link(nc.vector.tensor_scalar(a[:], m.pos[:], m.theta[:], None, ALU.mult))
                chain.link(nc.vector.tensor_scalar(n[:], a[:], 1.0 / TWO_PI, ROUND, ALU.mult, ALU.add))
                chain.link(nc.vector.tensor_scalar(n[:], n[:], -ROUND, None, ALU.add))
                for c in (C1, C2, C3):
                    chain.link(nc.vector.scalar_tensor_tensor(out=a[:], in0=n[:], scalar=-c, in1=a[:], op0=ALU.mult,
                                                              op1=ALU.add))
                chain.link(nc.vector.tensor_scalar(a[:], a[:], PI, -PI, ALU.min, ALU.max))
                chain.link(nc.vector.tensor_scalar(r[:], a[:], -1.0, None, ALU.mult))
                chain.link(nc.vector.tensor_tensor(r[:], r[:], a[:], ALU.max))
                chain.link(nc.vector.tensor_scalar(r[:], r[:], -1.0, TWO_PI / 4, ALU.mult, ALU.add))
                nc.vector.tensor_copy(n[:, 0:1], r[:, 0:1]).then_inc(ready, 1)
                dve.wait_ge(done, 2)
                chain.link(nc.vector.tensor_scalar(m.sinc[:], m.sinc[:], m.rope_sign[:], None, ALU.mult))

            @block.scalar
            def _(act):
                act.wait_ge(ready, 1)
                nc.scalar.activation(m.sinc[:], a[:], ACT.Sin).then_inc(done, 1)
                nc.scalar.activation(m.cosc[:], r[:], ACT.Sin).then_inc(done, 1)
                act.wait_ge(done, 2)


def wide_heads_stage(nc, m):
    ps = m.ps
    name = "wide"
    xs_ready = m.sem("wide_x_staged")
    proj_ready, proj_used = m.sem("wide_projected"), m.sem("wide_projection_used")
    rot_ready = m.sem("wide_rotated")
    v_made, v_copied = m.sem("wide_v_made"), m.sem("wide_v_copied")
    pv_ready, o_copied = m.sem("wide_pv_ready"), m.sem("wide_o_copied")
    y_ready, ao_ready = m.sem("wide_y_ready"), m.sem("wide_attn_out_ready")
    qbd_zeroed, bias_steps = m.sem("wide_qbd_zeroed"), m.sem("wide_bias_steps")
    with ExitStack() as ctx:
        sb = m.scoped(ctx, name)
        sm = Softmax(nc, m, name, sb, float(64) ** -0.5)
        xs = sb("xs", [P, P])
        ta, tb = sb("ta", [P, 2, HP, P]), sb("tb", [P, 2, HP, P])
        qbd = sb("qbd", [P, 2, HP, P])
        kr = sb("kr", [P, HP, P])
        V = sb("v", [P, HP * P])
        probs, probsT = sb("probs", [P, HP, 2, S]), sm.probsT
        oT = sb("oT", [P, HP, P])

        def proj_banks(n):
            return 2 * (n % 2)

        with nc.Block() as block:
            def project(pe, t, n):
                x = m.xT[:, bass.ds(t * P, P)]
                for hp in range(HP):
                    ins = nc.tensor.matmul(ps[:, proj_banks(n) + hp // 4, (hp % 4) * P:(hp % 4 + 1) * P],
                                           m.wqk[n][:, hp * P:(hp + 1) * P], x, start=True, stop=True)
                ins.then_inc(proj_ready, 1)

            def output(pe, t, last):
                pe.wait_ge(o_copied, 4 * t + 4)
                if last:
                    pe.wait_ge(ao_ready, t)
                else:
                    sm.less_ready.wait(pe, 2 * t + 4)
                for hp in range(HP):
                    ins = nc.tensor.matmul(ps[:, 4, 0:D], oT[:, hp, :], m.wo_c[:, hp, :], start=(hp == 0),
                                           stop=(hp == HP - 1))
                ins.then_inc(y_ready, 1)

            def turn_probs(pe, t, first):
                sm.probs_ready.wait(pe, 2 * t + 2)
                if not first:
                    pe.wait_ge(ao_ready, t)
                sm.turn(pe, probs, 4)

            def values_product(pe, t, b):
                for hp in range(HP):
                    if b == 0 and hp % 4 == 0:
                        sm.probsT_ready.wait(pe, 2 * t + hp // 4 + 1)
                    ins = nc.tensor.matmul(ps[:, (6, 0)[b] + hp // 4, (hp % 4) * P:(hp % 4 + 1) * P],
                                           V[S * b:S * b + S, hp * P:(hp + 1) * P], probsT[S * b:S * b + S, hp, :],
                                           start=True, stop=True)
                ins.then_inc(pv_ready, 1)

            def scores(pe, t, first):
                if not first:
                    sm.probsT_ready.wait(pe, 2 * t)
                for b in range(2):
                    pe.wait_ge(rot_ready, 4 * t + 3 + b)
                    nc.tensor.matmul(ps[:, 4 + b, :], m.ident_bf[:], m.causal_bf[:], start=True, stop=False)
                    for hp in range(HP):
                        ins = nc.tensor.matmul(ps[:, 4 + b, hp * S:(hp + 1) * S], qbd[:, b, hp, :],
                                               kr[:, hp, b * S:(b + 1) * S], start=False, stop=(hp == HP - 1))
                    ins.then_inc(sm.scores_ready.sem, 1)

            def values(pe, t, first):
                pe.wait_ge(xs_ready, t + 1)
                if not first:
                    pe.wait_ge(o_copied, 4 * t - 2)
                for c in range(2):
                    ins = nc.tensor.matmul(ps[:, 6 + c, :], xs[:], m.wv_c[:, c * BANK:(c + 1) * BANK],
                                           start=True, stop=True)
                ins.then_inc(v_made, 1)

            def pe_turn(pe, t, front, back, out):
                if front:
                    if back and out:
                        pe.wait_ge(o_copied, 4 * t - 4)
                    project(pe, t, 0)
                    if back:
                        pe.wait_ge(proj_used, 4 * t)
                    project(pe, t, 1)
                if out:
                    output(pe, t - 2, False)
                if front:
                    pe.wait_ge(proj_used, 4 * t + 1)
                    project(pe, t, 2)
                if back:
                    turn_probs(pe, t - 1, not out)
                if front:
                    pe.wait_ge(proj_used, 4 * t + 2)
                    project(pe, t, 3)
                if back:
                    pe.wait_ge(v_copied, t)
                    values_product(pe, t - 1, 0)
                    if front:
                        pe.wait_ge(proj_used, 4 * t + 3)
                    values_product(pe, t - 1, 1)
                if front:
                    scores(pe, t, not back)
                    values(pe, t, not back)

            @block.tensor
            def _(pe):
                pe.wait_ge(bias_steps, 1)
                for hp in range(HP):
                    nc.tensor.matmul(ps[:, 6, 0:D], ta[:, 0, hp, :], m.wo_c[:, hp, :], start=(hp == 0), stop=False)
                nc.tensor.matmul(ps[:, 6, 0:D], m.ones[0:1, 0:P], m.bo_c[:], start=False, stop=True
                                 ).then_inc(y_ready, 1)
                pe.wait_ge(bias_steps, 2)
                pe.wait_ge(qbd_zeroed, 1)
                pe_turn(pe, 0, True, False, False)
                pe_turn(pe, 1, True, True, False)
                with pe.Fori(0, PAIRS - 2) as u:
                    pe_turn(pe, u + 2, True, True, True)
                pe_turn(pe, PAIRS, False, True, True)
                output(pe, PAIRS - 1, True)

            def stage_x(act, t, first):
                if not first:
                    act.wait_ge(v_made, t)
                    act.sem_inc(m.turns_act, 1)
                nc.scalar.copy(xs[:], m.xT[:, bass.ds(t * P, P)]).then_inc(xs_ready, 1)

            def copy_values(act, t, first):
                act.wait_ge(v_made, t + 1)
                if not first:
                    act.wait_ge(pv_ready, 2 * t)
                nc.scalar.copy(V[:], ps[:, 6:8, :].rearrange("p c n -> p (c n)")).then_inc(v_copied, 1)

            def exps(act, t, first):
                for b in range(2):
                    if not first:
                        sm.probs_ready.wait(act, 2 * t + b - 1)
                    sm.exp(act, b, 2 * t + b)

            def copy_turned(act, t, first):
                if not first:
                    act.wait_ge(pv_ready, 2 * t)
                sm.copy_turned(act, t, 4)

            def copy_products(act, t, first):
                if not first:
                    act.wait_ge(y_ready, t + 1)
                for b in range(2):
                    act.wait_ge(pv_ready, 2 * t + b + 1)
                    for h2 in range(2):
                        rows, c = slice(S * h2, S * h2 + S), (6, 0)[b]
                        src = ps[rows, c:c + 2, :].rearrange("p c (h i) -> p (c h) i", i=P)
                        nc.scalar.copy(oT[rows, :, S * b:S * b + S], src[:, :, S * h2:S * h2 + S]
                                       ).then_inc(o_copied, 1)

            @block.scalar
            def _(act):
                stage_x(act, 0, True)
                exps(act, 0, True)
                copy_values(act, 0, True)
                stage_x(act, 1, False)
                copy_turned(act, 0, True)
                copy_products(act, 0, True)
                exps(act, 1, False)
                copy_values(act, 1, False)
                with act.Fori(0, PAIRS - 2) as u:
                    stage_x(act, u + 2, False)
                    copy_turned(act, u + 1, False)
                    copy_products(act, u + 1, False)
                    exps(act, u + 2, False)
                    copy_values(act, u + 2, False)
                copy_turned(act, PAIRS - 1, False)
                copy_products(act, PAIRS - 1, False)

            def divide(pool, t, first):
                pool.wait_ge(rot_ready, 4 * t + 4)
                if not first:
                    sm.turned.wait(pool, 2 * t)
                for b in range(2):
                    sm.recip_ready.wait(pool, 2 * t + b + 1)
                    nc.gpsimd.tensor_tensor(probs[:, :, b, :], sm.exps[:, :, b, :],
                                            sm.recip[:, b, :].unsqueeze(2).broadcast_to([P, HP, S]), ALU.mult
                                            ).then_inc(sm.probs_ready.sem, 1)

            def rotate(pool, t, first):
                if not first:
                    sm.scores_ready.wait(pool, 2 * t)
                    sm.probs_ready.wait(pool, 2 * t)
                pool.wait_ge(proj_used, 4 * t + 2)
                for h2 in range(2):
                    rows = slice(S * h2, S * h2 + S)
                    nc.gpsimd.tensor_tensor(qbd[rows, :, :, S * h2:S * h2 + S],
                                            ta[rows, 0].rearrange("p h (b i) -> p b h i", b=2),
                                            tb[rows, 0].rearrange("p h (b i) -> p b h i", b=2), ALU.add
                                            ).then_inc(rot_ready, 1)
                pool.wait_ge(rot_ready, 4 * t + 2)
                pool.wait_ge(proj_used, 4 * t + 4)
                for b in range(2):
                    cols = slice(S * b, S * b + S)
                    nc.gpsimd.tensor_tensor(kr[:, :, cols], ta[:, 1, :, cols], tb[:, 1, :, cols], ALU.add
                                            ).then_inc(rot_ready, 1)

            @block.gpsimd
            def _(pool):
                nc.gpsimd.memset(qbd[:], 0.0).then_inc(qbd_zeroed, 1)
                pool.wait_ge(qbd_zeroed, 1)
                rotate(pool, 0, True)
                divide(pool, 0, True)
                with pool.Fori(0, PAIRS - 1) as u:
                    rotate(pool, u + 1, False)
                    divide(pool, u + 1, False)

            def bias_turn(dve, t, n, first):
                dve.wait_ge(proj_ready, 4 * t + n + 1)
                if not first and n in (0, 2):
                    dve.wait_ge(rot_ready, 4 * t - (2 if n == 0 else 0))
                dst, table = ((ta, m.cosc), (tb, m.sinc))[n % 2]
                for hp in range(HP):
                    ins = nc.vector.scalar_tensor_tensor(
                        out=dst[:, n // 2, hp, :],
                        in0=ps[:, proj_banks(n) + hp // 4, (hp % 4) * P:(hp % 4 + 1) * P],
                        scalar=m.bqk[:, n, hp:hp + 1], in1=table[:], op0=ALU.add, op1=ALU.mult)
                ins.then_inc(proj_used, 1)

            def attn_out(dve, t):
                dve.wait_ge(y_ready, t + 2)
                tt = bass.ds(t, 1)
                nc.vector.tensor_tensor(m.AO[:, tt, :].rearrange("p o d -> p (o d)"), ps[:, 4, 0:D],
                                        m.Y[:, tt, :].rearrange("p o d -> p (o d)"), ALU.add
                                        ).then_inc(ao_ready, 1)

            def softmax(dve, t):
                for b in range(2):
                    sm.less_max(dve, b, 2 * t + b, 4 + b)
                for b in range(2):
                    sm.sum(dve, b, 2 * t + b)

            @block.vector
            def _(dve):
                nc.vector.tensor_copy(ta[:, 0], m.bv_c[:].unsqueeze(2).broadcast_to([P, HP, P])
                                      ).then_inc(bias_steps, 1)
                dve.wait_ge(y_ready, 1)
                nc.vector.tensor_tensor(m.Y[:], m.Y[:], ps[:, 6, 0:D].unsqueeze(1).broadcast_to([P, PAIRS, D]),
                                        ALU.add).then_inc(bias_steps, 1)
                dve.wait_ge(bias_steps, 2)
                for t in range(2):
                    for n in range(4):
                        bias_turn(dve, t, n, t == 0)
                    softmax(dve, t)
                with dve.Fori(0, PAIRS - 2) as u:
                    for n in range(2):
                        bias_turn(dve, u + 2, n, False)
                    attn_out(dve, u)
                    for n in range(2, 4):
                        bias_turn(dve, u + 2, n, False)
                    softmax(dve, u + 2)
                attn_out(dve, PAIRS - 2)
                attn_out(dve, PAIRS - 1)
    sm.close()


LAT = S
KEYS = CTX + LAT
EPS_RMS = 1e-8


def load_context(sp, m, dram, loaded, b, j):
    jj = bass.ds(j, 1)
    sp.dma_start(m.ctx_nat[:, b, 0:FULL, 0:DC],
                 dram["ctx"][jj, 0:FULL * P, :].rearrange("o (k p) d -> (o p) k d", p=P)).then_inc(loaded, 16)
    sp.dma_start(m.ctx_nat[0:REST, b, FULL, 0:DC],
                 dram["ctx"][jj, FULL * P:CTX, :].rearrange("o p d -> (o p) d")).then_inc(loaded, 16)


def l1_prepare_stage(nc, m, dram):
    ps = m.ps
    shift_made, shift_copied = m.sem("l1_shift_made"), m.sem("l1_shift_copied")
    q_made, squared, powered = m.sem("l1_q_made"), m.sem("l1_q_squared"), m.sem("l1_q_norms")
    own, ss_ready, q_ready = m.sem("l1_prep_dve_steps"), m.sem("l1_q_squares_summed"), m.sem("l1_q_normed")
    q_turned, qbd_zeroed = m.sem("l1_q_turned"), m.sem("l1_qbd_zeroed")
    m.l1_ctx_loaded = [m.sem("l1_ctx_loaded_even"), m.sem("l1_ctx_loaded_odd")]
    with ExitStack() as ctx:
        sb = m.scoped(ctx, "l1p")
        sq, qn = sb("sq", [P, PAIRS, D]), sb("qn", [P, PAIRS, D])
        ss, nrm, gain = sb("ss", [P, 16]), sb("nrm", [P, 16]), sb("gain", [P, D])
        with nc.Block() as block:
            @block.sync
            def _(sp):
                for b in range(2):
                    load_context(sp, m, dram, m.l1_ctx_loaded[b], b, b)

            @block.tensor
            def _(pe):
                nc.tensor.matmul(ps[0:1, 0, 0:2 * P], m.ln_x_b[:], m.wkv1[:], start=True, stop=True
                                 ).then_inc(shift_made, 1)
                for t in range(PAIRS):
                    ins = nc.tensor.matmul(ps[:, 2 + t // 4, (t % 4) * P:(t % 4 + 1) * P], m.xT[:, t * P:(t + 1) * P],
                                           m.wq1[:], start=True, stop=True)
                ins.then_inc(q_made, 1)
                pe.wait_ge(q_ready, 1)
                for t in range(PAIRS):
                    ins = nc.tensor.transpose(ps[:, 4 + t // 4, (t % 4) * P:(t % 4 + 1) * P], qn[:, t, :], m.ident[:])
                ins.then_inc(q_turned, 1)

            @block.scalar
            def _(act):
                act.wait_ge(shift_made, 1)
                nc.scalar.copy(m.WA[DC:DC + 1, :], ps[0:1, 0, 0:2 * P]).then_inc(shift_copied, 1)
                act.wait_ge(q_made, 1)
                nc.scalar.activation(sq[:], ps[:, 2:4, :].rearrange("p b (t d) -> p (b t) d", d=D), ACT.Square
                                     ).then_inc(squared, 1)
                act.wait_ge(shift_copied, 1)

            @block.gpsimd
            def _(pool):
                nc.gpsimd.memset(m.qbd1[:], 0.0).then_inc(qbd_zeroed, 1)
                pool.wait_ge(ss_ready, 1)
                nc.gpsimd.tensor_tensor(nrm[:], ss[:], m.half[:, 0:16], ALU.pow).then_inc(powered, 1)

            @block.vector
            def _(dve):
                chain, V = Chain(dve, own), nc.vector
                chain.mark(V.tensor_scalar(m.WA[0:DC, :], m.wkv1[:], m.ln_x_g[:], None, ALU.mult))
                chain.link(V.tensor_tensor(gain[:], m.qn_g[:], m.kn_g[:], ALU.mult))
                chain.link(V.tensor_scalar(gain[:], gain[:], float(64) ** -0.5 * 2 * float(64) ** 0.5, None,
                                           ALU.mult))
                dve.wait_ge(squared, 1)
                V.tensor_reduce(ss[:], sq[:].rearrange("p t (h d) -> p (t h) d", d=64), axis=AX.X, op=ALU.add
                                ).then_inc(ss_ready, 1)
                dve.wait_ge(powered, 1)
                chain.link(V.tensor_scalar(nrm[:], nrm[:], float(64) ** -0.5, EPS_RMS, ALU.mult, ALU.max))
                chain.link(V.reciprocal(nrm[:], nrm[:]))
                chain.link(V.tensor_tensor(qn[:].rearrange("p t (h d) -> p (t h) d", d=64),
                                           ps[:, 2:4, :].rearrange("p b (t d) -> p (b t) d", d=64),
                                           nrm[:].unsqueeze(2).broadcast_to([P, 16, 64]), ALU.mult))
                V.tensor_tensor(qn[:], qn[:], gain[:].unsqueeze(1).broadcast_to([P, PAIRS, D]), ALU.mult
                                ).then_inc(q_ready, 1)
                dve.wait_ge(q_turned, 1)
                dve.wait_ge(qbd_zeroed, 1)
                for h in range(2):
                    rows = slice(64 * h, 64 * h + 64)
                    chain.mark(V.tensor_copy(m.qbd1[rows, :, h, :],
                                             ps[rows, 4:6, :].rearrange("p c (b i) -> p (c b) i", i=S)))
                chain.settle()


def l1_cross_stage(nc, m, dram):
    ps = m.ps
    TILES = KT * P
    loaded = m.l1_ctx_loaded
    mask_loaded, mask_ready = m.sem("l1_mask_loaded"), m.sem("l1_mask_ready")
    sums, means = m.sem("l1_row_sums"), m.sem("l1_means")
    centered, squared = m.sem("l1_centered"), m.sem("l1_centered_squared")
    sqsums, variances, rstd_ready = m.sem("l1_square_sums"), m.sem("l1_variances"), m.sem("l1_rstd_ready")
    xh_ready = m.sem("l1_context_normed")
    xh_turned, xhT_ready = m.sem("l1_context_turned"), m.sem("l1_contextT_ready")
    staged = m.sem("l1_pair_staged")
    k_made, k_squared, kss_ready, knorm_ready = (m.sem(n) for n in (
        "l1_keys_made", "l1_keys_squared", "l1_key_squares_summed", "l1_key_norms"))
    rk_steps, kn_ready = m.sem("l1_key_scale_steps"), m.sem("l1_keys_normed")
    vlat_ready = m.sem("l1_latent_values_ready")
    kn_turned, knT_ready = m.sem("l1_keys_turned"), m.sem("l1_keysT_ready")
    scores_ready, mx_steps, exps_ready = m.sem("l1_scores_ready"), m.sem("l1_max_steps"), m.sem("l1_exps_ready")
    recip_ready = m.sem("l1_recip_ready")
    p_turned, pT_even_ready, pT_front_ready, pT_back_ready = (m.sem("l1_" + n) for n in (
        "probs_turned", "probsT_even_ready", "probsT_odd_front_ready", "probsT_odd_back_ready"))
    oT_made, oT_copied, o_made, o_copied = (m.sem("l1_" + n) for n in (
        "oT_made", "oT_copied", "o_made", "o_copied"))
    a_turned, aT_copied, y_made, x_updated = (m.sem("l1_" + n) for n in (
        "attn_turned", "attnT_copied", "y_made", "x_updated"))
    set_once = m.sem("l1_buffers_set")
    with ExitStack() as ctx:
        sb = m.scoped(ctx, "l1")
        mask_u8, mask_bf = sb("mask_u8", [BATCHES, CTX], U8), sb("mask_bf", [P, KEYS], BF16)
        pick = sb("pick", [P, BATCHES, P], BF16)
        xh = sb("xh", [P, 4, KT, DC + 1])
        sq, stat = sb("sq", [P, 2, KT, DC]), sb("stat", [P, 2, 4, KT])
        lat, qs = sb("lat", [P, P]), sb("qs", [P, 2, P])
        kss, knorm, krec = (sb(n, [P, 2, KT + 1, 2]) for n in ("kss", "knorm", "krec"))
        vlat = sb("vlat", [S, 2, P])
        ksq = sb("ksq_probs", [P, 2, KT + 1, P])
        kn = sb("kn_probsT", [P, 2, KT + 1, P])
        turned = sb("contextT_keysT", [P, 2, KEYS])
        probs = ksq[:].rearrange("p b k d -> p b (k d)")
        pT = kn
        negm, total, recip, mxp = (sb(n, [P, 2]) for n in ("negm", "total", "recip", "mxp"))
        spare = sb("spare", [P, 1])
        oT, attn, attnT = sb("oT", [DC + 1, 2, P]), sb("attn", [P, P]), sb("attnT", [P, P])

        def group(b):
            return ps[:, 4 * b:4 * b + 4, :].rearrange("p c n -> p (c n)")

        def half_tiles(h):
            return (0, 8) if h == 0 else (8, KT)

        with nc.Block() as block:
            @block.sync
            def _(sp):
                sp.dma_start(mask_u8[:], dram["mask"]).then_inc(mask_loaded, 16)
                with sp.Fori(0, PAIRS - 1) as t:
                    for b in range(2):
                        sp.wait_ge(centered, 2 * t + b + 1)
                        load_context(sp, m, dram, loaded[b], b, 2 * t + 2 + b)

            @block.gpsimd
            def _(pool):
                nc.gpsimd.memset(xh[:, :, :, DC:DC + 1], 1.0).then_inc(set_once, 1)
                nc.gpsimd.memset(mask_bf[:], 0.0).then_inc(set_once, 1)
                nc.gpsimd.memset(kss[:], 1.0).then_inc(set_once, 1)
                pool.wait_ge(set_once, 3)

                def center(b, q, j):
                    pool.wait_ge(means, j + 1)
                    nc.gpsimd.tensor_tensor(xh[:, 2 * q + b, :, 0:DC], m.ctx_nat[:, b, :, 0:DC],
                                            stat[:, b, 1, :].unsqueeze(2).broadcast_to([P, KT, DC]), ALU.subtract
                                            ).then_inc(centered, 1)

                def scale(b, q, j):
                    pool.wait_ge(variances, j + 1)
                    nc.gpsimd.tensor_tensor(stat[:, b, 3, :], stat[:, b, 2, :], m.nhalf[:, 0:KT], ALU.pow
                                            ).then_inc(rstd_ready, 1)
                    pool.wait_ge(rstd_ready, j + 1)
                    nc.gpsimd.tensor_tensor(xh[:, 2 * q + b, :, 0:DC], xh[:, 2 * q + b, :, 0:DC],
                                            stat[:, b, 3, :].unsqueeze(2).broadcast_to([P, KT, DC]), ALU.mult
                                            ).then_inc(xh_ready, 1)

                def pool_pair(t, q):
                    for b in range(2):
                        center(b, 1 - q, 2 * t + 2 + b)
                    for b in range(2):
                        scale(b, 1 - q, 2 * t + 2 + b)
                for b in range(2):
                    center(b, 0, b)
                for b in range(2):
                    scale(b, 0, b)
                with pool.Fori(0, PAIRS // 2 - 1) as u:
                    for q in range(2):
                        pool_pair(2 * u + q, q)
                pool_pair(PAIRS - 2, 0)

            def turn_context(pe, b, q, j):
                pe.wait_ge(xh_ready, j + 1)
                pe.sem_inc(m.turns_pe, 1)
                for k in range(KT):
                    ins = nc.tensor.transpose(ps[0:DC + 1, 4 * b + k // 4, (k % 4) * P:(k % 4 + 1) * P],
                                              xh[:, 2 * q + b, k, :], m.ident[:])
                    if k % 4 == 3 or k == KT - 1:
                        ins.then_inc(xh_turned, 1)

            def keys(pe, b, j):
                for k in range(KT):
                    if k % 4 == 0:
                        pe.wait_ge(xhT_ready, 4 * j + k // 4 + 1)
                    ins = nc.tensor.matmul(ps[:, 4 * b + k // 4, (k % 4) * P:(k % 4 + 1) * P],
                                           turned[0:DC + 1, b, k * P:(k + 1) * P], m.WA[:, 0:P],
                                           start=True, stop=True)
                    if k == 7:
                        ins.then_inc(k_made, 1)
                nc.tensor.matmul(ps[0:S, 4 * b + 3, P:3 * P], lat[:, b * S:(b + 1) * S], m.wlkv1[:],
                                 start=True, stop=True).then_inc(k_made, 1)

            def turn_keys(pe, b, j):
                for k in range(KT):
                    if k in (0, 8):
                        pe.wait_ge(kn_ready, 3 * j + (1 if k == 0 else 3))
                        pe.sem_inc(m.turns_pe, 1)
                    r = rows_of(k)
                    ins = nc.tensor.transpose(ps[:, 4 * b + k // 4, (k % 4) * P:(k % 4) * P + r], kn[0:r, b, k, :],
                                              m.ident[0:r, 0:r])
                    if k % 4 == 3:
                        ins.then_inc(kn_turned, 1)
                nc.tensor.transpose(ps[:, 4 * b + 3, REST:REST + LAT], kn[0:LAT, b, KT, :], m.ident[0:LAT, 0:LAT]
                                    ).then_inc(kn_turned, 1)

            def scores(pe, b, j):
                for c in range(4):
                    n = min(BANK, KEYS - c * BANK)
                    pe.wait_ge(knT_ready, 4 * j + c + 1)
                    nc.tensor.matmul(ps[:, 4 * b + c, 0:n], pick[:, bass.ds(j, 1), :].rearrange("p o q -> p (o q)"),
                                     mask_bf[:, c * BANK:c * BANK + n], start=True, stop=False)
                    ins = nc.tensor.matmul(ps[:, 4 * b + c, 0:n], qs[:, b, :], turned[:, b, c * BANK:c * BANK + n],
                                           start=False, stop=True)
                ins.then_inc(scores_ready, 1)

            def turn_probs(pe, b, j):
                pe.wait_ge(exps_ready, j + 1)
                pe.sem_inc(m.turns_pe, 1)
                for k in range(KT):
                    r = rows_of(k)
                    ins = nc.tensor.transpose(ps[0:r, 4 * b + k // 4, (k % 4) * P:(k % 4 + 1) * P],
                                              probs[:, b, k * P:k * P + r], m.ident[:])
                    if k % 4 == 3:
                        ins.then_inc(p_turned, 1)
                nc.tensor.transpose(ps[0:LAT, 4 * b + 3, P:2 * P], probs[:, b, CTX:KEYS], m.ident[:]
                                    ).then_inc(p_turned, 1)

            def output(pe, b, q, t):
                for k in range(KT):
                    if k in (0, 4, 8) and b == 0:
                        pe.wait_ge(pT_even_ready, 5 * t + (1, 2, 5)[k // 4])
                    elif k in (0, 4):
                        pe.wait_ge(pT_front_ready, 2 * t + k // 4 + 1)
                    elif k == 8:
                        pe.wait_ge(pT_back_ready, 3 * t + 3)
                    r = rows_of(k)
                    ins = nc.tensor.matmul(ps[0:DC + 1, 4 * b, 0:P], xh[0:r, 2 * q + b, k, :], pT[0:r, b, k, :],
                                           start=(k == 0), stop=(k == KT - 1))
                ins.then_inc(oT_made, 1)

            def values(pe, b, j):
                nc.tensor.matmul(ps[:, 4 * b + 1, 0:P], pT[0:LAT, b, KT, :], vlat[:, b, :], start=True, stop=False)
                pe.wait_ge(oT_copied, j + 1)
                nc.tensor.matmul(ps[:, 4 * b + 1, 0:P], oT[:, b, :], m.WA[:, P:2 * P], start=False, stop=True
                                 ).then_inc(o_made, 1)

            def pe_pair(pe, t, q):
                turn_context(pe, 0, q, 2 * t)
                pe.wait_ge(x_updated, t + 1)
                turn_context(pe, 1, q, 2 * t + 1)
                pe.wait_ge(staged, 3 * t + 3)
                for b in range(2):
                    keys(pe, b, 2 * t + b)
                for b in range(2):
                    turn_keys(pe, b, 2 * t + b)
                    scores(pe, b, 2 * t + b)
                turn_probs(pe, 0, 2 * t)
                output(pe, 0, q, t)
                turn_probs(pe, 1, 2 * t + 1)
                values(pe, 0, 2 * t)
                output(pe, 1, q, t)
                values(pe, 1, 2 * t + 1)
                pe.wait_ge(o_copied, 4 * t + 4)
                pe.sem_inc(m.turns_pe, 1)
                nc.tensor.transpose(ps[:, 0, 0:P], attn[:], m.ident[:]).then_inc(a_turned, 1)
                pe.wait_ge(aT_copied, t + 1)
                nc.tensor.matmul(ps[:, 4, 0:D], attnT[:], m.wo1[:], start=True, stop=False)
                nc.tensor.matmul(ps[:, 4, 0:D], m.ones[0:1, 0:P], m.bo1[:], start=False, stop=True
                                 ).then_inc(y_made, 1)

            @block.tensor
            def _(pe):
                pe.wait_ge(set_once, 3)
                pe.wait_ge(mask_ready, 2)
                with pe.Fori(0, PAIRS // 2) as u:
                    for q in range(2):
                        pe_pair(pe, 2 * u + q, q)

            def square_context(act, b, q, j):
                act.wait_ge(centered, j + 1)
                nc.scalar.activation(sq[:, b], xh[:, 2 * q + b, :, 0:DC], ACT.Square).then_inc(squared, 1)

            def act_pair(act, t, q, last):
                for b in range(2):
                    for c in range(4):
                        n = min(BANK, TILES - c * BANK)
                        act.wait_ge(xh_turned, 4 * (2 * t + b) + c + 1)
                        nc.scalar.copy(turned[0:DC + 1, b, c * BANK:c * BANK + n], ps[0:DC + 1, 4 * b + c, 0:n]
                                       ).then_inc(xhT_ready, 1)
                nc.scalar.activation(spare[:], m.half[:, 0:1], ACT.Sqrt)
                for b in range(2):
                    j = 2 * t + b
                    for h in range(2):
                        lo, hi = half_tiles(h)
                        act.wait_ge(k_made, 2 * j + h + 1)
                        nc.scalar.activation(ksq[:, b, lo:hi, :],
                                             group(b)[:, lo * P:hi * P].rearrange("p (k d) -> p k d", d=P),
                                             ACT.Square).then_inc(k_squared, 1)
                    nc.scalar.activation(ksq[0:S, b, KT, :], ps[0:S, 4 * b + 3, P:2 * P], ACT.Square
                                         ).then_inc(k_squared, 1)
                    nc.scalar.copy(vlat[:, b, :], ps[0:S, 4 * b + 3, 2 * P:3 * P]).then_inc(vlat_ready, 1)
                    act.wait_ge(kss_ready, 4 * j + 4)
                    nc.scalar.activation(knorm[:, b], kss[:, b], ACT.Sqrt).then_inc(knorm_ready, 1)

                def copy_keys(b):
                    for c in range(4):
                        n = min(BANK, KEYS - c * BANK)
                        act.wait_ge(kn_turned, 4 * (2 * t + b) + c + 1)
                        nc.scalar.copy(turned[:, b, c * BANK:c * BANK + n], ps[:, 4 * b + c, 0:n]
                                       ).then_inc(knT_ready, 1)

                def exp(b):
                    act.wait_ge(mx_steps, 2 * (2 * t + b) + 2)
                    nc.scalar.activation(probs[:, b, 0:KEYS], group(b)[:, 0:KEYS], ACT.Exp,
                                         bias=negm[:, b:b + 1], accum_out=total[:, b:b + 1]).then_inc(exps_ready, 1)

                def copy_probs(b, first, ready):
                    for c in range(first, 3):
                        act.wait_ge(p_turned, 4 * (2 * t + b) + c + 1)
                        nc.scalar.copy(pT[:, b, 4 * c:4 * c + 4, :],
                                       ps[:, 4 * b + c, :].rearrange("p (k q) -> p k q", q=P)).then_inc(ready, 1)
                    act.wait_ge(p_turned, 4 * (2 * t + b) + 4)
                    nc.scalar.copy(pT[0:REST, b, FULL, :], ps[0:REST, 4 * b + 3, 0:P]).then_inc(ready, 1)
                    nc.scalar.copy(pT[0:LAT, b, KT, :], ps[0:LAT, 4 * b + 3, P:2 * P]).then_inc(ready, 1)
                copy_keys(0)
                if not last:
                    for b in range(2):
                        square_context(act, b, 1 - q, 2 * t + 2 + b)
                copy_keys(1)
                nc.scalar.activation(spare[:], m.half[:, 0:1], ACT.Exp)
                exp(0)
                copy_probs(0, 0, pT_even_ready)
                exp(1)
                act.wait_ge(oT_made, 2 * t + 1)
                nc.scalar.copy(oT[:, 0, :], ps[0:DC + 1, 0, 0:P]).then_inc(oT_copied, 1)
                copy_probs(1, 2, pT_back_ready)
                act.wait_ge(oT_made, 2 * t + 2)
                nc.scalar.copy(oT[:, 1, :], ps[0:DC + 1, 4, 0:P]).then_inc(oT_copied, 1)
                act.wait_ge(a_turned, t + 1)
                nc.scalar.copy(attnT[:], ps[:, 0, 0:P]).then_inc(aT_copied, 1)

            @block.scalar
            def _(act):
                for b in range(2):
                    square_context(act, b, 0, b)
                with act.Fori(0, PAIRS // 2 - 1) as u:
                    for q in range(2):
                        act_pair(act, 2 * u + q, q, False)
                act_pair(act, PAIRS - 2, 0, False)
                act_pair(act, PAIRS - 1, 1, True)

            def mean(dve, b, j, t_load):
                dve.wait_ge(loaded[b], 32 * t_load)
                nc.vector.tensor_reduce(stat[:, b, 0, :], m.ctx_nat[:, b, :, 0:DC], axis=AX.X, op=ALU.add
                                        ).then_inc(sums, 1)
                dve.wait_ge(sums, j + 1)
                nc.vector.tensor_scalar(stat[:, b, 1, :], stat[:, b, 0, :], 1.0 / DC, None, ALU.mult
                                        ).then_inc(means, 1)

            def variance(dve, b, j):
                dve.wait_ge(squared, j + 1)
                nc.vector.tensor_reduce(stat[:, b, 2, :], sq[:, b], axis=AX.X, op=ALU.add).then_inc(sqsums, 1)
                dve.wait_ge(sqsums, j + 1)
                nc.vector.tensor_scalar(stat[:, b, 2, :], stat[:, b, 2, :], 1.0 / DC, 1e-5, ALU.mult, ALU.add
                                        ).then_inc(variances, 1)

            def dve_pair(dve, t, q, last):
                V = nc.vector
                V.tensor_copy(lat[:], m.xT[:, bass.ds(t * P, P)]).then_inc(staged, 1)
                for b in range(2):
                    V.tensor_copy(qs[:, b, :], m.qbd1[:, bass.ds(2 * t + b, 1), :, :].rearrange(
                        "p o h i -> p (o h i)")).then_inc(staged, 1)
                if not last:
                    for b in range(2):
                        mean(dve, b, 2 * t + 2 + b, t + 2)
                for b in range(2):
                    j = 2 * t + b
                    for h in range(2):
                        lo, hi = half_tiles(h)
                        dve.wait_ge(k_squared, 3 * j + h + 1)
                        V.tensor_reduce(kss[:, b, lo:hi, :].rearrange("p k h -> p (k h)"),
                                        ksq[:, b, lo:hi, :].rearrange("p k (h d) -> p (k h) d", d=64), axis=AX.X,
                                        op=ALU.add).then_inc(kss_ready, 1)
                    dve.wait_ge(k_squared, 3 * j + 3)
                    V.tensor_reduce(kss[0:S, b, KT, :], ksq[0:S, b, KT, :].rearrange("p (h d) -> p h d", d=64),
                                    axis=AX.X, op=ALU.add).then_inc(kss_ready, 1)
                    dve.wait_ge(kss_ready, 4 * j + 3)
                    V.tensor_scalar(kss[:, b], kss[:, b], 64 * EPS_RMS ** 2, None, ALU.max).then_inc(kss_ready, 1)
                    dve.wait_ge(knorm_ready, j + 1)
                    V.reciprocal(krec[:, b], knorm[:, b]).then_inc(rk_steps, 1)
                    dve.wait_ge(rk_steps, 4 * j + 1)
                    V.tensor_tensor(krec[:, b], krec[:, b], kss[:, b], ALU.mult).then_inc(rk_steps, 1)
                    dve.wait_ge(rk_steps, 4 * j + 2)
                    V.tensor_tensor(krec[:, b], krec[:, b], knorm[:, b], ALU.add).then_inc(rk_steps, 1)
                    dve.wait_ge(rk_steps, 4 * j + 3)
                    V.reciprocal(krec[:, b], krec[:, b]).then_inc(rk_steps, 1)
                    dve.wait_ge(rk_steps, 4 * j + 4)
                    dve.wait_ge(vlat_ready, j + 1)
                    for h in range(2):
                        lo, hi = half_tiles(h)
                        V.tensor_tensor(
                            kn[:, b, lo:hi, :].rearrange("p k (h d) -> p (k h) d", d=64),
                            group(b)[:, lo * P:hi * P].rearrange("p (k d) -> p k d", d=64),
                            krec[:, b, lo:hi, :].rearrange("p k h -> p (k h)").unsqueeze(2).broadcast_to(
                                [P, 2 * (hi - lo), 64]), ALU.mult).then_inc(kn_ready, 1)
                    V.tensor_tensor(kn[0:S, b, KT, :].rearrange("p (h d) -> p h d", d=64),
                                    ps[0:S, 4 * b + 3, P:2 * P].rearrange("p (h d) -> p h d", d=64),
                                    krec[0:S, b, KT, :].unsqueeze(2).broadcast_to([S, 2, 64]), ALU.mult
                                    ).then_inc(kn_ready, 1)

                def less_max(b):
                    dve.wait_ge(scores_ready, 2 * t + b + 1)
                    V.tensor_reduce(mxp[:, b:b + 1], group(b)[:, 0:KEYS], axis=AX.X, op=ALU.max
                                    ).then_inc(mx_steps, 1)
                    dve.wait_ge(mx_steps, 2 * (2 * t + b) + 1)
                    V.tensor_scalar(negm[:, b:b + 1], mxp[:, b:b + 1], -1.0, None, ALU.mult).then_inc(mx_steps, 1)
                less_max(0)
                if not last:
                    for b in range(2):
                        variance(dve, b, 2 * t + 2 + b)
                less_max(1)
                for b in range(2):
                    dve.wait_ge(exps_ready, 2 * t + b + 1)
                    V.reciprocal(recip[:, b:b + 1], total[:, b:b + 1]).then_inc(recip_ready, 1)
                for c in range(2):
                    dve.wait_ge(p_turned, 4 * (2 * t + 1) + c + 1)
                    V.tensor_copy(pT[:, 1, 4 * c:4 * c + 4, :], ps[:, 4 + c, :].rearrange("p (k q) -> p k q", q=P)
                                  ).then_inc(pT_front_ready, 1)
                dve.wait_ge(recip_ready, 2 * t + 2)
                for b in range(2):
                    dve.wait_ge(o_made, 2 * t + b + 1)
                    for h in range(2):
                        rows = slice(64 * h, 64 * h + 64)
                        V.tensor_scalar(attn[S * b:S * b + S, 64 * h:64 * h + 64],
                                        ps[rows, 4 * b + 1, 64 * h:64 * h + 64], recip[rows, b:b + 1], None, ALU.mult
                                        ).then_inc(o_copied, 1)
                dve.wait_ge(y_made, t + 1)
                xt = m.X[:, bass.ds(t, 1), :].rearrange("p o d -> p (o d)")
                V.tensor_tensor(xt, xt, ps[:, 4, 0:D], ALU.add).then_inc(x_updated, 1)

            @block.vector
            def _(dve):
                dve.sem_inc(x_updated, 1)
                dve.wait_ge(set_once, 3)
                for b in range(2):
                    mean(dve, b, b, 1)
                dve.wait_ge(mask_loaded, 16)
                nc.vector.tensor_scalar(mask_bf[0:BATCHES, 0:CTX], mask_u8[:], -NEG, NEG, ALU.mult, ALU.add
                                        ).then_inc(mask_ready, 1)
                nc.vector.tensor_copy(pick[:], m.ident[:, 0:BATCHES].unsqueeze(2).broadcast_to([P, BATCHES, P])
                                      ).then_inc(mask_ready, 1)
                for b in range(2):
                    variance(dve, b, b)
                with dve.Fori(0, PAIRS // 2 - 1) as u:
                    for q in range(2):
                        dve_pair(dve, 2 * u + q, q, False)
                dve_pair(dve, PAIRS - 2, 0, False)
                dve_pair(dve, PAIRS - 1, 1, True)


def router_stage(nc, m, name, E, top, wr, br, b2, soft, extra):
    ps = m.ps
    made, exps_ready, own, less_ready, gates_ready, turned, gT_ready, b_made = (m.tally("router_" + n) for n in (
        "logits_made", "exps_ready", "dve_steps", "less_ready", "gates_ready", "gates_turned", "gT_ready",
        "bias_made"))
    with ExitStack() as ctx:
        sb = m.scoped(ctx, name)
        a, w_, sel, eq = (sb(n, [P, PAIRS, E]) for n in ("a", "work", "sel", "eq"))
        one = sb("one", [P, PAIRS])
        tot = sb("tot", [P, PAIRS])
        gT = sb("gT", [E + 1, ROWS])
        def over(t):
            return t[:].unsqueeze(2).broadcast_to([P, PAIRS, E])
        with nc.Block() as block:
            @block.tensor
            def _(pe):
                for t in range(PAIRS):
                    out = ps[:, 0, 32 * t:32 * t + E]
                    ins = nc.tensor.matmul(out, m.xT[:, t * P:(t + 1) * P], wr[:], start=True, stop=br is None)
                    if br is not None:
                        ins = nc.tensor.matmul(out, m.ones[0:1, 0:P], br[:], start=False, stop=True)
                ins.then_inc(made.sem, 1)
                gates_ready.wait(pe, 1)
                for t in range(PAIRS):
                    ins = nc.tensor.transpose(ps[0:E + 1, 2 + t // 4, (t % 4) * P:(t % 4 + 1) * P],
                                              m.gates[:, t, 0:E + 1], m.ident[:])
                ins.then_inc(turned.sem, 1)
                gT_ready.wait(pe, 1)
                for t in range(PAIRS):
                    ins = nc.tensor.matmul(ps[:, 4 + t // 4, (t % 4) * P:(t % 4 + 1) * P], gT[:, t * P:(t + 1) * P],
                                           b2[:], start=True, stop=True)
                ins.then_inc(b_made.sem, 1)

            @block.scalar
            def _(act):
                less_ready.wait(act, 1)
                nc.scalar.activation(a[:], w_[:], ACT.Exp, scale=1.0 if soft else -1.0).then_inc(exps_ready.sem, 1)
                turned.wait(act, 1)
                nc.scalar.copy(gT[:], ps[0:E + 1, 2:4, :].rearrange("p b n -> p (b n)")).then_inc(gT_ready.sem, 1)
                gT_ready.wait(act, 1)

            @block.vector
            def _(dve):
                chain = Chain(dve, own.sem, own.base)
                logits = ps[:, 0, 0:32 * PAIRS].rearrange("p (t e) -> p t e", e=32)[:, :, 0:E]
                V = nc.vector
                made.wait(dve, 1)
                if soft:
                    chain.link(V.tensor_reduce(one[:], logits, axis=AX.X, op=ALU.max))
                    V.tensor_tensor(w_[:], logits, over(one), ALU.subtract).then_inc(less_ready.sem, 1)
                    exps_ready.wait(dve, 1)
                    chain.link(V.tensor_reduce(one[:], a[:], axis=AX.X, op=ALU.add))
                    chain.link(V.reciprocal(tot[:], one[:]))
                    chain.link(V.tensor_tensor(a[:], a[:], over(tot), ALU.mult))
                else:
                    V.tensor_copy(w_[:], logits).then_inc(less_ready.sem, 1)
                    exps_ready.wait(dve, 1)
                    chain.link(V.tensor_scalar(a[:], a[:], 1.0, None, ALU.add))
                    chain.link(V.reciprocal(a[:], a[:]))
                chain.link(V.tensor_copy(w_[:], a[:]))
                chain.link(V.memset(m.gates[:, :, 0:E], 0.0))
                chain.link(V.memset(m.gates[:, :, E:E + 1], 1.0))
                gates = m.gates[:, :, 0:E]
                for i in range(top):
                    chain.link(V.tensor_reduce(one[:], w_[:], axis=AX.X, op=ALU.max))
                    chain.link(V.tensor_tensor(eq[:], w_[:], over(one), ALU.is_equal))
                    chain.link(V.tensor_tensor(eq[:], eq[:], m.down[:, 32 - E:32].unsqueeze(1).broadcast_to(
                        [P, PAIRS, E]), ALU.mult))
                    chain.link(V.tensor_reduce(one[:], eq[:], axis=AX.X, op=ALU.max))
                    chain.link(V.tensor_tensor(sel[:], eq[:], over(one), ALU.is_equal))
                    chain.link(V.scalar_tensor_tensor(out=w_[:], in0=sel[:], scalar=-4.0, in1=w_[:], op0=ALU.mult,
                                                      op1=ALU.add))
                    chain.link(V.tensor_tensor(sel[:], sel[:], a[:], ALU.mult))
                    chain.link(V.tensor_tensor(gates, gates, sel[:], ALU.add))
                if not soft:
                    chain.link(V.tensor_reduce(one[:], gates, axis=AX.X, op=ALU.add))
                    chain.link(V.tensor_scalar(one[:], one[:], 1e-6, None, ALU.add))
                    chain.link(V.reciprocal(tot[:], one[:]))
                    chain.link(V.tensor_tensor(gates, gates, over(tot), ALU.mult))
                V.tensor_copy(one[:, 0:1], m.gates[:, 0, 0:1]).then_inc(gates_ready.sem, 1)
                for e in extra:
                    chain.link(V.tensor_tensor(m.X[:], m.X[:], e[:], ALU.add))
                b_made.wait(dve, 1)
                chain.link(V.tensor_tensor(m.X[:], m.X[:], ps[:, 4:6, :].rearrange("p b (t d) -> p (b t) d", d=D),
                                           ALU.add))
                own.close(chain.n)
    for tally in (made, exps_ready, less_ready, gates_ready, turned, gT_ready, b_made):
        tally.close(1)


def experts_stage(nc, m, name, n_experts, chunks, func, unroll, w1, w2, b1):
    ps = m.ps
    loaded = [m.tally(f"expert_weights_loaded_{i}") for i in range(unroll)]
    up_made, h_ready, down_made, gated, gate_staged, rows_split, weights_split = (m.tally("expert_" + n) for n in (
        "up_made", "hidden_ready", "down_made", "gated", "gate_staged", "rows_split", "weights_split"))
    turns = n_experts // unroll
    assert turns * unroll == n_experts
    even = unroll % 2 == 0
    with ExitStack() as ctx:
        sb = m.scoped(ctx, name)
        W1, W2 = sb("w1", [P, unroll, chunks * P]), sb("w2", [P, unroll, chunks, D])
        w1h, w1l = (sb(n, [P, unroll, chunks * P], F32R) for n in ("w1_high", "w1_low"))
        xh, xl = (sb(n, [P, ROWS], F32R) for n in ("x_high", "x_low"))
        B1 = sb("b1", [P, unroll, chunks])
        hid = sb("hid", [P, 2, chunks, ROWS])
        gate = sb("gate", [P, 2, PAIRS])
        with nc.Block() as block:
            @block.sync
            def _(sp):
                def load(i, e):
                    ee = bass.ds(e, 1)
                    sp.dma_start(W1[:, i, :], w1[ee].rearrange("o p h -> (o p) h")).then_inc(loaded[i].sem, 16)
                    sp.dma_start(W2[:, i], w2[ee].rearrange("o (c p) d -> p (o c) d", p=P)).then_inc(loaded[i].sem, 16)
                    sp.dma_start(B1[:, i, :], b1[ee].rearrange("o p c -> (o p) c")).then_inc(loaded[i].sem, 16)
                for i in range(unroll):
                    load(i, i)
                with sp.Fori(1, turns) as t:
                    for i in range(unroll):
                        down_made.wait(sp, 2 + (t - 1) * unroll + i + 1)
                        load(i, t * unroll + i)

            @block.tensor
            def _(pe):
                pe.sem_inc(down_made.sem, 2)

                rows_split.wait(pe, 2)

                def up(i, e):
                    weights_split.wait(pe, 2 * e + 2)
                    for c in range(chunks):
                        h_ready.wait(pe, 2 + chunks * e + c - 1)
                        for half in range(2):
                            out = ps[:, 2 * (((i * chunks) + c) % 2) + half, :]
                            w, x = slice(c * P, (c + 1) * P), slice(half * BANK, (half + 1) * BANK)
                            nc.tensor.matmul(out, w1h[:, i, w], xh[:, x], start=True, stop=False)
                            nc.tensor.matmul(out, w1h[:, i, w], xl[:, x], start=False, stop=False)
                            ins = nc.tensor.matmul(out, w1l[:, i, w], xh[:, x], start=False, stop=True)
                        ins.then_inc(up_made.sem, 1)

                def down(i, e):
                    gated.wait(pe, 2 + PAIRS + PAIRS * ((e - 1) if (even or i) else e))
                    for tile in range(PAIRS):
                        for c in range(chunks):
                            if tile == 0:
                                h_ready.wait(pe, 2 + chunks * e + c + 1)
                            ins = nc.tensor.matmul(ps[:, 4 + 2 * (i % 2) + tile // 4, (tile % 4) * P:(tile % 4 + 1) * P],
                                                   hid[:, i % 2, c, tile * P:(tile + 1) * P], W2[:, i, c, :],
                                                   start=(c == 0), stop=(c == chunks - 1))
                    ins.then_inc(down_made.sem, 1)

                with pe.Fori(0, turns) as t:
                    up(0, t * unroll)
                    for i in range(1, unroll):
                        up(i, t * unroll + i)
                        down(i - 1, t * unroll + i - 1)
                    down(unroll - 1, t * unroll + unroll - 1)

            @block.gpsimd
            def _(pool):
                def split(i, t):
                    e = t * unroll + i
                    loaded[i].wait(pool, 48 * (t + 1))
                    pool.sem_inc(m.turns_pool, 1)
                    nc.gpsimd.tensor_copy(w1h[:, i, :], W1[:, i, :]).then_inc(weights_split.sem, 1)
                    weights_split.wait(pool, 2 * e + 1)
                    nc.gpsimd.tensor_tensor(w1l[:, i, :], W1[:, i, :], w1h[:, i, :], ALU.subtract
                                            ).then_inc(weights_split.sem, 1)
                for i in range(unroll):
                    split(i, 0)
                with pool.Fori(1, turns) as t:
                    for i in range(unroll):
                        up_made.wait(pool, chunks * ((t - 1) * unroll + i + 1))
                        split(i, t)

            @block.scalar
            def _(act):
                act.sem_inc(h_ready.sem, 2)
                with act.Fori(0, turns) as t:
                    for i in range(unroll):
                        e = t * unroll + i
                        for c in range(chunks):
                            up_made.wait(act, chunks * e + c + 1)
                            down_made.wait(act, 2 + ((e - 1) if (even or i) else e))
                            nc.scalar.activation(hid[:, i % 2, c, :],
                                                 ps[:, 2 * (((i * chunks) + c) % 2):2 * (((i * chunks) + c) % 2) + 2, :]
                                                 .rearrange("p b n -> p (b n)"), func, bias=B1[:, i, c:c + 1]
                                                 ).then_inc(h_ready.sem, 1)

            @block.vector
            def _(dve):
                nc.vector.tensor_copy(xh[:], m.xT[:]).then_inc(rows_split.sem, 1)
                rows_split.wait(dve, 1)
                nc.vector.tensor_tensor(xl[:], m.xT[:], xh[:], ALU.subtract).then_inc(rows_split.sem, 1)
                dve.sem_inc(gated.sem, 2 + PAIRS)
                with dve.Fori(0, turns) as t:
                    for i in range(unroll):
                        e = t * unroll + i
                        gated.wait(dve, 2 + PAIRS + PAIRS * e)
                        nc.vector.tensor_copy(gate[:, i % 2, :], m.gates[:, :, bass.ds(e, 1)].rearrange(
                            "p t o -> p (t o)")).then_inc(gate_staged.sem, 1)
                        gate_staged.wait(dve, e + 1)
                        down_made.wait(dve, 2 + e + 1)
                        for tile in range(PAIRS):
                            nc.vector.scalar_tensor_tensor(
                                out=m.X[:, tile, :],
                                in0=ps[:, 4 + 2 * (i % 2) + tile // 4, (tile % 4) * P:(tile % 4 + 1) * P],
                                scalar=gate[:, i % 2, tile:tile + 1], in1=m.X[:, tile, :], op0=ALU.mult, op1=ALU.add
                                ).then_inc(gated.sem, 1)
                gated.wait(dve, 2 + PAIRS + PAIRS * n_experts)
    for tally, n in [(up_made, chunks * n_experts), (h_ready, 2 + chunks * n_experts), (down_made, 2 + n_experts),
                     (gated, 2 + PAIRS + PAIRS * n_experts), (gate_staged, n_experts),
                     (rows_split, 2), (weights_split, 2 * n_experts)
                     ] + [(tally, 48 * turns) for tally in loaded]:
        tally.close(n)


def store_stage(nc, m, src, out):
    stored = m.sem("output_stored")
    with nc.Block() as block:
        @block.sync
        def _(sp):
            sp.dma_start(out.rearrange("(t b) s d -> (b s) t d", b=2), src[:]).then_inc(stored, 16)
            sp.wait_ge(stored, 16)


def build(nc, dram, out):
    with ExitStack() as ctx:
        def sb(name, shape, dt=F32):
            return ctx.enter_context(nc.sbuf_tensor(name, shape, dt))

        m = Core()
        m.H0 = 8
        m.sem = lambda name: ctx.enter_context(nc.semaphore(name))
        tallies = {}

        def tally(name):
            if name not in tallies:
                tallies[name] = Tally(m.sem(name))
            return tallies[name]
        m.tally = tally
        m.scoped = lambda c, tag: (lambda name, shape, dt=F32:
                                   c.enter_context(nc.sbuf_tensor(tag + "_" + name, shape, dt)))
        m.ps = ctx.enter_context(nc.psum_tensor("ps", [P, 8, BANK], F32))
        m.X = sb("X", [P, PAIRS, D])
        m.xT = sb("xT", [P, ROWS])
        m.Y = sb("Y", [P, PAIRS, D])
        m.nhalf, m.half = sb("nhalf", [P, 32]), sb("half", [P, 32])
        m.ones, m.ones_bf = sb("ones", [1, BANK]), sb("ones_bf", [1, P], BF16)
        m.ident_bf = sb("ident_bf", [P, P], BF16)
        m.causal_bf, m.strided_bf = sb("causal_bf", [P, BANK], BF16), sb("strided_bf", [P, BANK], BF16)
        m.ctx_nat = sb("ctx_nat", [P, 2, KT, DC + 1])
        m.turns_pool = m.sem("turns_pool")
        m.turns_act, m.turns_pe, m.turns_dve = m.sem("turns_act"), m.sem("turns_pe"), m.sem("turns_dve")
        m.loads = []

        def resident(attr, shape, source):
            t = sb(attr, shape)
            m.loads.append((t[:], source))
            return t

        m.ident = resident("ident", [P, P], dram["ident"])
        m.masks = m.Y[:].rearrange("p t d -> p (t d)")
        m.loads += [(m.masks[:, 0:BANK], dram["causal"]), (m.masks[:, BANK:2 * BANK], dram["strided"])]
        m.wqT0 = resident("wqT0", [S, 8, D], dram["wqT0"].rearrange("(h e) d -> e h d", h=8))
        m.wkT0 = resident("wkT0", [S, 8, DC], dram["wkT0"].rearrange("(h e) d -> e h d", h=8))
        m.wvT0 = resident("wvT0", [S, 8, DC], dram["wvT0"].rearrange("(h e) d -> e h d", h=8))
        m.wo0 = resident("wo0", [S, 8, D], dram["L0_xattn_Wo"].rearrange("(h e) d -> e h d", h=8))
        m.bo0 = resident("bo0", [1, D], dram["L0_xattn_bo"].rearrange("(o d) -> o d", o=1))
        m.n_first_loads = len(m.loads)
        m.qmask = resident("qmask", [P, 2], dram["qmask"])
        m.kmask = resident("kmask", [P, HP], dram["kmask"])
        m.cosb = resident("cosb", [P, S], dram["cosb"])
        m.sinb = resident("sinb", [P, S], dram["sinb"])
        m.pos = resident("pos", [P, P], dram["pos"])
        m.down = resident("down", [P, 32], dram["down"])
        m.rope_sign = resident("rope_sign", [P, 1], dram["rope_sign"])
        m.small0 = []
        for n in ("wqB", "wqBs", "wkB", "wkBs", "wvB", "woB"):
            m.small0.append(resident(n, [P, P], dram[n]))
        m.wqk = []
        for n in ("wqC", "wqCs", "wkC", "wkCs"):
            m.wqk.append(resident(n, [P, HP * P], dram[n]))
        m.bqk = resident("bqk", [P, 4, HP], dram["bqkC"])
        m.wv_c = resident("wv_c", [P, HP * P], dram["L0_ffn_v_w"])
        m.bv_c = resident("bv_c", [P, HP], dram["bvC"])
        m.wo_c = resident("wo_c", [P, HP, D], dram["L0_ffn_o_w"].rearrange("(h p) d -> p h d", p=P))
        m.bo_c = resident("bo_c", [1, D], dram["L0_ffn_o_b"].rearrange("(o d) -> o d", o=1))
        m.theta = sb("theta", [P, 1])
        for q in range(4):
            m.loads.append((m.theta[32 * q:32 * q + 32, :], dram["L0_ffn_theta"].rearrange("(p o) -> p o", o=1)))
        m.gain1 = resident("gain1", [P, D], dram["L0_ffn_gamma1"].partition_broadcast(P))
        m.gain2 = resident("gain2", [P, D], dram["L0_ffn_gamma2"].partition_broadcast(P))
        m.wr0 = resident("wr0", [P, 31], dram["L0_ffn_router_w"])
        m.br0 = resident("br0", [1, 31], dram["L0_ffn_router_b"].rearrange("(o d) -> o d", o=1))
        m.b2_0 = resident("b2_0", [32, D], dram["b2_0"])
        def column(source):
            return source.rearrange("(p o) -> p o", o=1)

        def row(source):
            return source.rearrange("(o d) -> o d", o=1)
        m.ln_l_g = resident("ln_l_g", [P, D], dram["L1_xattn_ln_l_g"].partition_broadcast(P))
        m.ln_l_b = resident("ln_l_b", [P, D], dram["L1_xattn_ln_l_b"].partition_broadcast(P))
        m.ln_x_g = resident("ln_x_g", [DC, 1], column(dram["L1_xattn_ln_x_g"]))
        m.ln_x_b = resident("ln_x_b", [DC, 1], column(dram["L1_xattn_ln_x_b"]))
        m.qn_g, m.kn_g = sb("qn_g", [P, D]), sb("kn_g", [P, D])
        for h in range(2):
            for t, n in ((m.qn_g, "L1_xattn_qn_g"), (m.kn_g, "L1_xattn_kn_g")):
                m.loads.append((t[:, 64 * h:64 * h + 64], dram[n].partition_broadcast(P)))
        m.wq1 = resident("wq1", [P, P], dram["wq1"])
        m.wkv1 = resident("wkv1", [DC, 2 * P], dram["wkv1"])
        m.wlkv1 = resident("wlkv1", [P, 2 * P], dram["wlkv1"])
        m.wo1 = resident("wo1", [P, P], dram["wo1"])
        m.bo1 = resident("bo1", [1, P], row(dram["L1_xattn_bo"]))
        m.wq_e, m.wk_e, m.wv_e = (resident(f"w{n}_e", [P, P], dram[f"L1_attn_W{n}"]) for n in "qkv")
        m.wo_e = resident("wo_e", [P, P], dram["L1_attn_Wp"])
        m.bq_e = resident("bq_e", [P, 1], column(dram["L1_attn_bq"]))
        m.bk_e = resident("bk_e", [P, 1], column(dram["L1_attn_bk"]))
        m.bv_e = resident("bv_e", [P, D], dram["L1_attn_bv"].partition_broadcast(P))
        m.bo_e = resident("bo_e", [1, D], row(dram["L1_attn_bp"]))
        m.gain6 = resident("gain6", [P, D], dram["L1_ffn_norm_weight"].partition_broadcast(P))
        m.wr1 = resident("wr1", [P, 8], dram["wr1"])
        m.b2_1 = resident("b2_1", [9, D], dram["b2_1"])
        m.gates = sb("gates", [P, PAIRS, 32])
        m.cosc, m.sinc = sb("cosc", [P, P]), sb("sinc", [P, P])
        load_stage(nc, m, dram)
        ln = [("ln", 1e-5, None, None)]

        def scope():
            c = ExitStack()
            return c, lambda name, shape, dt=F32: c.enter_context(nc.sbuf_tensor(name, shape, dt))
        c0, s0 = scope()
        with c0:
            m.mq0, m.nv0 = s0("mq0", [P, 8, P]), s0("nv0", [DC, 8, D])
            m.U = s0("U", [DC, BATCHES, 8, S])
            norm_stage(nc, m, "n0", m.X, m.Y, m.xT, ln)
            l0_fold_stage(nc, m)
            l0_cross_stage(nc, m, dram)
        rest_loaded_stage(nc, m)
        c0, s0 = scope()
        with c0:
            m.qT, m.kT, m.V = s0("qT", [P, ROWS]), s0("kT", [P, ROWS]), s0("V", [P, PAIRS, HP, 2, 16])
            norm_stage(nc, m, "n1", m.X, m.Y, m.xT, ln)
            project_small_heads_stage(nc, m, "p1", m.small0[:5], True, None)
            small_heads_stage(nc, m, "a1", m.causal_bf, m.small0[5], None)
        c0, s0 = scope()
        with c0:
            m.AO = s0("AO", [P, PAIRS, D])
            norm_stage(nc, m, "n2", m.X, m.Y, m.xT, ln + [("rms", 1e-5, m.gain1, None)])
            angles_stage(nc, m)
            wide_heads_stage(nc, m)
            norm_stage(nc, m, "n3", m.AO, m.Y, m.xT, [("rms", 1e-5, m.gain2, None)])
            router_stage(nc, m, "r0", 31, 3, m.wr0, m.br0, m.b2_0, True, [m.AO, m.Y])
            experts_stage(nc, m, "e0", 32, 1, ACT.Gelu, 4, dram["w1_0"], dram["w2_0"], dram["b1_0"])
        c0, s0 = scope()
        with c0:
            m.qbd1, m.WA = s0("qbd1", [P, BATCHES, 2, S]), s0("WA", [DC + 1, 2 * P])
            norm_stage(nc, m, "n4", m.X, m.Y, m.xT, ln + [("ln", 1e-5, m.ln_l_g, m.ln_l_b)])
            l1_prepare_stage(nc, m, dram)
            l1_cross_stage(nc, m, dram)
        c0, s0 = scope()
        with c0:
            m.qT, m.kT, m.V = s0("qT1", [P, ROWS]), s0("kT1", [P, ROWS]), s0("V1", [P, PAIRS, HP, 2, 16])
            norm_stage(nc, m, "n5", m.X, m.Y, m.xT, ln)
            project_small_heads_stage(nc, m, "p5", [m.wq_e, m.wk_e, m.wv_e], False, [m.bq_e, m.bk_e, m.bv_e])
            small_heads_stage(nc, m, "a5", m.strided_bf, m.wo_e, m.bo_e)
        norm_stage(nc, m, "n6", m.X, m.Y, m.xT, ln + [("rms", 1e-8, m.gain6, None)])
        router_stage(nc, m, "r1", 8, 2, m.wr1, None, m.b2_1, False, [])
        experts_stage(nc, m, "e1", 9, 4, ACT.Relu, 3, dram["w1_1"], dram["w2_1"], dram["b1_1"])
        store_stage(nc, m, m.X, out)


def kernel(**inputs):
    import numpy as np
    import concourse.bacc as bacc
    from concourse.bass_utils import run_bass_kernel_spmd

    arrays = {n: np.ascontiguousarray(a) for n, a in inputs.items()}
    arrays["ctx"] = arrays.pop("ctx_768")
    arrays["ctxT"] = np.ascontiguousarray(arrays["ctx"].transpose(0, 2, 1))
    for new, old in (("wqT0", "L0_xattn_Wq"), ("wkT0", "L0_xattn_Wk"), ("wvT0", "L0_xattn_Wv")):
        arrays[new] = np.ascontiguousarray(arrays[old].T)
    i, key = np.arange(128)[:, None] % 64, np.arange(512)[None, :] % 64
    arrays["ident"] = np.eye(128, dtype=np.float32)
    arrays["causal"] = np.where(key <= i, 0.0, NEG).astype(np.float32)
    arrays["strided"] = np.where((key <= i) & (key % 4 != 3), 0.0, NEG).astype(np.float32)

    h, feature = np.arange(128) // 8, np.arange(128) % 8
    arrays["qmask"] = (h[:, None] % 2 == np.arange(2)).astype(np.float32)
    arrays["kmask"] = (h[:, None] // 2 == np.arange(8)).astype(np.float32)
    inv = (1.0 / 10000.0 ** (np.arange(0, 8, 2, dtype=np.float32) / 8)).astype(np.float32)
    angle = (np.arange(64, dtype=np.float32)[None, :] * inv[feature % 4][:, None]).astype(np.float32)
    arrays["cosb"] = np.cos(angle)
    arrays["sinb"] = np.sin(angle) * np.where(feature < 4, -1, 1).astype(np.float32)[:, None]
    arrays["pos"] = np.tile(np.arange(64, dtype=np.float32), (128, 2))
    arrays["rope_sign"] = np.where(np.arange(128) % 64 < 32, -1, 1).astype(np.float32)[:, None]
    arrays["down"] = np.tile(np.arange(32, 0, -1).astype(np.float32), (128, 1))
    swap8 = (np.arange(16)[:, None] * 8 + (np.arange(8) + 4) % 8).reshape(-1)
    for new, old in (("wqB", "L0_attn_W_q"), ("wkB", "L0_attn_W_k"), ("wvB", "L0_attn_W_v"), ("woB", "L0_attn_W_o")):
        arrays[new] = np.ascontiguousarray(arrays[old].T)
    for n in ("wqB", "wkB"):
        arrays[n + "s"] = np.ascontiguousarray(arrays[n][:, swap8])
    halves = np.concatenate([np.arange(0, 64, 2), np.arange(1, 64, 2)])
    split = (np.arange(16)[:, None] * 64 + halves).reshape(-1)
    swapped = (np.arange(16)[:, None] * 64 + np.roll(halves, 32)).reshape(-1)
    biases = []
    for q in "qk":
        w, bias = arrays[f"L0_ffn_{q}_w"], arrays[f"L0_ffn_{q}_b"]
        for tag, order in (("", split), ("s", swapped)):
            arrays[f"w{q}C{tag}"] = np.ascontiguousarray(w[:, order])
            biases.append(bias[order].reshape(8, 128).T)
    arrays["bvC"] = np.ascontiguousarray(arrays["L0_ffn_v_b"].reshape(8, 128).T)
    arrays["bqkC"] = np.ascontiguousarray(np.stack(biases, 1))
    arrays["w1_0"] = np.concatenate([arrays["L0_ffn_re_w1"], arrays["L0_ffn_sh_w1"][None]])
    arrays["w2_0"] = np.concatenate([arrays["L0_ffn_re_w2"], arrays["L0_ffn_sh_w2"][None]])
    arrays["b1_0"] = np.concatenate([arrays["L0_ffn_re_b1"], arrays["L0_ffn_sh_b1"][None]])[:, :, None]
    arrays["b2_0"] = np.concatenate([arrays["L0_ffn_re_b2"], arrays["L0_ffn_sh_b2"][None]])
    arrays["mask"] = arrays["mask_BxS2_bk0"]
    for new, old in (("wq1", "Wq"), ("wkv1", "Wkv"), ("wlkv1", "Wlkv"), ("wo1", "Wo")):
        arrays[new] = np.ascontiguousarray(arrays["L1_xattn_" + old].T)
    arrays["wr1"] = np.ascontiguousarray(arrays["L1_ffn_router_w"].T)
    for new, old in (("w1_1", "w1"), ("w2_1", "w2"), ("b1_1", "b1"), ("b2_1", "b2")):
        arrays[new] = np.concatenate([arrays["L1_ffn_e" + old], arrays["L1_ffn_s" + old][None]])
    arrays["b1_1"] = np.ascontiguousarray(arrays["b1_1"].reshape(9, 4, 128).transpose(0, 2, 1))

    nc = bacc.Bacc("TRN2", target_bir_lowering=False, num_devices=1)
    dram = {}
    for n in USED:
        a = arrays[n]
        dram[n] = nc.dram_tensor("in_" + n, a.shape, mybir.dt.from_np(a.dtype), kind="ExternalInput").ap()
    out = nc.dram_tensor("out", (BATCHES, S, D), F32, kind="ExternalOutput").ap()
    build(nc, dram, out)
    got = run_bass_kernel_spmd(nc, [{"in_" + n: arrays[n] for n in USED}], core_ids=[0])
    return got.results[0]["out"]


USED = ["x", "ctx", "ctxT", "ident", "causal", "strided", "wqT0", "wkT0", "wvT0", "L0_xattn_Wo", "L0_xattn_bo",
        "qmask", "kmask", "cosb", "sinb", "pos", "down", "rope_sign", "wqB", "wqBs", "wkB", "wkBs", "wvB", "woB",
        "wqC", "wqCs", "wkC", "wkCs", "bqkC", "L0_ffn_v_w", "bvC", "L0_ffn_o_w", "L0_ffn_o_b", "L0_ffn_theta",
        "L0_ffn_gamma1", "L0_ffn_gamma2", "L0_ffn_router_w", "L0_ffn_router_b", "b2_0", "w1_0", "w2_0", "b1_0",
        "mask", "L1_xattn_ln_l_g", "L1_xattn_ln_l_b", "L1_xattn_ln_x_g", "L1_xattn_ln_x_b", "L1_xattn_qn_g",
        "L1_xattn_kn_g", "wq1", "wkv1", "wlkv1", "wo1", "L1_xattn_bo", "L1_attn_Wq", "L1_attn_Wk", "L1_attn_Wv",
        "L1_attn_Wp", "L1_attn_bq", "L1_attn_bk", "L1_attn_bv", "L1_attn_bp", "L1_ffn_norm_weight", "wr1", "b2_1",
        "w1_1", "w2_1", "b1_1"]
```
